# Optimizing a Trainium2 kernel written in Bass

```python
import numpy as np
import jax
import jax.numpy as jnp

def _softmax(x, axis=-1):
    return jax.nn.softmax(x, axis=axis)

def _gelu(x):
    return jax.nn.gelu(x, approximate=True)

def _silu(x):
    return jax.nn.silu(x)

def _sigmoid(x):
    return jax.nn.sigmoid(x)

def _layernorm(x, axis=-1, eps=1e-05):
    m = jnp.mean(x, axis=axis, keepdims=True)
    v = jnp.var(x, axis=axis, keepdims=True)
    return (x - m) / jnp.sqrt(v + eps)

def _scatter_add(tgt, idx, src, axis=0):
    return tgt.at[idx].add(src)

def _segment_sum(src, seg, n):
    return jax.ops.segment_sum(src, seg, n)
kernel_name = 'mk_gnn_preln_d4_gnn_r64_026b00'

def setup_inputs(seed: int=0):
    np.random.seed(seed)
    _w = jnp.asarray

    def _rec_inputs():
        import jax
        import jax.numpy as jnp
        _gk = jax.random.key(seed)
        x = -0.000202 + 1 * jax.random.normal(jax.random.fold_in(_gk, 1), (50000, 128), jnp.float32)
        src = jax.random.randint(jax.random.fold_in(_gk, 2), (12500,), 0, 50000, jnp.int32)
        dst = jnp.minimum((50000 * jax.random.uniform(jax.random.fold_in(_gk, 3), (12500,)) ** 2.0).astype(jnp.int32), 49999)
        _o = jnp.argsort(dst, stable=True)
        src = src[_o]
        dst = dst[_o]
        edge_attr_128 = -6.47781e-05 + 0.999943 * jax.random.normal(jax.random.fold_in(_gk, 13), (12500, 128), jnp.float32)
        edge_weight = jax.random.uniform(jax.random.fold_in(_gk, 15), (12500,), jnp.float32, 0.0, 0.999999)
        return (x, src, dst, edge_attr_128, edge_weight)
    x, src, dst, edge_attr_128, edge_weight = _rec_inputs()

    def _L0_gnn_setup():
        import jax, jax.numpy as jnp
        import numpy as np
        N_NODES = 50000
        N_EDGES = 500000
        D = 128
        D_OUT = 128
        L_TRANS = 2
        L_GNN = 3
        EPS_LN = 1e-05
        EPS_BN = 1e-05

        def _ln(x, g, b):
            mu = jnp.mean(x, axis=-1, keepdims=True)
            var = jnp.mean(jnp.square(x - mu), axis=-1, keepdims=True)
            return (x - mu) * jax.lax.rsqrt(var + EPS_LN) * g + b

        def _bn_eval(x, g, b):
            return x * (g / np.sqrt(1.0 + EPS_BN)) + b

        def _attn(x, wq, wk, wv):
            n = x.shape[0]
            q = x @ wq
            k = x @ wk
            v = x @ wv
            eps = 1e-06
            q = jnp.where(q == 0, eps, q)
            k = jnp.where(k == 0, eps, k)
            q = q / jnp.linalg.norm(q, axis=-1, keepdims=True)
            k = k / jnp.linalg.norm(k, axis=-1, keepdims=True)
            kv = jnp.einsum('lm,ld->md', k, v)
            num = q @ kv + n * v
            denom = q @ jnp.sum(k, axis=0) + n
            return num / denom[:, None]

        def _gcn(x, edge_index, w, b, n):
            sl = jnp.arange(n, dtype=edge_index.dtype)
            row = jnp.concatenate([edge_index[0], sl])
            col = jnp.concatenate([edge_index[1], sl])
            deg = jax.ops.segment_sum(jnp.ones_like(col, dtype=x.dtype), col, num_segments=n)
            dinv = jnp.where(deg > 0, jax.lax.rsqrt(deg), 0.0)
            norm = dinv[row] * dinv[col]
            xw = x @ w
            out = jax.ops.segment_sum(norm[:, None] * xw[row], col, num_segments=n)
            return out + b
        key = jax.random.key(seed)
        ks = jax.random.split(key, 8)
        s = 1.0 / np.sqrt(D)
        return {'x': jax.random.normal(ks[0], (N_NODES, D), jnp.float32), 'edge_index': jax.random.randint(ks[1], (2, N_EDGES), 0, N_NODES, dtype=jnp.int32), 't_fc_w': jax.random.normal(ks[2], (D, D), jnp.float32) * s, 't_fc_b': jnp.zeros((D,), jnp.float32), 't_ln_g': jnp.ones((L_TRANS + 1, D), jnp.float32), 't_ln_b': jnp.zeros((L_TRANS + 1, D), jnp.float32), 'qkv_w': jax.random.normal(ks[3], (L_TRANS, 3, D, D), jnp.float32) * s, 'g_fc_w': jax.random.normal(ks[4], (D, D), jnp.float32) * s, 'g_fc_b': jnp.zeros((D,), jnp.float32), 'bn_g': jnp.ones((L_GNN + 1, D), jnp.float32), 'bn_b': jnp.zeros((L_GNN + 1, D), jnp.float32), 'conv_w': jax.random.normal(ks[5], (L_GNN, D, D), jnp.float32) * s, 'conv_b': jnp.zeros((L_GNN, D), jnp.float32), 'fc_w': jax.random.normal(ks[6], (D, D_OUT), jnp.float32) * s, 'fc_b': jnp.zeros((D_OUT,), jnp.float32)}
    _L0_gnn_all = _L0_gnn_setup()
    _L0_gnn_in = {k: v for k, v in _L0_gnn_all.items() if k in ('t_fc_w', 't_fc_b', 't_ln_g', 't_ln_b', 'qkv_w', 'g_fc_w', 'g_fc_b', 'bn_g', 'bn_b', 'conv_w', 'conv_b', 'fc_w', 'fc_b')}
    del _L0_gnn_all

    def _L1_gnn_setup():
        import jax, jax.numpy as jnp
        import numpy as np
        N_NODES = 100000
        N_EDGES = 25000
        D_X = 128
        D_E = 128
        D_U = 16
        D_IN = D_X + D_E + D_U
        H = 128
        D_OUT = 128
        LN_EPS = 1e-05

        def _layer_norm(x, gamma, beta):
            mu = jnp.mean(x, axis=-1, keepdims=True)
            var = jnp.var(x, axis=-1, keepdims=True)
            return (x - mu) * jax.lax.rsqrt(var + LN_EPS) * gamma + beta
        key = jax.random.key(seed)
        ks = jax.random.split(key, 12)
        x = jax.random.normal(ks[0], (N_NODES, D_X), dtype=jnp.float32)
        edge_attr = jax.random.normal(ks[1], (N_EDGES, D_E), dtype=jnp.float32)
        u = jax.random.normal(ks[2], (1, D_U), dtype=jnp.float32)
        edge_index = jax.random.randint(ks[3], (2, N_EDGES), 0, N_NODES, dtype=jnp.int64)
        batch = jnp.zeros((N_NODES,), dtype=jnp.int64)

        def lin(k, din, dout):
            s = 1.0 / np.sqrt(din)
            kw, kb = jax.random.split(k)
            W = jax.random.uniform(kw, (din, dout), minval=-s, maxval=s, dtype=jnp.float32)
            b = jax.random.uniform(kb, (dout,), minval=-s, maxval=s, dtype=jnp.float32)
            return (W, b)
        W1, b1 = lin(ks[4], D_IN, H)
        W2, b2 = lin(ks[5], H, H)
        W3, b3 = lin(ks[6], H, D_OUT)
        g1 = jnp.ones((H,), jnp.float32)
        be1 = jnp.zeros((H,), jnp.float32)
        g2 = jnp.ones((H,), jnp.float32)
        be2 = jnp.zeros((H,), jnp.float32)
        return {'x': x, 'edge_attr': edge_attr, 'u': u, 'W1': W1, 'b1': b1, 'g1': g1, 'be1': be1, 'W2': W2, 'b2': b2, 'g2': g2, 'be2': be2, 'W3': W3, 'b3': b3, 'edge_index': edge_index, 'batch': batch}
    _L1_gnn_all = _L1_gnn_setup()
    _L1_gnn_in = {k: v for k, v in _L1_gnn_all.items() if k in ('u', 'W1', 'b1', 'g1', 'be1', 'W2', 'b2', 'g2', 'be2', 'W3', 'b3')}
    del _L1_gnn_all

    def _L2_gnn_setup():
        import jax, jax.numpy as jnp
        import numpy as np
        N_NODES = 625
        N_EDGES = 10000
        D = 128
        L = 3
        BN_EPS = 1e-05

        def _bn(x, gamma, beta):
            m = jnp.mean(x, axis=0)
            v = jnp.var(x, axis=0)
            return gamma * (x - m) * jax.lax.rsqrt(v + BN_EPS) + beta
        key = jax.random.key(seed)
        ks = jax.random.split(key, 12)
        return {'h': jax.random.normal(ks[0], (N_NODES, D), dtype=jnp.float32), 'src': jax.random.randint(ks[1], (N_EDGES,), 0, N_NODES, dtype=jnp.int32), 'dst': jax.random.randint(ks[2], (N_EDGES,), 0, N_NODES, dtype=jnp.int32), 'ew': jax.random.uniform(ks[3], (N_EDGES,), dtype=jnp.float32), 'eps_list': jnp.zeros((L,), dtype=jnp.float32), 'W1': jax.random.normal(ks[4], (L, D, D), dtype=jnp.float32) * (1.0 / np.sqrt(D)), 'b1': jax.random.normal(ks[5], (L, D), dtype=jnp.float32) * 0.02, 'g1': jax.random.uniform(ks[6], (L, D), dtype=jnp.float32) + 0.5, 'bt1': jax.random.normal(ks[7], (L, D), dtype=jnp.float32) * 0.02, 'W2': jax.random.normal(ks[8], (L, D, D), dtype=jnp.float32) * (1.0 / np.sqrt(D)), 'b2': jax.random.normal(ks[9], (L, D), dtype=jnp.float32) * 0.02, 'g2': jax.random.uniform(ks[10], (L, D), dtype=jnp.float32) + 0.5, 'bt2': jax.random.normal(ks[11], (L, D), dtype=jnp.float32) * 0.02}
    _L2_gnn_all = _L2_gnn_setup()
    _L2_gnn_in = {k: v for k, v in _L2_gnn_all.items() if k in ('eps_list', 'W1', 'b1', 'g1', 'bt1', 'W2', 'b2', 'g2', 'bt2')}
    del _L2_gnn_all

    def _L3_gnn_setup():
        import jax, jax.numpy as jnp
        import numpy as np
        EPS = 0.0
        key = jax.random.key(seed)
        kx, ke, kw, k1, k2 = jax.random.split(key, 5)
        N, E, D, H = (100000, 9375, 128, 128)
        x = jax.random.normal(kx, (N, D), dtype=jnp.float32)
        edge_index = jax.random.randint(ke, (2, E), 0, N, dtype=jnp.int64)
        edge_weight = jax.random.uniform(kw, (E,), dtype=jnp.float32)
        W1 = jax.random.normal(k1, (D, H), dtype=jnp.float32) * (1.0 / np.sqrt(D))
        b1 = jnp.zeros((H,), dtype=jnp.float32)
        W2 = jax.random.normal(k2, (H, D), dtype=jnp.float32) * (1.0 / np.sqrt(H))
        b2 = jnp.zeros((D,), dtype=jnp.float32)
        return {'x': x, 'edge_index': edge_index, 'edge_weight': edge_weight, 'W1': W1, 'b1': b1, 'W2': W2, 'b2': b2}
    _L3_gnn_all = _L3_gnn_setup()
    _L3_gnn_in = {k: v for k, v in _L3_gnn_all.items() if k in ('W1', 'b1', 'W2', 'b2')}
    del _L3_gnn_all
    return {'x': x, 'src': src, 'dst': dst, 'edge_attr_128': edge_attr_128, 'edge_weight': edge_weight, 'L0_gnn_t_fc_w': _L0_gnn_in['t_fc_w'], 'L0_gnn_t_fc_b': _L0_gnn_in['t_fc_b'], 'L0_gnn_t_ln_g': _L0_gnn_in['t_ln_g'], 'L0_gnn_t_ln_b': _L0_gnn_in['t_ln_b'], 'L0_gnn_qkv_w': _L0_gnn_in['qkv_w'], 'L0_gnn_g_fc_w': _L0_gnn_in['g_fc_w'], 'L0_gnn_g_fc_b': _L0_gnn_in['g_fc_b'], 'L0_gnn_bn_g': _L0_gnn_in['bn_g'], 'L0_gnn_bn_b': _L0_gnn_in['bn_b'], 'L0_gnn_conv_w': _L0_gnn_in['conv_w'], 'L0_gnn_conv_b': _L0_gnn_in['conv_b'], 'L0_gnn_fc_w': _L0_gnn_in['fc_w'], 'L0_gnn_fc_b': _L0_gnn_in['fc_b'], 'L1_gnn_u': _L1_gnn_in['u'], 'L1_gnn_W1': _L1_gnn_in['W1'], 'L1_gnn_b1': _L1_gnn_in['b1'], 'L1_gnn_g1': _L1_gnn_in['g1'], 'L1_gnn_be1': _L1_gnn_in['be1'], 'L1_gnn_W2': _L1_gnn_in['W2'], 'L1_gnn_b2': _L1_gnn_in['b2'], 'L1_gnn_g2': _L1_gnn_in['g2'], 'L1_gnn_be2': _L1_gnn_in['be2'], 'L1_gnn_W3': _L1_gnn_in['W3'], 'L1_gnn_b3': _L1_gnn_in['b3'], 'L2_gnn_eps_list': _L2_gnn_in['eps_list'], 'L2_gnn_W1': _L2_gnn_in['W1'], 'L2_gnn_b1': _L2_gnn_in['b1'], 'L2_gnn_g1': _L2_gnn_in['g1'], 'L2_gnn_bt1': _L2_gnn_in['bt1'], 'L2_gnn_W2': _L2_gnn_in['W2'], 'L2_gnn_b2': _L2_gnn_in['b2'], 'L2_gnn_g2': _L2_gnn_in['g2'], 'L2_gnn_bt2': _L2_gnn_in['bt2'], 'L3_gnn_W1': _L3_gnn_in['W1'], 'L3_gnn_b1': _L3_gnn_in['b1'], 'L3_gnn_W2': _L3_gnn_in['W2'], 'L3_gnn_b2': _L3_gnn_in['b2']}

def reference(x, src, dst, edge_attr_128, edge_weight, L0_gnn_t_fc_w, L0_gnn_t_fc_b, L0_gnn_t_ln_g, L0_gnn_t_ln_b, L0_gnn_qkv_w, L0_gnn_g_fc_w, L0_gnn_g_fc_b, L0_gnn_bn_g, L0_gnn_bn_b, L0_gnn_conv_w, L0_gnn_conv_b, L0_gnn_fc_w, L0_gnn_fc_b, L1_gnn_u, L1_gnn_W1, L1_gnn_b1, L1_gnn_g1, L1_gnn_be1, L1_gnn_W2, L1_gnn_b2, L1_gnn_g2, L1_gnn_be2, L1_gnn_W3, L1_gnn_b3, L2_gnn_eps_list, L2_gnn_W1, L2_gnn_b1, L2_gnn_g1, L2_gnn_bt1, L2_gnn_W2, L2_gnn_b2, L2_gnn_g2, L2_gnn_bt2, L3_gnn_W1, L3_gnn_b1, L3_gnn_W2, L3_gnn_b2):
    import jax
    import jax.numpy as jnp

    def _L0_gnn_ref(x, edge_index, t_fc_w, t_fc_b, t_ln_g, t_ln_b, qkv_w, g_fc_w, g_fc_b, bn_g, bn_b, conv_w, conv_b, fc_w, fc_b):
        import jax, jax.numpy as jnp
        import numpy as np
        N_NODES = 50000
        N_EDGES = 500000
        D = 128
        D_OUT = 128
        L_TRANS = 2
        L_GNN = 3
        EPS_LN = 1e-05
        EPS_BN = 1e-05

        def _ln(x, g, b):
            mu = jnp.mean(x, axis=-1, keepdims=True)
            var = jnp.mean(jnp.square(x - mu), axis=-1, keepdims=True)
            return (x - mu) * jax.lax.rsqrt(var + EPS_LN) * g + b

        def _bn_eval(x, g, b):
            return x * (g / np.sqrt(1.0 + EPS_BN)) + b

        def _attn(x, wq, wk, wv):
            n = x.shape[0]
            q = x @ wq
            k = x @ wk
            v = x @ wv
            eps = 1e-06
            q = jnp.where(q == 0, eps, q)
            k = jnp.where(k == 0, eps, k)
            q = q / jnp.linalg.norm(q, axis=-1, keepdims=True)
            k = k / jnp.linalg.norm(k, axis=-1, keepdims=True)
            kv = jnp.einsum('lm,ld->md', k, v)
            num = q @ kv + n * v
            denom = q @ jnp.sum(k, axis=0) + n
            return num / denom[:, None]

        def _gcn(x, edge_index, w, b, n):
            sl = jnp.arange(n, dtype=edge_index.dtype)
            row = jnp.concatenate([edge_index[0], sl])
            col = jnp.concatenate([edge_index[1], sl])
            deg = jax.ops.segment_sum(jnp.ones_like(col, dtype=x.dtype), col, num_segments=n)
            dinv = jnp.where(deg > 0, jax.lax.rsqrt(deg), 0.0)
            norm = dinv[row] * dinv[col]
            xw = x @ w
            out = jax.ops.segment_sum(norm[:, None] * xw[row], col, num_segments=n)
            return out + b
        n = x.shape[0]
        h = jax.nn.relu(_ln(x @ t_fc_w + t_fc_b, t_ln_g[0], t_ln_b[0]))
        layers = [h]
        cur = h
        for i in range(L_TRANS):
            a = _attn(cur, qkv_w[i, 0], qkv_w[i, 1], qkv_w[i, 2])
            cur = jax.nn.relu(_ln((a + layers[i]) * 0.5, t_ln_g[i + 1], t_ln_b[i + 1]))
            layers.append(cur)
        x1 = cur
        g = jax.nn.relu(_bn_eval(x @ g_fc_w + g_fc_b, bn_g[0], bn_b[0]))
        last = g
        for i in range(L_GNN):
            g = _gcn(g, edge_index, conv_w[i], conv_b[i], n)
            g = jax.nn.relu(_bn_eval(g, bn_g[i + 1], bn_b[i + 1])) + last
        x2 = g
        return (0.5 * x2 + 0.5 * x1) @ fc_w + fc_b

    def _L1_gnn_ref(x, edge_attr, u, W1, b1, g1, be1, W2, b2, g2, be2, W3, b3, edge_index, batch):
        import jax, jax.numpy as jnp
        import numpy as np
        N_NODES = 100000
        N_EDGES = 25000
        D_X = 128
        D_E = 128
        D_U = 16
        D_IN = D_X + D_E + D_U
        H = 128
        D_OUT = 128
        LN_EPS = 1e-05

        def _layer_norm(x, gamma, beta):
            mu = jnp.mean(x, axis=-1, keepdims=True)
            var = jnp.var(x, axis=-1, keepdims=True)
            return (x - mu) * jax.lax.rsqrt(var + LN_EPS) * gamma + beta
        edge_dst = edge_index[1]
        agg = jax.ops.segment_sum(edge_attr, edge_dst, num_segments=x.shape[0])
        u_exp = jnp.broadcast_to(u, (x.shape[0], u.shape[1]))
        h = jnp.concatenate([x, agg, u_exp], axis=1)
        h = _layer_norm(jax.nn.relu(h @ W1 + b1), g1, be1)
        h = _layer_norm(jax.nn.relu(h @ W2 + b2), g2, be2)
        return h @ W3 + b3

    def _L2_gnn_ref(h, src, dst, ew, eps_list, W1, b1, g1, bt1, W2, b2, g2, bt2):
        import jax, jax.numpy as jnp
        import numpy as np
        N_NODES = 625
        N_EDGES = 10000
        D = 128
        L = 3
        BN_EPS = 1e-05

        def _bn(x, gamma, beta):
            m = jnp.mean(x, axis=0)
            v = jnp.var(x, axis=0)
            return gamma * (x - m) * jax.lax.rsqrt(v + BN_EPS) + beta
        n = h.shape[0]
        for l in range(L):
            msg = ew[:, None] * h[src]
            agg = jax.ops.segment_sum(msg, dst, num_segments=n)
            x = (1.0 + eps_list[l]) * h + agg
            t = jax.nn.relu(_bn(x @ W1[l] + b1[l], g1[l], bt1[l]))
            t = jax.nn.relu(t @ W2[l] + b2[l])
            h = jax.nn.relu(_bn(t, g2[l], bt2[l]))
        return h

    def _L3_gnn_ref(x, edge_index, edge_weight, W1, b1, W2, b2):
        import jax, jax.numpy as jnp
        import numpy as np
        EPS = 0.0
        N = x.shape[0]
        src, dst = (edge_index[0], edge_index[1])
        msg = edge_weight[:, None] * x[src]
        agg = jax.ops.segment_sum(msg, dst, num_segments=N)
        out = (1.0 + EPS) * x + agg
        h = jax.nn.relu(out @ W1 + b1)
        return h @ W2 + b2
    edge_index = jnp.stack([src, dst])
    batch0 = jnp.zeros((50000,), jnp.int32)
    h = jnp.maximum(_layernorm(x, axis=-1), 0.0)
    x = x + _L0_gnn_ref(h, edge_index, L0_gnn_t_fc_w, L0_gnn_t_fc_b, L0_gnn_t_ln_g, L0_gnn_t_ln_b, L0_gnn_qkv_w, L0_gnn_g_fc_w, L0_gnn_g_fc_b, L0_gnn_bn_g, L0_gnn_bn_b, L0_gnn_conv_w, L0_gnn_conv_b, L0_gnn_fc_w, L0_gnn_fc_b)
    h = jnp.maximum(_layernorm(x, axis=-1), 0.0)
    x = x + _L1_gnn_ref(h, edge_attr_128, L1_gnn_u, L1_gnn_W1, L1_gnn_b1, L1_gnn_g1, L1_gnn_be1, L1_gnn_W2, L1_gnn_b2, L1_gnn_g2, L1_gnn_be2, L1_gnn_W3, L1_gnn_b3, edge_index, batch0)
    h = jnp.maximum(_layernorm(x, axis=-1), 0.0)
    x = x + _L2_gnn_ref(h, src, dst, edge_weight, L2_gnn_eps_list, L2_gnn_W1, L2_gnn_b1, L2_gnn_g1, L2_gnn_bt1, L2_gnn_W2, L2_gnn_b2, L2_gnn_g2, L2_gnn_bt2)
    h = jnp.maximum(_layernorm(x, axis=-1), 0.0)
    x = x + _L3_gnn_ref(h, edge_index, edge_weight, L3_gnn_W1, L3_gnn_b1, L3_gnn_W2, L3_gnn_b2)
    return x

_drawn_inputs = setup_inputs


def setup_inputs(seed=0):
    import zlib

    import numpy as np

    out = dict(_drawn_inputs(seed))
    spreads = {'L0_gnn_t_fc_b': (0.0, 0.1),
     'L0_gnn_t_ln_g': (1.0, 0.2),
     'L0_gnn_t_ln_b': (0.0, 0.1),
     'L0_gnn_g_fc_b': (0.0, 0.1),
     'L0_gnn_bn_g': (1.0, 0.2),
     'L0_gnn_bn_b': (0.0, 0.1),
     'L0_gnn_conv_b': (0.0, 0.1),
     'L0_gnn_fc_b': (0.0, 0.1),
     'L1_gnn_g1': (1.0, 0.2),
     'L1_gnn_be1': (0.0, 0.1),
     'L1_gnn_g2': (1.0, 0.2),
     'L1_gnn_be2': (0.0, 0.1),
     'L2_gnn_eps_list': (0.0, 0.1),
     'L3_gnn_b1': (0.0, 0.1),
     'L3_gnn_b2': (0.0, 0.1)}
    factors = {'L2_gnn_b1': 8.0, 'L2_gnn_bt2': 3.038}
    for name, (base, spread) in spreads.items():
        noise = np.random.default_rng([zlib.crc32(name.encode()), seed]).standard_normal(out[name].shape)
        drawn = base * np.exp(spread * noise) if base else spread * noise
        out[name] = jnp.asarray(drawn.astype(out[name].dtype))
    for name, factor in factors.items():
        out[name] = (out[name] * factor).astype(out[name].dtype)
    return out
```

```python
from contextlib import ExitStack

import concourse.bass as bass
from concourse import mybir

F32 = mybir.dt.float32
BF16 = mybir.dt.bfloat16
I32 = mybir.dt.int32
ALU = mybir.AluOpType
ACT = mybir.ActivationFunctionType
AX = mybir.AxisListType

D = 128
P = 128
J = 4
GROUP = P * J
EP = 125
RING = 5
LN_EPS = 1e-5
GUARD = 1e6


class Marks:

    def __init__(self, eng, sem):
        self.eng, self.sem, self.n, self.per_step, self.i = eng, sem, 0, None, 0

    def step(self, i):
        if self.per_step is None and not (isinstance(i, int) and i == 0):
            self.per_step = self.n
        self.i, self.n = i, 0

    def up(self, instruction):
        instruction.then_inc(self.sem, 1)
        self.n += 1

    def wait(self):
        base = 0 if self.per_step is None else self.i * self.per_step
        self.eng.wait_ge(self.sem, base + self.n)

    def settle(self):
        self.wait()
        self.eng.sem_inc(self.sem, 1)
        self.n += 1


def sweep(eng, steps, body):
    body(0)
    if steps > 2:
        with eng.Fori(1, steps - 1) as i:
            body(i)
    body(steps - 1)


def build(nc, t, out):
    x_in = t["x"]
    N = x_in.shape[0]
    E = t["src"].shape[0]
    G = -(-N // GROUP)
    PAIRS = G // 2
    TAILP = (N - GROUP * (G - 1)) // J
    TILES = E // EP
    NPAD = G * GROUP
    assert G % 2 == 0 and TAILP * J == N - GROUP * (G - 1) and TILES * EP == E and TILES % RING == 0
    EITER = TILES // RING

    def dram(name, shape):
        return nc.dram_tensor(name, shape, F32).ap()

    def grouped(buf):
        return buf[0:NPAD, :].rearrange("(g p j) d -> g p (j d)", p=P, j=J)

    full = (N // GROUP) * GROUP
    x_groups = x_in[0:full, :].rearrange("(g p j) d -> g p (j d)", p=P, j=J)
    x_tail = x_in[full:N, :].rearrange("(p j) d -> p (j d)", j=J)
    out_groups = out[0:full, :].rearrange("(g p j) d -> g p (j d)", p=P, j=J)
    out_tail = out[full:N, :].rearrange("(p j) d -> p (j d)", j=J)

    def at(view, g):
        return view[g, :, :] if isinstance(g, int) else view[bass.ds(g, 1), :, :].rearrange("a p f -> (a p) f")

    table = [dram(f"table{k}", [NPAD + P, D]) for k in range(2)]
    cur = [dram(f"cur{k}", [G, P, GROUP]) for k in range(2)]
    g_first = dram("g_first", [G, P, GROUP])
    xres = [dram(f"xres{k}", [NPAD, D]) for k in range(2)]
    degree = dram("degree", [NPAD + P, 1])

    top = ExitStack()
    with top:
        def keep(name, shape, dt=F32):
            return top.enter_context(nc.sbuf_tensor(name, shape, dt))

        ident = keep("ident", [P, P])
        ones3 = keep("ones3", [3, P], BF16)
        onescol = keep("onescol", [P, 1])
        zrow = keep("zrow", [P, D])
        same = keep("same", [EP, TILES, EP], BF16)
        added = keep("added", [EP, TILES, D])
        src_i = keep("src_i", [EP, TILES], I32)
        dst_i = keep("dst_i", [EP, TILES], I32)
        put_i = keep("put_i", [EP, TILES], I32)
        gcn_coef = keep("gcn_coef", [EP, TILES])
        edge_w = keep("edge_w", [EP, TILES])
        dinv2 = keep("dinv2", [P, G * J])
        NCOL = 48
        cols = keep("cols", [P, NCOL])
        col_at = {}

        def col(name):
            if name not in col_at:
                col_at[name] = len(col_at)
                assert len(col_at) <= NCOL
            c = col_at[name]
            return cols[:, c:c + 1]
        BIASES = ["t_fc", "fc", "l1c", "l1b2", "l1b3", "l3b2"]
        bias3 = keep("bias3", [3, len(BIASES), GROUP], BF16)
        kvsum = keep("kvsum", [P, D + 1])
        bnstat = keep("bnstat", [P, (G + 1) * J, 6])

        def bias(name):
            return bias3[:, BIASES.index(name), :]

        stage = [""]
        pool_sems = {}
        base = {}

        def before_stage(k):
            return base.get(k, 0)

        def pool_dma_sem(k):
            if k not in pool_sems:
                pool_sems[k] = top.enter_context(nc.semaphore(k))
            return pool_sems[k]

        def run_block(name, sems, emit, sw_counts=None):
            stage[0] = name
            with ExitStack() as ctx:
                s = {k: pool_dma_sem(k) if k.startswith("sw_") else ctx.enter_context(nc.semaphore(f"{name}_{k}"))
                     for k in sems}
                with nc.Block() as block:
                    emit(ctx, block, s)
                nums = [v for k, v in s.items() if not k.startswith("sw_")]
                nc.all_engine_barrier()
                for k in sems:
                    if k.startswith("sw_"):
                        base[k] = base.get(k, 0) + sw_counts[k]
                for v in nums:
                    nc.gpsimd.sem_clear(v)
                nc.all_engine_barrier()

        COLS = {
            "bng0": t["L0_gnn_bn_g"][0], "bnb0": t["L0_gnn_bn_b"][0], "gfcb": t["L0_gnn_g_fc_b"],
            "b1L3": t["L3_gnn_b1"], "g1L1": t["L1_gnn_g1"], "be1L1": t["L1_gnn_be1"],
            "g2L1": t["L1_gnn_g2"], "be2L1": t["L1_gnn_be2"],
        }
        for k in range(3):
            COLS[f"lng{k}"] = t["L0_gnn_t_ln_g"][k]
            COLS[f"lnb{k}"] = t["L0_gnn_t_ln_b"][k]
            COLS[f"bng{k + 1}"] = t["L0_gnn_bn_g"][k + 1]
            COLS[f"bnb{k + 1}"] = t["L0_gnn_bn_b"][k + 1]
            COLS[f"cb{k}"] = t["L0_gnn_conv_b"][k]
            for n in ("b1", "b2", "g1", "bt1", "g2", "bt2"):
                COLS[f"{n}_{k}"] = t[f"L2_gnn_{n}"][k]
        for n in COLS:
            col(n)
        NCOLS_IN = len(COLS)
        eps1 = keep("eps1", [P, 3])
        bnsc = keep("bnsc", [P, 4])
        bnbi = keep("bnbi", [P, 4])

        def prepare(ctx, block, s):
            def sb(name, shape, dt=F32):
                return ctx.enter_context(nc.sbuf_tensor(f"{stage[0]}_{name}", shape, dt))
            brow = sb("brow", [3, len(BIASES), D])
            rest = sb("rest", [3, len(BIASES), D])
            hi = sb("hi", [3, len(BIASES), D], BF16)
            mid = sb("mid", [3, len(BIASES), D], BF16)
            lo = sb("lo", [3, len(BIASES), D], BF16)
            pick = sb("pick", [3, len(BIASES), D])
            pick2 = sb("pick2", [3, len(BIASES), D])
            ucol = sb("ucol", [16, 1])
            u3 = sb("u3", [16, 3])
            w1c = sb("w1c", [16, D])
            ones = sb("ones", [P, (NPAD + P) // P])
            psc = ctx.enter_context(nc.psum_tensor(f"{stage[0]}_psc", [P, D], F32))

            @block.gpsimd
            def _(pool):
                nc.gpsimd.memset(ident[:], 0.0).then_inc(s["pz"], 1)
                pool.wait_ge(s["pz"], 1)
                nc.gpsimd.affine_select(out=ident[:], in_=ident[:], compare_op=ALU.not_equal, fill=1.0,
                                        base=0, pattern=[[-1, P]], channel_multiplier=1).then_inc(s["pi"], 1)

            @block.sync
            def _(sp):
                n = 0
                for name, v in COLS.items():
                    sp.dma_start(col(name), v.rearrange("(p a) -> p a", a=1)).then_inc(s["ld"], 16)
                    n += 1
                rows = {"t_fc": t["L0_gnn_t_fc_b"], "fc": t["L0_gnn_fc_b"], "l1c": t["L1_gnn_b1"],
                        "l1b2": t["L1_gnn_b2"], "l1b3": t["L1_gnn_b3"], "l3b2": t["L3_gnn_b2"]}
                for name, v in rows.items():
                    for k in range(3):
                        sp.dma_start(brow[k:k + 1, BIASES.index(name), :],
                                     v.rearrange("(a d) -> a d", a=1)).then_inc(s["ld"], 16)
                        n += 1
                sp.dma_start(ucol[:], t["L1_gnn_u"].rearrange("a d -> d a")).then_inc(s["ld"], 16)
                sp.dma_start(w1c[:], t["L1_gnn_W1"][2 * D:2 * D + 16, :]).then_inc(s["ld"], 16)
                sp.dma_start(eps1[:], t["L2_gnn_eps_list"].partition_broadcast(P)).then_inc(s["ld"], 16)
                sp.dma_start(src_i[:], t["src"].rearrange("(p c) -> p c", p=EP)).then_inc(s["ld"], 16)
                sp.dma_start(dst_i[:], t["dst"].rearrange("(p c) -> p c", p=EP)).then_inc(s["ld"], 16)
                sp.dma_start(edge_w[:], t["edge_weight"].rearrange("(p c) -> p c", p=EP)).then_inc(s["ld"], 16)
                assert n + 6 == len(COLS) + 3 * len(BIASES) + 6
                sp.wait_ge(s["set"], 1)
                for k in range(2):
                    sp.dma_start(table[k][NPAD:NPAD + P, :], zrow[:]).then_inc(s["st"], 16)
                sp.dma_start(degree.rearrange("(p c) a -> p (c a)", p=P), ones[:]).then_inc(s["st"], 16)
                sp.wait_ge(s["st"], 48)

            LOADS = 16 * (len(COLS) + 3 * len(BIASES) + 6)

            @block.tensor
            def _(pe):
                pe.wait_ge(s["u3"], 1)
                nc.tensor.matmul(psc[0:3, :], u3[:], w1c[:], start=True, stop=True).then_inc(s["mm"], 1)

            @block.vector
            def _(dve):
                m = Marks(dve, s["dv"])

                def link(ins):
                    m.up(ins)
                    m.wait()
                nc.vector.memset(zrow[:], 0.0)
                nc.vector.memset(ones[:], 1.0).then_inc(s["set"], 1)
                nc.vector.memset(onescol[:], 1.0)
                link(nc.vector.memset(ones3[:], 1.0))
                dve.wait_ge(s["ld"], LOADS)
                nc.vector.tensor_copy(u3[:], ucol[:, 0:1].to_broadcast([16, 3])).then_inc(s["u3"], 1)
                dve.wait_ge(s["mm"], 1)
                c = BIASES.index("l1c")
                link(nc.vector.tensor_tensor(brow[:, c, :], psc[0:3, :], brow[:, c, :], ALU.add))
                link(nc.vector.tensor_scalar(eps1[:], eps1[:], 1.0, None, ALU.add))
                link(nc.vector.tensor_copy(hi[:], brow[:]))
                link(nc.vector.tensor_tensor(rest[:], brow[:], hi[:], ALU.subtract))
                link(nc.vector.tensor_copy(mid[:], rest[:]))
                link(nc.vector.tensor_tensor(rest[:], rest[:], mid[:], ALU.subtract))
                link(nc.vector.tensor_copy(lo[:], rest[:]))
                dve.wait_ge(s["pi"], 1)
                link(nc.vector.tensor_scalar(pick[:], hi[:], ident[0:3, 0:1], None, ALU.mult))
                link(nc.vector.scalar_tensor_tensor(out=pick2[:], in0=mid[:], scalar=ident[0:3, 1:2], in1=pick[:],
                                                    op0=ALU.mult, op1=ALU.add))
                link(nc.vector.scalar_tensor_tensor(out=pick[:], in0=lo[:], scalar=ident[0:3, 2:3], in1=pick2[:],
                                                    op0=ALU.mult, op1=ALU.add))
                for j in range(J):
                    link(nc.vector.tensor_copy(bias3[:, :, j * D:(j + 1) * D], pick[:]))
                for k in range(4):
                    b = col("gfcb") if k == 0 else col(f"cb{k - 1}")
                    link(nc.vector.tensor_scalar(bnsc[:, k:k + 1], col(f"bng{k}"), (1.0 + 1e-5) ** -0.5, None, ALU.mult))
                    link(nc.vector.scalar_tensor_tensor(out=bnbi[:, k:k + 1], in0=b, scalar=bnsc[:, k:k + 1],
                                                        in1=col(f"bnb{k}"), op0=ALU.mult, op1=ALU.add))
        run_block("prep", ["pz", "pi", "ld", "set", "st", "u3", "mm", "dv"], prepare)

        dstf = keep("dstf", [EP, TILES])
        count = keep("count", [EP, TILES])
        before = keep("before", [EP, TILES])

        def match_edges(ctx, block, s):
            def sb(name, shape, dt=F32):
                return ctx.enter_context(nc.sbuf_tensor(f"{stage[0]}_{name}", shape, dt))
            lower = sb("lower", [EP, EP])
            spare = sb("spare", [EP, TILES])
            tmp = sb("tmp", [EP, TILES])
            late = sb("late", [EP, TILES])
            wide = [sb(f"wide{r}", [EP, EP]) for r in range(RING)]
            eq = [sb(f"eq{r}", [EP, EP]) for r in range(RING)]
            low = [sb(f"low{r}", [EP, EP]) for r in range(RING)]
            ps = [ctx.enter_context(nc.psum_tensor(f"{stage[0]}_ps{r}", [P, 512], F32)) for r in range(RING)]

            @block.gpsimd
            def _(pool):
                nc.gpsimd.memset(lower[:], 1.0).then_inc(s["pc"], 1)
                pool.wait_ge(s["pc"], 1)
                nc.gpsimd.affine_select(out=lower[:], in_=lower[:], compare_op=ALU.is_gt, fill=0.0,
                                        base=0, pattern=[[-1, EP]], channel_multiplier=1).then_inc(s["pc"], 1)
                nc.gpsimd.iota(spare[:], [[0, TILES]], base=NPAD, channel_multiplier=1,
                               allow_small_or_imprecise_dtypes=True).then_inc(s["pc"], 1)

            @block.tensor
            def _(pe):
                def body(i):
                    for r in range(RING):
                        pe.wait_ge(s["wide"], RING * i + r + 1)
                        if not (isinstance(i, int) and i == 0):
                            pe.wait_ge(s["eq"], RING * i + r + 1 - RING)
                        nc.tensor.transpose(ps[r][0:EP, 0:EP], wide[r][:], ident[0:EP, 0:EP]).then_inc(s["tr"], 1)
                sweep(pe, EITER, body)

            @block.vector
            def _(dve):
                m = Marks(dve, s["dv"])

                def link(ins):
                    m.up(ins)
                    m.wait()
                link(nc.vector.tensor_copy(dstf[:], dst_i[:]))
                dve.wait_ge(s["pc"], 3)

                def body(i):
                    for r in range(RING):
                        t_ = RING * i + r
                        if not (isinstance(i, int) and i == 0):
                            dve.wait_ge(s["tr"], RING * i + r + 1 - RING)
                        d = dstf[:, bass.ds(t_, 1)]
                        nc.vector.tensor_copy(wide[r][:], d.to_broadcast([EP, EP])).then_inc(s["wide"], 1)
                    for r in range(RING):
                        t_ = RING * i + r
                        dve.wait_ge(s["tr"], RING * i + r + 1)
                        nc.vector.tensor_scalar(eq[r][:], ps[r][0:EP, 0:EP], dstf[:, bass.ds(t_, 1)], None,
                                                ALU.is_equal).then_inc(s["eq"], 1)
                    for r in range(RING):
                        t_ = RING * i + r
                        dve.wait_ge(s["eq"], RING * i + r + 1)
                        nc.vector.tensor_copy(same[:, bass.ds(t_, 1), :].rearrange("p a f -> p (a f)"), eq[r][:])
                        nc.vector.tensor_reduce(count[:, bass.ds(t_, 1)], eq[r][:], AX.X, ALU.add)
                        nc.vector.tensor_tensor(low[r][:], eq[r][:], lower[:], ALU.mult).then_inc(s["low"], 1)
                    for r in range(RING):
                        t_ = RING * i + r
                        dve.wait_ge(s["low"], RING * i + r + 1)
                        nc.vector.tensor_reduce(before[:, bass.ds(t_, 1)], low[r][:], AX.X, ALU.add).then_inc(s["red"], 1)
                sweep(dve, EITER, body)
                dve.wait_ge(s["red"], TILES)
                link(nc.vector.tensor_scalar(late[:], before[:], 0.5, None, ALU.is_gt))
                link(nc.vector.tensor_tensor(tmp[:], spare[:], dstf[:], ALU.subtract))
                link(nc.vector.tensor_tensor(tmp[:], tmp[:], late[:], ALU.mult))
                link(nc.vector.tensor_tensor(tmp[:], tmp[:], dstf[:], ALU.add))
                link(nc.vector.tensor_copy(put_i[:], tmp[:]))
        run_block("match", ["pc", "wide", "tr", "eq", "low", "red", "dv"], match_edges)

        def count_degrees(ctx, block, s):
            def sb(name, shape, dt=F32):
                return ctx.enter_context(nc.sbuf_tensor(f"{stage[0]}_{name}", shape, dt))
            put = [sb(f"put{r}", [EP, 1], I32) for r in range(RING)]
            num = [sb(f"num{r}", [EP, 1]) for r in range(RING)]
            si = [sb(f"si{r}", [EP, 1], I32) for r in range(RING)]
            di = [sb(f"di{r}", [EP, 1], I32) for r in range(RING)]
            gs = [sb(f"gs{r}", [EP, 1]) for r in range(RING)]
            gd = [sb(f"gd{r}", [EP, 1]) for r in range(RING)]
            deg_s = sb("deg_s", [EP, TILES])
            deg_d = sb("deg_d", [EP, TILES])
            deg_n = sb("deg_n", [P, G, J])
            ratio = sb("ratio", [EP, TILES])

            @block.gpsimd
            def _(pool):
                def add_counts(i):
                    for r in range(RING):
                        pool.wait_ge(s["stage"], RING * i + r + 1)
                        if not (isinstance(i, int) and i == 0 and r == 0):
                            pool.wait_ge(s["sw_added"], before_stage("sw_added") + 16 * (RING * i + r))
                        pool.sem_inc(s["pace"], 1)
                        nc.gpsimd.indirect_dma_start(degree, bass.IndirectOffsetOnAxis(put[r][:, 0:1], 0), num[r][:], None,
                                                     compute_op=ALU.add).then_inc(s["sw_added"], 16)
                sweep(pool, EITER, add_counts)
                pool.wait_ge(s["sw_added"], before_stage("sw_added") + 16 * TILES)
                pool.dma_start(deg_n[:], degree[0:NPAD, :].rearrange("(g p j) a -> p g (j a)", p=P, j=J)).then_inc(s["sw_dn"], 16)

                def read_degrees(i):
                    for r in range(RING):
                        pool.wait_ge(s["stage2"], RING * i + r + 1)
                        pool.sem_inc(s["pace"], 1)
                        nc.gpsimd.indirect_dma_start(gs[r][:], None, degree, bass.IndirectOffsetOnAxis(si[r][:, 0:1], 0)
                                                     ).then_inc(s[f"sw_got{r}"], 16)
                        nc.gpsimd.indirect_dma_start(gd[r][:], None, degree, bass.IndirectOffsetOnAxis(di[r][:, 0:1], 0)
                                                     ).then_inc(s[f"sw_got{r}"], 16)
                sweep(pool, EITER, read_degrees)

            @block.vector
            def _(dve):
                def stage(i):
                    for r in range(RING):
                        t_ = RING * i + r
                        if not (isinstance(i, int) and i == 0):
                            dve.wait_ge(s["sw_added"], before_stage("sw_added") + 16 * (RING * i + r + 1 - RING))
                        nc.vector.tensor_copy(put[r][:], put_i[:, bass.ds(t_, 1)])
                        nc.vector.tensor_copy(num[r][:], count[:, bass.ds(t_, 1)]).then_inc(s["stage"], 1)
                sweep(dve, EITER, stage)

                def stage2(i):
                    for r in range(RING):
                        t_ = RING * i + r
                        nc.vector.tensor_copy(si[r][:], src_i[:, bass.ds(t_, 1)])
                        nc.vector.tensor_copy(di[r][:], dst_i[:, bass.ds(t_, 1)]).then_inc(s["stage2"], 1)
                    for r in range(RING):
                        t_ = RING * i + r
                        dve.wait_ge(s[f"sw_got{r}"], before_stage(f"sw_got{r}") + 32 * (i + 1))
                        nc.vector.tensor_copy(deg_s[:, bass.ds(t_, 1)], gs[r][:])
                        nc.vector.tensor_copy(deg_d[:, bass.ds(t_, 1)], gd[r][:]).then_inc(s["cp"], 1)
                sweep(dve, EITER, stage2)
                dve.wait_ge(s["sw_dn"], before_stage("sw_dn") + 16)
                nc.vector.reciprocal(dinv2[:], deg_n[:].rearrange("p g j -> p (g j)"))
                dve.wait_ge(s["cp"], TILES)
                nc.vector.reciprocal(ratio[:], deg_s[:]).then_inc(s["dv"], 1)
                dve.wait_ge(s["dv"], 1)
                nc.vector.tensor_tensor(ratio[:], ratio[:], deg_d[:], ALU.mult).then_inc(s["ratio"], 1)

            @block.scalar
            def _(act):
                act.wait_ge(s["ratio"], 1)
                nc.scalar.activation(gcn_coef[:], ratio[:], ACT.Sqrt)
        run_block("degree", ["stage", "sw_added", "sw_dn", "stage2", "cp", "ratio", "pace", "dv"] + [f"sw_got{r}" for r in range(RING)],
                  count_degrees, {"sw_added": 16 * TILES, "sw_dn": 16, **{f"sw_got{r}": 32 * EITER for r in range(RING)}})


        SLOTS = (0, 1)

        def first_step(i):
            return isinstance(i, int) and i == 0

        def last_step(i):
            return isinstance(i, int) and i == PAIRS - 1

        def is_tail(i, b):
            return last_step(i) and b == 1

        def nth(i, b):
            return 2 * i + b + 1

        def again(eng, sem, i, b):
            if not first_step(i):
                eng.wait_ge(sem, 2 * i + b - 1)

        def turn4(ps, src):
            for j in range(J):
                last = nc.tensor.transpose(ps[:, j * D:(j + 1) * D], src[:, j * D:(j + 1) * D], ident[:])
            return last

        def rows4(ps, feat, w, bias_name=None):
            if bias_name:
                nc.tensor.matmul(ps[:], ones3[:], bias(bias_name), start=True, stop=False)
            for j in range(J):
                last = nc.tensor.matmul(ps[:, j * D:(j + 1) * D], feat[:, j * D:(j + 1) * D], w[:],
                                        start=not bias_name, stop=True if not bias_name else j == J - 1)
            return last

        def norm_tiles(sb, name):
            return dict(st=[sb(f"{name}st{b}", [P, J, 6]) for b in SLOTS], mv=sb(f"{name}mv", [P, 2, J, 2]),
                        sd=sb(f"{name}sd", [P, 2, J]), rs=sb(f"{name}rs", [P, 2, J]))

        def norm_on_dve(dve, m, i, T, src, dst, ready, var, std, done):
            for b in SLOTS:
                ready(b)
                for j in range(J):
                    last = nc.vector.bn_stats(T["st"][b][:, j, :], src[b][:, j * D:(j + 1) * D])
                m.up(last)
            m.settle()
            for b in SLOTS:
                for j in range(J):
                    last = nc.vector.bn_aggr(T["mv"][:, b, j, :], T["st"][b][:, j, :])
            last.then_inc(var, 1)
            dve.wait_ge(std, i + 1)
            m.up(nc.vector.reciprocal(T["rs"][:], T["sd"][:]))
            m.wait()
            for b in SLOTS:
                for j in range(J):
                    last = nc.vector.tensor_scalar(dst[b][:, j * D:(j + 1) * D], src[b][:, j * D:(j + 1) * D],
                                                   T["mv"][:, b, j, 0:1], T["rs"][:, b, j:j + 1],
                                                   ALU.subtract, ALU.mult)
                last.then_inc(done, 1)

        def root_on_act(act, i, T, var, std, eps):
            act.wait_ge(var, i + 1)
            nc.scalar.activation(T["sd"][:], T["mv"][:, :, :, 1], ACT.Sqrt, bias=eps).then_inc(std, 1)

        epsc = keep("epsc", [P, 3])
        eps_ln, eps_half, eps_zero = epsc[:, 0:1], epsc[:, 1:2], epsc[:, 2:3]

        def weight_tiles(ctx, names):
            return {n: ctx.enter_context(nc.sbuf_tensor(f"{stage[0]}_w_{n}", [P, D], F32)) for n in names}

        def kv_tiles(sb):
            return dict(kc=[sb(f"kc{b}", [P, GROUP]) for b in SLOTS], kf=[sb(f"kf{b}", [P, GROUP]) for b in SLOTS],
                        sk=[sb(f"sk{b}", [P, GROUP]) for b in SLOTS], ss=sb("ss", [P, 2, J]),
                        nk=sb("nk", [P, 2, J]), rk=sb("rk", [P, 2, J]),
                        vs=[sb(f"vs{b}", [P, J, D + 1]) for b in SLOTS])

        KV_SEMS = ["kv", "kc", "kf", "sk", "ss", "nk", "vs", "acc"]

        def kv_on_act(act, s, i, T, k_ps):
            for b in SLOTS:
                act.wait_ge(s["kv"], nth(i, b))
                again(act, s["kf"], i, b)
                nc.scalar.copy(T["kc"][b][:], k_ps[b][:]).then_inc(s["kc"], 1)
            for b in SLOTS:
                act.wait_ge(s["kf"], nth(i, b))
                nc.scalar.activation(T["sk"][b][:], T["kf"][b][:], ACT.Square).then_inc(s["sk"], 1)
            act.wait_ge(s["ss"], i + 1)
            nc.scalar.activation(T["nk"][:], T["ss"][:], ACT.Sqrt).then_inc(s["nk"], 1)

        def kv_on_dve(dve, m, s, i, T, v_ps):
            for b in SLOTS:
                dve.wait_ge(s["kc"], nth(i, b))
                again(dve, s["acc"], i, b)
                nc.vector.scalar_tensor_tensor(out=T["kf"][b][:], in0=T["kc"][b][:], scalar=0.0, in1=T["kc"][b][:],
                                               op0=ALU.is_equal, op1=ALU.add).then_inc(s["kf"], 1)
            for b in SLOTS:
                dve.wait_ge(s["sk"], nth(i, b))
                last = nc.vector.tensor_reduce(T["ss"][:, b, :], T["sk"][b][:].rearrange("p (j d) -> p j d", j=J),
                                               AX.X, ALU.add)
            last.then_inc(s["ss"], 1)
            dve.wait_ge(s["nk"], i + 1)
            m.up(nc.vector.reciprocal(T["rk"][:], T["nk"][:]))
            m.wait()
            for b in SLOTS:
                r = T["rk"][:, b, :]
                nc.vector.tensor_tensor(T["vs"][b][:, :, 0:D], v_ps[b][:].rearrange("p (j d) -> p j d", j=J),
                                        r.unsqueeze(2).to_broadcast([P, J, D]), ALU.mult)
                nc.vector.tensor_copy(T["vs"][b][:, :, D:D + 1], r.unsqueeze(2)).then_inc(s["vs"], 1)

        def kv_on_pe(pe, s, i, T, acc_ps):
            for b in SLOTS:
                pe.wait_ge(s["vs"], nth(i, b))
                rows = TAILP if is_tail(i, b) else P
                for j in range(J):
                    last = nc.tensor.matmul(acc_ps[:, 0:D + 1], T["kf"][b][0:rows, j * D:(j + 1) * D],
                                            T["vs"][b][0:rows, j, :],
                                            start=first_step(i) and b == 0 and j == 0,
                                            stop=is_tail(i, b) and j == J - 1, skip_group_check=True)
                last.then_inc(s["acc"], 1)

        def kv_end(act, s, acc_ps):
            act.wait_ge(s["acc"], G)
            nc.scalar.mul(kvsum[:], acc_ps[:, 0:D + 1], 1.0 / N).then_inc(s["kvdone"], 1)

        def load_and_store(sp, loads, stores):
            def body(i):
                loads(i)
                if not first_step(i):
                    stores(i - 1)
            sweep(sp, PAIRS, body)
            stores(PAIRS - 1)

        W = t["L0_gnn_qkv_w"]

        def pass_first(ctx, block, s):
            def sb(name, shape, dt=F32):
                return ctx.enter_context(nc.sbuf_tensor(f"{stage[0]}_{name}", shape, dt))

            def pair(name):
                return [sb(f"{name}{b}", [P, GROUP]) for b in SLOTS]
            w = weight_tiles(ctx, ["fc", "g", "conv", "k", "v"])
            xt, xn, h0, zn, hT, g0, yo = (pair(n) for n in ("xt", "xn", "h0", "zn", "hT", "g0", "yo"))
            T1, T2, TK = norm_tiles(sb, "n1"), norm_tiles(sb, "n2"), kv_tiles(sb)
            A, B, C = ([ctx.enter_context(nc.psum_tensor(f"{stage[0]}_{n}{b}", [P, GROUP], F32)) for b in SLOTS] for n in "ABC")
            accp = ctx.enter_context(nc.psum_tensor(f"{stage[0]}_accp", [P, GROUP], F32))

            @block.sync
            def _(sp):
                for n, v in (("fc", t["L0_gnn_t_fc_w"]), ("g", t["L0_gnn_g_fc_w"]), ("conv", t["L0_gnn_conv_w"][0]),
                             ("k", W[0, 1]), ("v", W[0, 2])):
                    sp.dma_start(w[n][:], v).then_inc(s["w"], 16)

                def loads(i):
                    for b in SLOTS:
                        again(sp, s["xn"], i, b)
                        if is_tail(i, b):
                            sp.dma_start(xt[b][0:TAILP, :], x_tail).then_inc(s[f"ld{b}"], 16)
                        else:
                            sp.dma_start(xt[b][:], at(x_groups, 2 * i + b)).then_inc(s[f"ld{b}"], 16)

                def stores(i):
                    for b in SLOTS:
                        sp.wait_ge(s["g0"], nth(i, b))
                        sp.dma_start(at(g_first, 2 * i + b), g0[b][:]).then_inc(s[f"g0st{b}"], 16)
                    for b in SLOTS:
                        sp.wait_ge(s["yo"], nth(i, b))
                        sp.dma_start(at(grouped(table[0]), 2 * i + b), yo[b][:]).then_inc(s[f"yost{b}"], 16)
                    for b in SLOTS:
                        sp.wait_ge(s["hT"], nth(i, b))
                        sp.dma_start(at(cur[0], 2 * i + b), hT[b][:]).then_inc(s[f"hTst{b}"], 16)
                load_and_store(sp, loads, stores)
                for b in SLOTS:
                    for n in ("g0st", "hTst", "yost"):
                        sp.wait_ge(s[f"{n}{b}"], 16 * PAIRS)

            @block.tensor
            def _(pe):
                pe.wait_ge(s["w"], 80)
                pe.wait_ge(s["wk"], 1)

                def body(i):
                    for b in SLOTS:
                        pe.wait_ge(s["xn"], nth(i, b))
                        again(pe, s["kc"], i, b)
                        turn4(A[b], xn[b]).then_inc(s["tr"], 1)
                    for b in SLOTS:
                        pe.wait_ge(s["h0"], nth(i, b))
                        rows4(A[b], h0[b], w["fc"], "t_fc").then_inc(s["z"], 1)
                        again(pe, s["vs"], i, b)
                        nc.tensor.matmul(B[b][:], w["g"][:], h0[b][:], start=True, stop=True).then_inc(s["g"], 1)
                    for b in SLOTS:
                        pe.wait_ge(s["g0"], nth(i, b))
                        again(pe, s["yo"], i, b)
                        rows4(C[b], g0[b], w["conv"]).then_inc(s["y"], 1)
                    for b in SLOTS:
                        pe.wait_ge(s["zn"], nth(i, b))
                        turn4(A[b], zn[b]).then_inc(s["tz"], 1)
                    for b in SLOTS:
                        pe.wait_ge(s["hT"], nth(i, b))
                        rows4(A[b], hT[b], w["k"])
                        rows4(B[b], hT[b], w["v"]).then_inc(s["kv"], 1)
                    kv_on_pe(pe, s, i, TK, accp)
                sweep(pe, PAIRS, body)

            @block.scalar
            def _(act):
                def body(i):
                    root_on_act(act, i, T1, s["var1"], s["std1"], eps_ln)
                    for b in SLOTS:
                        act.wait_ge(s["tr"], nth(i, b))
                        again(act, s["g"], i, b)
                        nc.scalar.activation(h0[b][:], A[b][:], ACT.Relu).then_inc(s["h0"], 1)
                    for b in SLOTS:
                        act.wait_ge(s["g"], nth(i, b))
                        if not first_step(i):
                            act.wait_ge(s[f"g0st{b}"], 16 * i)
                        nc.scalar.activation(g0[b][:], B[b][:], ACT.Relu, bias=bnbi[:, 0:1],
                                             scale=bnsc[:, 0:1]).then_inc(s["g0"], 1)
                    root_on_act(act, i, T2, s["var2"], s["std2"], eps_ln)
                    for b in SLOTS:
                        act.wait_ge(s["y"], nth(i, b))
                        if not first_step(i):
                            act.wait_ge(s[f"yost{b}"], 16 * i)
                        nc.scalar.copy(yo[b][:], C[b][:]).then_inc(s["yo"], 1)
                    for b in SLOTS:
                        act.wait_ge(s["tz"], nth(i, b))
                        if not first_step(i):
                            act.wait_ge(s[f"hTst{b}"], 16 * i)
                        nc.scalar.activation(hT[b][:], A[b][:], ACT.Relu, bias=col("lnb0"),
                                             scale=col("lng0")).then_inc(s["hT"], 1)
                    kv_on_act(act, s, i, TK, A)
                sweep(act, PAIRS, body)
                kv_end(act, s, accp)
                act.wait_ge(s["kvdone"], 1)

            @block.vector
            def _(dve):
                m = Marks(dve, s["dv"])
                dve.wait_ge(s["w"], 80)
                nc.vector.tensor_scalar(w["k"][:], w["k"][:], GUARD, None, ALU.mult).then_inc(s["wk"], 1)

                def body(i):
                    m.step(i)

                    def ready1(b):
                        dve.wait_ge(s[f"ld{b}"], 16 * (i + 1))
                        again(dve, s["tr"], i, b)
                    norm_on_dve(dve, m, i, T1, xt, xn, ready1, s["var1"], s["std1"], s["xn"])

                    def ready2(b):
                        dve.wait_ge(s["z"], nth(i, b))
                        again(dve, s["tz"], i, b)
                    norm_on_dve(dve, m, i, T2, A, zn, ready2, s["var2"], s["std2"], s["zn"])
                    kv_on_dve(dve, m, s, i, TK, B)
                sweep(dve, PAIRS, body)

        def st(*names):
            return [f"{n}{b}" for n in names for b in SLOTS]

        def set_eps(ctx, block, s):
            @block.vector
            def _(dve):
                nc.vector.memset(eps_ln, LN_EPS)
                nc.vector.memset(eps_half, 4 * LN_EPS)
                nc.vector.memset(eps_zero, 0.0)
        run_block("eps", [], set_eps)
        run_block("first", ["w", "wk", "xn", "g0", "hT", "yo", "tr", "h0", "z", "g", "y", "zn", "tz", "var1", "std1",
                            "var2", "std2", "dv", "kvdone"] + KV_SEMS + st("ld", "g0st", "hTst", "yost"), pass_first)

        def gather_edges(rows, coef):
            def emit(ctx, block, s):
                def sb(name, shape, dt=F32):
                    return ctx.enter_context(nc.sbuf_tensor(f"{stage[0]}_{name}", shape, dt))
                idx = [sb(f"idx{r}", [EP, 1], I32) for r in range(RING)]
                got = [sb(f"got{r}", [EP, D]) for r in range(RING)]
                mix = [sb(f"mix{r}", [EP, EP]) for r in range(RING)]
                ps = [ctx.enter_context(nc.psum_tensor(f"{stage[0]}_ps{r}", [P, 512], F32)) for r in range(RING)]

                @block.gpsimd
                def _(pool):
                    def body(i):
                        for r in range(RING):
                            pool.wait_ge(s["idx"], RING * i + r + 1)
                            if not first_step(i):
                                pool.wait_ge(s["mm"], RING * i + r + 1 - RING)
                            pool.sem_inc(s["pace"], 1)
                            nc.gpsimd.indirect_dma_start(got[r][:], None, rows, bass.IndirectOffsetOnAxis(idx[r][:, 0:1], 0)
                                                         ).then_inc(s[f"sw_got{r}"], 16)
                    sweep(pool, EITER, body)

                @block.vector
                def _(dve):
                    def body(i):
                        for r in range(RING):
                            tile = RING * i + r
                            if not first_step(i):
                                dve.wait_ge(s[f"sw_got{r}"], before_stage(f"sw_got{r}") + 16 * i)
                                dve.wait_ge(s["mm"], RING * i + r + 1 - RING)
                            nc.vector.tensor_copy(idx[r][:], src_i[:, bass.ds(tile, 1)]).then_inc(s["idx"], 1)
                            nc.vector.tensor_scalar(mix[r][:], same[:, bass.ds(tile, 1), :].rearrange("p a f -> p (a f)"),
                                                    coef[:, bass.ds(tile, 1)], None, ALU.mult).then_inc(s["mix"], 1)
                    sweep(dve, EITER, body)

                @block.tensor
                def _(pe):
                    def body(i):
                        for r in range(RING):
                            pe.wait_ge(s["mix"], RING * i + r + 1)
                            pe.wait_ge(s[f"sw_got{r}"], before_stage(f"sw_got{r}") + 16 * (i + 1))
                            if not first_step(i):
                                pe.wait_ge(s["out"], RING * i + r + 1 - RING)
                            nc.tensor.matmul(ps[r][0:EP, 0:D], mix[r][:], got[r][:], start=True, stop=True).then_inc(s["mm"], 1)
                    sweep(pe, EITER, body)

                @block.scalar
                def _(act):
                    def body(i):
                        for r in range(RING):
                            act.wait_ge(s["mm"], RING * i + r + 1)
                            nc.scalar.copy(added[:, bass.ds(RING * i + r, 1), :].rearrange("p a f -> p (a f)"),
                                           ps[r][0:EP, 0:D]).then_inc(s["out"], 1)
                    sweep(act, EITER, body)
            return ["idx", "mm", "pace", "mix", "out"] + [f"sw_got{r}" for r in range(RING)], emit

        def project_edge_attr(ctx, block, s):
            def sb(name, shape, dt=F32):
                return ctx.enter_context(nc.sbuf_tensor(f"{stage[0]}_{name}", shape, dt))
            w = sb("w_edge", [P, D])
            ea = [sb(f"ea{r}", [EP, D]) for r in range(RING)]
            mix = [sb(f"mix{r}", [EP, EP]) for r in range(RING)]
            sumT = [sb(f"sumT{r}", [P, EP]) for r in range(RING)]
            ps = [ctx.enter_context(nc.psum_tensor(f"{stage[0]}_ps{r}", [P, 512], F32)) for r in range(RING)]
            attr = t["edge_attr_128"].rearrange("(p c) d -> p c d", p=EP)

            @block.sync
            def _(sp):
                sp.dma_start(w[:], t["L1_gnn_W1"][D:2 * D, :]).then_inc(s["w"], 16)

                def body(i):
                    for r in range(RING):
                        if not first_step(i):
                            sp.wait_ge(s["sum"], RING * i + r + 1 - RING)
                        sp.dma_start(ea[r][:], attr[:, bass.ds(RING * i + r, 1), :].rearrange("p a f -> p (a f)")
                                     ).then_inc(s[f"got{r}"], 16)
                sweep(sp, EITER, body)

            @block.vector
            def _(dve):
                def body(i):
                    for r in range(RING):
                        if not first_step(i):
                            dve.wait_ge(s["sum"], RING * i + r + 1 - RING)
                        nc.vector.tensor_copy(mix[r][:], same[:, bass.ds(RING * i + r, 1), :].rearrange("p a f -> p (a f)")
                                              ).then_inc(s["mix"], 1)
                sweep(dve, EITER, body)

            @block.tensor
            def _(pe):
                pe.wait_ge(s["w"], 16)

                def body(i):
                    for r in range(RING):
                        pe.wait_ge(s["mix"], RING * i + r + 1)
                        pe.wait_ge(s[f"got{r}"], 16 * (i + 1))
                        if not first_step(i):
                            pe.wait_ge(s["out"], RING * i + r + 1 - RING)
                        nc.tensor.matmul(ps[r][:, 0:EP], ea[r][:], mix[r][:], start=True, stop=True).then_inc(s["sum"], 1)
                    for r in range(RING):
                        pe.wait_ge(s["sumT"], RING * i + r + 1)
                        nc.tensor.matmul(ps[r][0:EP, 128:128 + D], sumT[r][:], w[:], start=True, stop=True).then_inc(s["mm"], 1)
                sweep(pe, EITER, body)

            @block.scalar
            def _(act):
                def body(i):
                    for r in range(RING):
                        act.wait_ge(s["sum"], RING * i + r + 1)
                        if not first_step(i):
                            act.wait_ge(s["mm"], RING * i + r + 1 - RING)
                        nc.scalar.copy(sumT[r][:], ps[r][:, 0:EP]).then_inc(s["sumT"], 1)
                    for r in range(RING):
                        act.wait_ge(s["mm"], RING * i + r + 1)
                        nc.scalar.copy(added[:, bass.ds(RING * i + r, 1), :].rearrange("p a f -> p (a f)"),
                                       ps[r][0:EP, 128:128 + D]).then_inc(s["out"], 1)
                sweep(act, EITER, body)
        ATTR_SEMS = ["w", "sum", "mix", "sumT", "mm", "out"] + [f"got{r}" for r in range(RING)]

        def add_edges(rows):
            def emit(ctx, block, s):
                def sb(name, shape, dt=F32):
                    return ctx.enter_context(nc.sbuf_tensor(f"{stage[0]}_{name}", shape, dt))
                idx = [sb(f"idx{r}", [EP, 1], I32) for r in range(RING)]
                msg = [sb(f"msg{r}", [EP, D]) for r in range(RING)]

                @block.vector
                def _(dve):
                    def body(i):
                        for r in range(RING):
                            tile = RING * i + r
                            if not first_step(i):
                                dve.wait_ge(s["sw_added"], before_stage("sw_added") + 16 * (RING * i + r + 1 - RING))
                            nc.vector.tensor_copy(idx[r][:], put_i[:, bass.ds(tile, 1)])
                            nc.vector.tensor_copy(msg[r][:], added[:, bass.ds(tile, 1), :].rearrange("p a f -> p (a f)")
                                                  ).then_inc(s["stage"], 1)
                    sweep(dve, EITER, body)

                @block.gpsimd
                def _(pool):
                    def body(i):
                        for r in range(RING):
                            pool.wait_ge(s["stage"], RING * i + r + 1)
                            if not (first_step(i) and r == 0):
                                pool.wait_ge(s["sw_added"], before_stage("sw_added") + 16 * (RING * i + r))
                            pool.sem_inc(s["pace"], 1)
                            nc.gpsimd.indirect_dma_start(rows, bass.IndirectOffsetOnAxis(idx[r][:, 0:1], 0), msg[r][:], None,
                                                         compute_op=ALU.add).then_inc(s["sw_added"], 16)
                    sweep(pool, EITER, body)
                    pool.wait_ge(s["sw_added"], before_stage("sw_added") + 16 * TILES)
            return ["stage", "sw_added", "pace"], emit

        def aggregate(name, source, coef, target):
            run_block(f"{name}_g", *gather_edges(source, coef), {f"sw_got{r}": 16 * EITER for r in range(RING)})
            run_block(f"{name}_a", *add_edges(target), {"sw_added": 16 * TILES})

        def attention(layer):
            source, dest, more = cur[layer], cur[1 - layer], layer == 0

            def emit(ctx, block, s):
                def sb(name, shape, dt=F32):
                    return ctx.enter_context(nc.sbuf_tensor(f"{stage[0]}_{name}", shape, dt))

                def pair(name):
                    return [sb(f"{name}{b}", [P, GROUP]) for b in SLOTS]
                w = weight_tiles(ctx, ["q", "v", "k2", "v2"])
                hT, hn, qc, qf, sq, t1, su, nn, cT = (pair(n) for n in ("hT", "hn", "qc", "qf", "sq", "t1", "su", "nn", "cT"))
                small = {n: sb(n, [P, 2, J]) for n in ("nq", "rq", "cr", "den", "beta", "alpha")}
                T1, TK = norm_tiles(sb, "n1"), kv_tiles(sb)
                A, B, C = ([ctx.enter_context(nc.psum_tensor(f"{stage[0]}_{n}{b}", [P, GROUP], F32)) for b in SLOTS] for n in "ABC")
                accp = ctx.enter_context(nc.psum_tensor(f"{stage[0]}_accp", [P, GROUP], F32))

                @block.sync
                def _(sp):
                    for n, v in (("q", W[layer, 0]), ("v", W[layer, 2]), ("k2", W[1, 1]), ("v2", W[1, 2])):
                        sp.dma_start(w[n][:], v).then_inc(s["w"], 16)

                    def loads(i):
                        for b in SLOTS:
                            again(sp, s["v"], i, b)
                            sp.dma_start(hT[b][:], at(source, 2 * i + b)).then_inc(s[f"ld{b}"], 16)

                    def stores(i):
                        for b in SLOTS:
                            sp.wait_ge(s["cT"], nth(i, b))
                            sp.dma_start(at(dest, 2 * i + b), cT[b][:]).then_inc(s[f"cTst{b}"], 16)
                    load_and_store(sp, loads, stores)
                    for b in SLOTS:
                        sp.wait_ge(s[f"cTst{b}"], 16 * PAIRS)

                @block.tensor
                def _(pe):
                    pe.wait_ge(s["w"], 64)
                    pe.wait_ge(s["wk"], 1)

                    def body(i):
                        for b in SLOTS:
                            pe.wait_ge(s[f"ld{b}"], 16 * (i + 1))
                            if more:
                                again(pe, s["kc"], i, b)
                            else:
                                again(pe, s["t1"], i, b)
                            turn4(A[b], hT[b]).then_inc(s["th"], 1)
                            if not more:
                                again(pe, s["cT"], i, b)
                            nc.tensor.matmul(B[b][:], w["q"][:], hT[b][:], start=True, stop=True).then_inc(s["q"], 1)
                            if more:
                                again(pe, s["vs"], i, b)
                            else:
                                again(pe, s["su"], i, b)
                            rows4(C[b], hT[b], w["v"]).then_inc(s["v"], 1)
                        for b in SLOTS:
                            pe.wait_ge(s["hn"], nth(i, b))
                            pe.wait_ge(s["qf"], nth(i, b))
                            for j in range(J):
                                nc.tensor.matmul(B[b][:, j:j + 1], qf[b][:, j * D:(j + 1) * D], kvsum[:, D:D + 1],
                                                 start=True, stop=True)
                            for j in range(J):
                                last = nc.tensor.matmul(A[b][:, j * D:(j + 1) * D], qf[b][:, j * D:(j + 1) * D],
                                                        kvsum[:, 0:D], start=True, stop=True)
                            last.then_inc(s["p1"], 1)
                        for b in SLOTS:
                            pe.wait_ge(s["sq"], nth(i, b))
                            for j in range(J):
                                last = nc.tensor.matmul(B[b][:, J + j:J + j + 1], sq[b][:, j * D:(j + 1) * D], onescol[:],
                                                        start=True, stop=True)
                            last.then_inc(s["n2"], 1)
                        for b in SLOTS:
                            pe.wait_ge(s["nn"], nth(i, b))
                            turn4(B[b], nn[b]).then_inc(s["tc"], 1)
                        if more:
                            for b in SLOTS:
                                pe.wait_ge(s["cT"], nth(i, b))
                                rows4(A[b], cT[b], w["k2"])
                                rows4(C[b], cT[b], w["v2"]).then_inc(s["kv"], 1)
                            kv_on_pe(pe, s, i, TK, accp)
                    sweep(pe, PAIRS, body)

                @block.scalar
                def _(act):
                    def body(i):
                        for b in SLOTS:
                            act.wait_ge(s["q"], nth(i, b))
                            again(act, s["qf"], i, b)
                            nc.scalar.copy(qc[b][:], B[b][:]).then_inc(s["qc"], 1)
                            again(act, s["t1"], i, b)
                            nc.scalar.copy(hn[b][:], A[b][:]).then_inc(s["hn"], 1)
                        for b in SLOTS:
                            act.wait_ge(s["qf"], nth(i, b))
                            again(act, s["n2"], i, b)
                            nc.scalar.activation(sq[b][:], qf[b][:], ACT.Square).then_inc(s["sq"], 1)
                        for b in SLOTS:
                            act.wait_ge(s["n2"], nth(i, b))
                            nc.scalar.activation(small["nq"][:, b, :], B[b][:, J:2 * J], ACT.Sqrt).then_inc(s["nq"], 1)
                        root_on_act(act, i, T1, s["var1"], s["std1"], eps_half)
                        for b in SLOTS:
                            act.wait_ge(s["tc"], nth(i, b))
                            if not first_step(i):
                                act.wait_ge(s[f"cTst{b}"], 16 * i)
                            nc.scalar.activation(cT[b][:], B[b][:], ACT.Relu, bias=col(f"lnb{layer + 1}"),
                                                 scale=col(f"lng{layer + 1}")).then_inc(s["cT"], 1)
                        if more:
                            kv_on_act(act, s, i, TK, A)
                    sweep(act, PAIRS, body)
                    if more:
                        kv_end(act, s, accp)
                        act.wait_ge(s["kvdone"], 1)

                @block.vector
                def _(dve):
                    m = Marks(dve, s["dv"])
                    dve.wait_ge(s["w"], 64)
                    nc.vector.tensor_scalar(w["q"][:], w["q"][:], GUARD, None, ALU.mult)
                    nc.vector.tensor_scalar(w["k2"][:], w["k2"][:], GUARD, None, ALU.mult).then_inc(s["wk"], 1)

                    def body(i):
                        m.step(i)
                        for b in SLOTS:
                            dve.wait_ge(s["qc"], nth(i, b))
                            again(dve, s["n2"], i, b)
                            again(dve, s["sq"], i, b)
                            nc.vector.scalar_tensor_tensor(out=qf[b][:], in0=qc[b][:], scalar=0.0, in1=qc[b][:],
                                                           op0=ALU.is_equal, op1=ALU.add).then_inc(s["qf"], 1)
                        dve.wait_ge(s["nq"], 2 * i + 2)
                        m.up(nc.vector.reciprocal(small["rq"][:], small["nq"][:]))
                        m.wait()
                        for b in SLOTS:
                            last = nc.vector.tensor_tensor(small["cr"][:, b, :], B[b][:, 0:J], small["rq"][:, b, :], ALU.mult)
                        m.up(last)
                        m.wait()
                        m.up(nc.vector.tensor_scalar(small["den"][:], small["cr"][:], 1.0, None, ALU.add))
                        m.wait()
                        m.up(nc.vector.reciprocal(small["beta"][:], small["den"][:]))
                        m.wait()
                        m.up(nc.vector.tensor_tensor(small["alpha"][:], small["beta"][:], small["rq"][:], ALU.mult))
                        m.wait()
                        for b in SLOTS:
                            for j in range(J):
                                js = slice(j * D, (j + 1) * D)
                                last = nc.vector.scalar_tensor_tensor(
                                    out=t1[b][:, js], in0=A[b][:, js], scalar=small["alpha"][:, b, j:j + 1],
                                    in1=hn[b][:, js], op0=ALU.mult, op1=ALU.add)
                            last.then_inc(s["t1"], 1)
                        for b in SLOTS:
                            dve.wait_ge(s["t1"], nth(i, b))
                            for j in range(J):
                                js = slice(j * D, (j + 1) * D)
                                last = nc.vector.scalar_tensor_tensor(
                                    out=su[b][:, js], in0=C[b][:, js], scalar=small["beta"][:, b, j:j + 1],
                                    in1=t1[b][:, js], op0=ALU.mult, op1=ALU.add)
                            last.then_inc(s["su"], 1)

                        def ready(b):
                            dve.wait_ge(s["su"], nth(i, b))
                            again(dve, s["tc"], i, b)
                        norm_on_dve(dve, m, i, T1, su, nn, ready, s["var1"], s["std1"], s["nn"])
                        if more:
                            kv_on_dve(dve, m, s, i, TK, C)
                    sweep(dve, PAIRS, body)
            return (["w", "wk", "v", "cT", "th", "q", "hn", "qf", "p1", "sq", "n2", "nn", "tc", "qc", "nq", "t1", "su",
                     "var1", "std1", "dv", "kvdone"] + KV_SEMS + st("ld", "cTst")), emit

        def gcn(layer):
            def emit(ctx, block, s):
                def sb(name, shape, dt=F32):
                    return ctx.enter_context(nc.sbuf_tensor(f"{stage[0]}_{name}", shape, dt))

                def pair(name):
                    return [sb(f"{name}{b}", [P, GROUP]) for b in SLOTS]
                w = weight_tiles(ctx, ["conv"])
                ta, gf, sc, gr, gT, yo = (pair(n) for n in ("ta", "gf", "sc", "gr", "gT", "yo"))
                A, B = ([ctx.enter_context(nc.psum_tensor(f"{stage[0]}_{n}{b}", [P, GROUP], F32)) for b in SLOTS] for n in "AB")

                @block.sync
                def _(sp):
                    sp.dma_start(w["conv"][:], t["L0_gnn_conv_w"][layer + 1]).then_inc(s["w"], 16)

                    def loads(i):
                        for b in SLOTS:
                            again(sp, s["sc"], i, b)
                            sp.dma_start(ta[b][:], at(grouped(table[0]), 2 * i + b)).then_inc(s[f"lt{b}"], 16)
                            again(sp, s["gT"], i, b)
                            sp.dma_start(gf[b][:], at(g_first, 2 * i + b)).then_inc(s[f"lg{b}"], 16)

                    def stores(i):
                        for b in SLOTS:
                            sp.wait_ge(s["yo"], nth(i, b))
                            sp.dma_start(at(grouped(table[0]), 2 * i + b), yo[b][:]).then_inc(s[f"yost{b}"], 16)
                    load_and_store(sp, loads, stores)
                    for b in SLOTS:
                        sp.wait_ge(s[f"yost{b}"], 16 * PAIRS)

                @block.vector
                def _(dve):
                    def body(i):
                        for b in SLOTS:
                            dve.wait_ge(s[f"lt{b}"], 16 * (i + 1))
                            again(dve, s["tr"], i, b)
                            for j in range(J):
                                js = slice(j * D, (j + 1) * D)
                                last = nc.vector.tensor_scalar(sc[b][:, js], ta[b][:, js],
                                                               dinv2[:, bass.ds((2 * i + b) * J + j, 1)], None, ALU.mult)
                            last.then_inc(s["sc"], 1)
                    sweep(dve, PAIRS, body)

                @block.gpsimd
                def _(pool):
                    def body(i):
                        for b in SLOTS:
                            pool.wait_ge(s["gr"], nth(i, b))
                            pool.wait_ge(s[f"lg{b}"], 16 * (i + 1))
                            again(pool, s["y"], i, b)
                            nc.gpsimd.tensor_tensor(gT[b][:], gr[b][:], gf[b][:], ALU.add).then_inc(s["gT"], 1)
                    sweep(pool, PAIRS, body)

                @block.scalar
                def _(act):
                    def body(i):
                        for b in SLOTS:
                            act.wait_ge(s["tr"], nth(i, b))
                            again(act, s["gT"], i, b)
                            nc.scalar.activation(gr[b][:], A[b][:], ACT.Relu, bias=bnbi[:, layer + 1:layer + 2],
                                                 scale=bnsc[:, layer + 1:layer + 2]).then_inc(s["gr"], 1)
                        for b in SLOTS:
                            act.wait_ge(s["y"], nth(i, b))
                            if not first_step(i):
                                act.wait_ge(s[f"yost{b}"], 16 * i)
                            nc.scalar.copy(yo[b][:], B[b][:]).then_inc(s["yo"], 1)
                    sweep(act, PAIRS, body)

                @block.tensor
                def _(pe):
                    pe.wait_ge(s["w"], 16)

                    def body(i):
                        for b in SLOTS:
                            pe.wait_ge(s["sc"], nth(i, b))
                            again(pe, s["gr"], i, b)
                            turn4(A[b], sc[b]).then_inc(s["tr"], 1)
                        for b in SLOTS:
                            pe.wait_ge(s["gT"], nth(i, b))
                            again(pe, s["yo"], i, b)
                            rows4(B[b], gT[b], w["conv"]).then_inc(s["y"], 1)
                    sweep(pe, PAIRS, body)
            return ["w", "sc", "tr", "gr", "gT", "y", "yo"] + st("lt", "lg", "yost"), emit

        def join(ctx, block, s):
            def sb(name, shape, dt=F32):
                return ctx.enter_context(nc.sbuf_tensor(f"{stage[0]}_{name}", shape, dt))

            def pair(name):
                return [sb(f"{name}{b}", [P, GROUP]) for b in SLOTS]
            w = weight_tiles(ctx, ["out", "w1"])
            ta, gf, x1, xr, sc, gr, gx, mT, xo, nn, hT, yo = (pair(n) for n in (
                "ta", "gf", "x1", "xr", "sc", "gr", "gx", "mT", "xo", "nn", "hT", "yo"))
            T1 = norm_tiles(sb, "n1")
            A, B = ([ctx.enter_context(nc.psum_tensor(f"{stage[0]}_{n}{b}", [P, GROUP], F32)) for b in SLOTS] for n in "AB")

            @block.sync
            def _(sp):
                sp.dma_start(w["out"][:], t["L0_gnn_fc_w"]).then_inc(s["w"], 16)
                sp.dma_start(w["w1"][:], t["L1_gnn_W1"][0:D, :]).then_inc(s["w"], 16)

                def loads(i):
                    for b in SLOTS:
                        again(sp, s["sc"], i, b)
                        sp.dma_start(ta[b][:], at(grouped(table[0]), 2 * i + b)).then_inc(s[f"lt{b}"], 16)
                        again(sp, s["gx"], i, b)
                        sp.dma_start(gf[b][:], at(g_first, 2 * i + b)).then_inc(s[f"lg{b}"], 16)
                        sp.dma_start(x1[b][:], at(cur[0], 2 * i + b)).then_inc(s[f"lg{b}"], 16)
                        again(sp, s["xo"], i, b)
                        if is_tail(i, b):
                            sp.dma_start(xr[b][0:TAILP, :], x_tail).then_inc(s[f"lx{b}"], 16)
                        else:
                            sp.dma_start(xr[b][:], at(x_groups, 2 * i + b)).then_inc(s[f"lx{b}"], 16)

                def stores(i):
                    for b in SLOTS:
                        sp.wait_ge(s["xo"], nth(i, b))
                        sp.dma_start(at(grouped(xres[0]), 2 * i + b), xo[b][:]).then_inc(s[f"xost{b}"], 16)
                    for b in SLOTS:
                        sp.wait_ge(s["yo"], nth(i, b))
                        sp.dma_start(at(grouped(table[0]), 2 * i + b), yo[b][:]).then_inc(s[f"yost{b}"], 16)
                load_and_store(sp, loads, stores)
                for b in SLOTS:
                    sp.wait_ge(s[f"xost{b}"], 16 * PAIRS)
                    sp.wait_ge(s[f"yost{b}"], 16 * PAIRS)

            @block.gpsimd
            def _(pool):
                def body(i):
                    for b in SLOTS:
                        pool.wait_ge(s[f"lg{b}"], 32 * (i + 1))
                        again(pool, s["mT"], i, b)
                        nc.gpsimd.tensor_tensor(gx[b][:], gf[b][:], x1[b][:], ALU.add).then_inc(s["gx"], 1)
                sweep(pool, PAIRS, body)

            @block.tensor
            def _(pe):
                pe.wait_ge(s["w"], 32)
                pe.wait_ge(s["wh"], 1)

                def body(i):
                    for b in SLOTS:
                        pe.wait_ge(s["sc"], nth(i, b))
                        again(pe, s["hT"], i, b)
                        turn4(A[b], sc[b]).then_inc(s["tr"], 1)
                    for b in SLOTS:
                        pe.wait_ge(s["mT"], nth(i, b))
                        again(pe, s["yo"], i, b)
                        rows4(B[b], mT[b], w["out"], "fc").then_inc(s["o"], 1)
                    for b in SLOTS:
                        pe.wait_ge(s["nn"], nth(i, b))
                        turn4(A[b], nn[b]).then_inc(s["tn"], 1)
                    for b in SLOTS:
                        pe.wait_ge(s["hT"], nth(i, b))
                        rows4(B[b], hT[b], w["w1"], "l1c").then_inc(s["y"], 1)
                sweep(pe, PAIRS, body)

            @block.scalar
            def _(act):
                def body(i):
                    for b in SLOTS:
                        act.wait_ge(s["tr"], nth(i, b))
                        again(act, s["mT"], i, b)
                        nc.scalar.activation(gr[b][:], A[b][:], ACT.Relu, bias=bnbi[:, 3:4],
                                             scale=bnsc[:, 3:4]).then_inc(s["gr"], 1)
                    root_on_act(act, i, T1, s["var1"], s["std1"], eps_ln)
                    for b in SLOTS:
                        act.wait_ge(s["tn"], nth(i, b))
                        again(act, s["y"], i, b)
                        nc.scalar.activation(hT[b][:], A[b][:], ACT.Relu).then_inc(s["hT"], 1)
                    for b in SLOTS:
                        act.wait_ge(s["y"], nth(i, b))
                        if not first_step(i):
                            act.wait_ge(s[f"yost{b}"], 16 * i)
                        nc.scalar.copy(yo[b][:], B[b][:]).then_inc(s["yo"], 1)
                sweep(act, PAIRS, body)

            @block.vector
            def _(dve):
                m = Marks(dve, s["dv"])
                dve.wait_ge(s["w"], 32)
                nc.vector.tensor_scalar(w["out"][:], w["out"][:], 0.5, None, ALU.mult).then_inc(s["wh"], 1)

                def body(i):
                    m.step(i)
                    for b in SLOTS:
                        dve.wait_ge(s[f"lt{b}"], 16 * (i + 1))
                        again(dve, s["tr"], i, b)
                        for j in range(J):
                            js = slice(j * D, (j + 1) * D)
                            last = nc.vector.tensor_scalar(sc[b][:, js], ta[b][:, js],
                                                           dinv2[:, bass.ds((2 * i + b) * J + j, 1)], None, ALU.mult)
                        last.then_inc(s["sc"], 1)
                    for b in SLOTS:
                        dve.wait_ge(s["gr"], nth(i, b))
                        dve.wait_ge(s["gx"], nth(i, b))
                        again(dve, s["o"], i, b)
                        nc.vector.tensor_tensor(mT[b][:], gr[b][:], gx[b][:], ALU.add).then_inc(s["mT"], 1)
                    for b in SLOTS:
                        dve.wait_ge(s["o"], nth(i, b))
                        dve.wait_ge(s[f"lx{b}"], 16 * (i + 1))
                        if not first_step(i):
                            dve.wait_ge(s[f"xost{b}"], 16 * i)
                        nc.vector.tensor_tensor(xo[b][:], B[b][:], xr[b][:], ALU.add).then_inc(s["xo"], 1)

                    def ready(b):
                        dve.wait_ge(s["xo"], nth(i, b))
                        again(dve, s["tn"], i, b)
                    norm_on_dve(dve, m, i, T1, xo, nn, ready, s["var1"], s["std1"], s["nn"])
                sweep(dve, PAIRS, body)
        JOIN_SEMS = (["w", "wh", "sc", "gx", "xo", "yo", "mT", "hT", "tr", "o", "nn", "tn", "y", "gr", "var1", "std1", "dv"]
                     + st("lt", "lg", "lx", "xost", "yost"))

        def second(ctx, block, s):
            def sb(name, shape, dt=F32):
                return ctx.enter_context(nc.sbuf_tensor(f"{stage[0]}_{name}", shape, dt))

            def pair(name):
                return [sb(f"{name}{b}", [P, GROUP]) for b in SLOTS]
            w = weight_tiles(ctx, ["w2", "w3", "gin"])
            ta, xr, r1, n1, h1, r2, n2, h2, xo, n3, h3, yo, ye = (pair(n) for n in (
                "ta", "xr", "r1", "n1", "h1", "r2", "n2", "h2", "xo", "n3", "h3", "yo", "ye"))
            T1, T2, T3 = norm_tiles(sb, "t1"), norm_tiles(sb, "t2"), norm_tiles(sb, "t3")
            A, B, C, E_ = ([ctx.enter_context(nc.psum_tensor(f"{stage[0]}_{n}{b}", [P, GROUP], F32)) for b in SLOTS] for n in "ABCE")

            @block.sync
            def _(sp):
                for n, v in (("w2", t["L1_gnn_W2"]), ("w3", t["L1_gnn_W3"]), ("gin", t["L2_gnn_W1"][0])):
                    sp.dma_start(w[n][:], v).then_inc(s["w"], 16)

                def loads(i):
                    for b in SLOTS:
                        again(sp, s["r1"], i, b)
                        sp.dma_start(ta[b][:], at(grouped(table[0]), 2 * i + b)).then_inc(s[f"lt{b}"], 16)
                        again(sp, s["xo"], i, b)
                        sp.dma_start(xr[b][:], at(grouped(xres[0]), 2 * i + b)).then_inc(s[f"lx{b}"], 16)

                def stores(i):
                    for b in SLOTS:
                        sp.wait_ge(s["xo"], nth(i, b))
                        sp.dma_start(at(grouped(xres[1]), 2 * i + b), xo[b][:]).then_inc(s[f"xost{b}"], 16)
                    for b in SLOTS:
                        sp.wait_ge(s["yo"], nth(i, b))
                        sp.dma_start(at(grouped(table[0]), 2 * i + b), yo[b][:]).then_inc(s[f"yost{b}"], 16)
                        sp.wait_ge(s["ye"], nth(i, b))
                        sp.dma_start(at(grouped(table[1]), 2 * i + b), ye[b][:]).then_inc(s[f"yest{b}"], 16)
                load_and_store(sp, loads, stores)
                for b in SLOTS:
                    for n in ("xost", "yost", "yest"):
                        sp.wait_ge(s[f"{n}{b}"], 16 * PAIRS)

            @block.gpsimd
            def _(pool):
                def body(i):
                    for b in SLOTS:
                        pool.wait_ge(s[f"lt{b}"], 16 * (i + 1))
                        again(pool, s["n1"], i, b)
                        pool.sem_inc(s["pace"], 1)
                        nc.gpsimd.tensor_scalar(r1[b][:], ta[b][:], 0.0, None, ALU.max).then_inc(s["r1"], 1)
                sweep(pool, PAIRS, body)

            @block.tensor
            def _(pe):
                pe.wait_ge(s["w"], 48)

                def body(i):
                    for b in SLOTS:
                        pe.wait_ge(s["n1"], nth(i, b))
                        again(pe, s["h3"], i, b)
                        turn4(A[b], n1[b]).then_inc(s["tn1"], 1)
                    for b in SLOTS:
                        pe.wait_ge(s["h1"], nth(i, b))
                        again(pe, s["yo"], i, b)
                        again(pe, s["ye"], i, b)
                        rows4(B[b], h1[b], w["w2"], "l1b2").then_inc(s["z2"], 1)
                    for b in SLOTS:
                        pe.wait_ge(s["n2"], nth(i, b))
                        turn4(C[b], n2[b]).then_inc(s["tn2"], 1)
                    for b in SLOTS:
                        pe.wait_ge(s["h2"], nth(i, b))
                        rows4(E_[b], h2[b], w["w3"], "l1b3").then_inc(s["z3"], 1)
                    for b in SLOTS:
                        pe.wait_ge(s["n3"], nth(i, b))
                        turn4(A[b], n3[b]).then_inc(s["tn3"], 1)
                    for b in SLOTS:
                        pe.wait_ge(s["h3"], nth(i, b))
                        rows4(B[b], h3[b], w["gin"]).then_inc(s["y"], 1)
                sweep(pe, PAIRS, body)

            @block.scalar
            def _(act):
                def body(i):
                    root_on_act(act, i, T1, s["var1"], s["std1"], eps_ln)
                    for b in SLOTS:
                        act.wait_ge(s["tn1"], nth(i, b))
                        nc.scalar.activation(h1[b][:], A[b][:], ACT.Identity, bias=col("be1L1"),
                                             scale=col("g1L1")).then_inc(s["h1"], 1)
                    for b in SLOTS:
                        act.wait_ge(s["z2"], nth(i, b))
                        again(act, s["n2"], i, b)
                        nc.scalar.activation(r2[b][:], B[b][:], ACT.Relu).then_inc(s["r2"], 1)
                    root_on_act(act, i, T2, s["var2"], s["std2"], eps_ln)
                    for b in SLOTS:
                        act.wait_ge(s["tn2"], nth(i, b))
                        nc.scalar.activation(h2[b][:], C[b][:], ACT.Identity, bias=col("be2L1"),
                                             scale=col("g2L1")).then_inc(s["h2"], 1)
                    root_on_act(act, i, T3, s["var3"], s["std3"], eps_ln)
                    for b in SLOTS:
                        act.wait_ge(s["tn3"], nth(i, b))
                        again(act, s["y"], i, b)
                        nc.scalar.activation(h3[b][:], A[b][:], ACT.Relu).then_inc(s["h3"], 1)
                    for b in SLOTS:
                        act.wait_ge(s["y"], nth(i, b))
                        if not first_step(i):
                            act.wait_ge(s[f"yost{b}"], 16 * i)
                            act.wait_ge(s[f"yest{b}"], 16 * i)
                        nc.scalar.copy(yo[b][:], B[b][:]).then_inc(s["yo"], 1)
                        nc.scalar.activation(ye[b][:], B[b][:], ACT.Copy, scale=eps1[:, 0:1]).then_inc(s["ye"], 1)
                sweep(act, PAIRS, body)

            @block.vector
            def _(dve):
                m = Marks(dve, s["dv"])

                def body(i):
                    m.step(i)

                    def ready1(b):
                        dve.wait_ge(s["r1"], nth(i, b))
                        again(dve, s["tn1"], i, b)
                    norm_on_dve(dve, m, i, T1, r1, n1, ready1, s["var1"], s["std1"], s["n1"])

                    def ready2(b):
                        dve.wait_ge(s["r2"], nth(i, b))
                        again(dve, s["tn2"], i, b)
                    norm_on_dve(dve, m, i, T2, r2, n2, ready2, s["var2"], s["std2"], s["n2"])
                    for b in SLOTS:
                        dve.wait_ge(s["z3"], nth(i, b))
                        dve.wait_ge(s[f"lx{b}"], 16 * (i + 1))
                        if not first_step(i):
                            dve.wait_ge(s[f"xost{b}"], 16 * i)
                        nc.vector.tensor_tensor(xo[b][:], E_[b][:], xr[b][:], ALU.add).then_inc(s["xo"], 1)

                    def ready3(b):
                        dve.wait_ge(s["xo"], nth(i, b))
                        again(dve, s["tn3"], i, b)
                    norm_on_dve(dve, m, i, T3, xo, n3, ready3, s["var3"], s["std3"], s["n3"])
                sweep(dve, PAIRS, body)
        SECOND_SEMS = (["w", "pace", "r1", "n1", "n2", "n3", "xo", "yo", "ye", "tn1", "tn2", "tn3", "h1", "h2", "h3", "z2", "z3",
                        "r2", "y", "var1", "var2", "var3", "std1", "std2", "std3", "dv"]
                       + st("lt", "lx", "xost", "yost", "yest"))

        bnmv = keep("bnmv", [P, 2])
        bnsd = keep("bnsd", [P, 1])
        gsc = keep("gsc", [P, 1])
        gbi = keep("gbi", [P, 1])
        gtmp = keep("gtmp", [P, 1])

        def batch_stats(dve, i, b, src):
            rows = TAILP if is_tail(i, b) else P
            if rows == P:
                return nc.vector.bn_stats(bnstat[:, bass.ds(2 * i + b, 1), :].rearrange("p a f -> p (a f)"), src[:])
            for j in range(J):
                last = nc.vector.bn_stats(bnstat[:, G - 1 + j, :], src[:, j * D:j * D + rows])
            return last

        def gin_turn(layer):
            def emit(ctx, block, s):
                def sb(name, shape, dt=F32):
                    return ctx.enter_context(nc.sbuf_tensor(f"{stage[0]}_{name}", shape, dt))
                ta = [sb(f"ta{b}", [P, GROUP]) for b in SLOTS]
                zT = [sb(f"zT{b}", [P, GROUP]) for b in SLOTS]
                A = [ctx.enter_context(nc.psum_tensor(f"{stage[0]}_A{b}", [P, GROUP], F32)) for b in SLOTS]

                @block.sync
                def _(sp):
                    def loads(i):
                        for b in SLOTS:
                            again(sp, s["tr"], i, b)
                            sp.dma_start(ta[b][:], at(grouped(table[1]), 2 * i + b)).then_inc(s[f"lt{b}"], 16)

                    def stores(i):
                        for b in SLOTS:
                            sp.wait_ge(s["zT"], nth(i, b))
                            sp.dma_start(at(cur[0], 2 * i + b), zT[b][:]).then_inc(s[f"zst{b}"], 16)
                    load_and_store(sp, loads, stores)
                    for b in SLOTS:
                        sp.wait_ge(s[f"zst{b}"], 16 * PAIRS)

                @block.tensor
                def _(pe):
                    def body(i):
                        for b in SLOTS:
                            pe.wait_ge(s[f"lt{b}"], 16 * (i + 1))
                            again(pe, s["zT"], i, b)
                            turn4(A[b], ta[b]).then_inc(s["tr"], 1)
                    sweep(pe, PAIRS, body)

                @block.scalar
                def _(act):
                    def body(i):
                        for b in SLOTS:
                            act.wait_ge(s["tr"], nth(i, b))
                            again(act, s["bs"], i, b)
                            if not first_step(i):
                                act.wait_ge(s[f"zst{b}"], 16 * i)
                            nc.scalar.activation(zT[b][:], A[b][:], ACT.Identity, bias=col(f"b1_{layer}")).then_inc(s["zT"], 1)
                    sweep(act, PAIRS, body)
                    batch_root(act, s)

                @block.vector
                def _(dve):
                    def body(i):
                        for b in SLOTS:
                            dve.wait_ge(s["zT"], nth(i, b))
                            batch_stats(dve, i, b, zT[b]).then_inc(s["bs"], 1)
                    sweep(dve, PAIRS, body)
                    batch_scale(dve, s, col(f"g1_{layer}"), col(f"bt1_{layer}"))
            return ["tr", "zT", "bs", "dv", "bvar", "bstd"] + st("lt", "zst"), emit

        def batch_root(act, s):
            act.wait_ge(s["bvar"], 1)
            nc.scalar.activation(bnsd[:], bnmv[:, 1:2], ACT.Sqrt, bias=eps_ln).then_inc(s["bstd"], 1)

        def batch_scale(dve, s, g, b):
            dve.wait_ge(s["bs"], G)
            nc.vector.bn_aggr(bnmv[:], bnstat[:, 0:G - 1 + J, :].rearrange("p a f -> p (a f)")).then_inc(s["bvar"], 1)
            dve.wait_ge(s["bstd"], 1)
            nc.vector.reciprocal(gtmp[:], bnsd[:]).then_inc(s["dv"], 1)
            dve.wait_ge(s["dv"], 1)
            nc.vector.tensor_tensor(gsc[:], gtmp[:], g, ALU.mult).then_inc(s["dv"], 1)
            dve.wait_ge(s["dv"], 2)
            nc.vector.tensor_tensor(gtmp[:], bnmv[:, 0:1], gsc[:], ALU.mult).then_inc(s["dv"], 1)
            dve.wait_ge(s["dv"], 3)
            nc.vector.tensor_tensor(gbi[:], b, gtmp[:], ALU.subtract)

        def gin_middle(layer):
            def emit(ctx, block, s):
                def sb(name, shape, dt=F32):
                    return ctx.enter_context(nc.sbuf_tensor(f"{stage[0]}_{name}", shape, dt))

                def pair(name):
                    return [sb(f"{name}{b}", [P, GROUP]) for b in SLOTS]
                w = weight_tiles(ctx, ["w2"])
                zT, tT, uT = pair("zT"), pair("tT"), pair("uT")
                A = [ctx.enter_context(nc.psum_tensor(f"{stage[0]}_A{b}", [P, GROUP], F32)) for b in SLOTS]

                @block.sync
                def _(sp):
                    sp.dma_start(w["w2"][:], t["L2_gnn_W2"][layer]).then_inc(s["w"], 16)

                    def loads(i):
                        for b in SLOTS:
                            again(sp, s["tT"], i, b)
                            sp.dma_start(zT[b][:], at(cur[0], 2 * i + b)).then_inc(s[f"lt{b}"], 16)

                    def stores(i):
                        for b in SLOTS:
                            sp.wait_ge(s["uT"], nth(i, b))
                            sp.dma_start(at(cur[1], 2 * i + b), uT[b][:]).then_inc(s[f"ust{b}"], 16)
                    load_and_store(sp, loads, stores)
                    for b in SLOTS:
                        sp.wait_ge(s[f"ust{b}"], 16 * PAIRS)

                @block.tensor
                def _(pe):
                    pe.wait_ge(s["w"], 16)

                    def body(i):
                        for b in SLOTS:
                            pe.wait_ge(s["tT"], nth(i, b))
                            again(pe, s["uT"], i, b)
                            nc.tensor.matmul(A[b][:], w["w2"][:], tT[b][:], start=True, stop=True).then_inc(s["mm"], 1)
                    sweep(pe, PAIRS, body)

                @block.scalar
                def _(act):
                    def body(i):
                        for b in SLOTS:
                            act.wait_ge(s[f"lt{b}"], 16 * (i + 1))
                            again(act, s["mm"], i, b)
                            nc.scalar.activation(tT[b][:], zT[b][:], ACT.Relu, bias=gsc_bias[0], scale=gsc_bias[1]
                                                 ).then_inc(s["tT"], 1)
                        for b in SLOTS:
                            act.wait_ge(s["mm"], nth(i, b))
                            again(act, s["bs"], i, b)
                            if not first_step(i):
                                act.wait_ge(s[f"ust{b}"], 16 * i)
                            nc.scalar.activation(uT[b][:], A[b][:], ACT.Relu, bias=col(f"b2_{layer}")).then_inc(s["uT"], 1)
                    sweep(act, PAIRS, body)
                    batch_root(act, s)

                @block.vector
                def _(dve):
                    def body(i):
                        for b in SLOTS:
                            dve.wait_ge(s["uT"], nth(i, b))
                            batch_stats(dve, i, b, uT[b]).then_inc(s["bs"], 1)
                    sweep(dve, PAIRS, body)
                    dve.wait_ge(s["tT"], G)
                    batch_scale(dve, s, col(f"g2_{layer}"), col(f"bt2_{layer}"))
            return ["w", "tT", "uT", "mm", "bs", "dv", "bvar", "bstd"] + st("lt", "ust"), emit
        gsc_bias = (gbi[:, 0:1], gsc[:, 0:1])

        def gin_next(layer):
            def emit(ctx, block, s):
                def sb(name, shape, dt=F32):
                    return ctx.enter_context(nc.sbuf_tensor(f"{stage[0]}_{name}", shape, dt))

                def pair(name):
                    return [sb(f"{name}{b}", [P, GROUP]) for b in SLOTS]
                w = weight_tiles(ctx, ["w1"])
                uT, hT, yo, ye = pair("uT"), pair("hT"), pair("yo"), pair("ye")
                A = [ctx.enter_context(nc.psum_tensor(f"{stage[0]}_A{b}", [P, GROUP], F32)) for b in SLOTS]

                @block.sync
                def _(sp):
                    sp.dma_start(w["w1"][:], t["L2_gnn_W1"][layer + 1]).then_inc(s["w"], 16)

                    def loads(i):
                        for b in SLOTS:
                            again(sp, s["hT"], i, b)
                            sp.dma_start(uT[b][:], at(cur[1], 2 * i + b)).then_inc(s[f"lt{b}"], 16)

                    def stores(i):
                        for b in SLOTS:
                            sp.wait_ge(s["yo"], nth(i, b))
                            sp.dma_start(at(grouped(table[0]), 2 * i + b), yo[b][:]).then_inc(s[f"yost{b}"], 16)
                            sp.wait_ge(s["ye"], nth(i, b))
                            sp.dma_start(at(grouped(table[1]), 2 * i + b), ye[b][:]).then_inc(s[f"yest{b}"], 16)
                    load_and_store(sp, loads, stores)
                    for b in SLOTS:
                        sp.wait_ge(s[f"yost{b}"], 16 * PAIRS)
                        sp.wait_ge(s[f"yest{b}"], 16 * PAIRS)

                @block.tensor
                def _(pe):
                    pe.wait_ge(s["w"], 16)

                    def body(i):
                        for b in SLOTS:
                            pe.wait_ge(s["hT"], nth(i, b))
                            again(pe, s["yo"], i, b)
                            rows4(A[b], hT[b], w["w1"]).then_inc(s["mm"], 1)
                    sweep(pe, PAIRS, body)

                @block.scalar
                def _(act):
                    def body(i):
                        for b in SLOTS:
                            act.wait_ge(s[f"lt{b}"], 16 * (i + 1))
                            again(act, s["mm"], i, b)
                            nc.scalar.activation(hT[b][:], uT[b][:], ACT.Relu, bias=gsc_bias[0], scale=gsc_bias[1]
                                                 ).then_inc(s["hT"], 1)
                        for b in SLOTS:
                            act.wait_ge(s["mm"], nth(i, b))
                            again(act, s["ye"], i, b)
                            if not first_step(i):
                                act.wait_ge(s[f"yost{b}"], 16 * i)
                            nc.scalar.copy(yo[b][:], A[b][:]).then_inc(s["yo"], 1)
                    sweep(act, PAIRS, body)

                @block.vector
                def _(dve):
                    def body(i):
                        for b in SLOTS:
                            dve.wait_ge(s["yo"], nth(i, b))
                            if not first_step(i):
                                dve.wait_ge(s[f"yest{b}"], 16 * i)
                            nc.vector.tensor_scalar(ye[b][:], yo[b][:], eps1[:, layer + 1:layer + 2], None, ALU.mult
                                                    ).then_inc(s["ye"], 1)
                    sweep(dve, PAIRS, body)
            return ["w", "hT", "mm", "yo", "ye"] + st("lt", "yost", "yest"), emit

        def gin_last(ctx, block, s):
            def sb(name, shape, dt=F32):
                return ctx.enter_context(nc.sbuf_tensor(f"{stage[0]}_{name}", shape, dt))

            def pair(name):
                return [sb(f"{name}{b}", [P, GROUP]) for b in SLOTS]
            w = weight_tiles(ctx, ["w1"])
            uT, hT, xr, xo, nn, fT, yo = (pair(n) for n in ("uT", "hT", "xr", "xo", "nn", "fT", "yo"))
            T1 = norm_tiles(sb, "n1")
            A, B = ([ctx.enter_context(nc.psum_tensor(f"{stage[0]}_{n}{b}", [P, GROUP], F32)) for b in SLOTS] for n in "AB")

            @block.sync
            def _(sp):
                sp.dma_start(w["w1"][:], t["L3_gnn_W1"]).then_inc(s["w"], 16)

                def loads(i):
                    for b in SLOTS:
                        again(sp, s["hT"], i, b)
                        sp.dma_start(uT[b][:], at(cur[1], 2 * i + b)).then_inc(s[f"lt{b}"], 16)
                        again(sp, s["xo"], i, b)
                        sp.dma_start(xr[b][:], at(grouped(xres[1]), 2 * i + b)).then_inc(s[f"lx{b}"], 16)

                def stores(i):
                    for b in SLOTS:
                        sp.wait_ge(s["xo"], nth(i, b))
                        sp.dma_start(at(grouped(xres[0]), 2 * i + b), xo[b][:]).then_inc(s[f"xost{b}"], 16)
                    for b in SLOTS:
                        sp.wait_ge(s["yo"], nth(i, b))
                        sp.dma_start(at(grouped(table[0]), 2 * i + b), yo[b][:]).then_inc(s[f"yost{b}"], 16)
                load_and_store(sp, loads, stores)
                for b in SLOTS:
                    sp.wait_ge(s[f"xost{b}"], 16 * PAIRS)
                    sp.wait_ge(s[f"yost{b}"], 16 * PAIRS)

            @block.tensor
            def _(pe):
                pe.wait_ge(s["w"], 16)

                def body(i):
                    for b in SLOTS:
                        pe.wait_ge(s["hT"], nth(i, b))
                        again(pe, s["fT"], i, b)
                        turn4(A[b], hT[b]).then_inc(s["th"], 1)
                    for b in SLOTS:
                        pe.wait_ge(s["nn"], nth(i, b))
                        turn4(A[b], nn[b]).then_inc(s["tn"], 1)
                    for b in SLOTS:
                        pe.wait_ge(s["fT"], nth(i, b))
                        again(pe, s["yo"], i, b)
                        rows4(B[b], fT[b], w["w1"]).then_inc(s["y"], 1)
                sweep(pe, PAIRS, body)

            @block.scalar
            def _(act):
                def body(i):
                    for b in SLOTS:
                        act.wait_ge(s[f"lt{b}"], 16 * (i + 1))
                        again(act, s["th"], i, b)
                        nc.scalar.activation(hT[b][:], uT[b][:], ACT.Relu, bias=gsc_bias[0], scale=gsc_bias[1]
                                             ).then_inc(s["hT"], 1)
                    root_on_act(act, i, T1, s["var1"], s["std1"], eps_ln)
                    for b in SLOTS:
                        act.wait_ge(s["tn"], nth(i, b))
                        again(act, s["y"], i, b)
                        nc.scalar.activation(fT[b][:], A[b][:], ACT.Relu).then_inc(s["fT"], 1)
                    for b in SLOTS:
                        act.wait_ge(s["y"], nth(i, b))
                        if not first_step(i):
                            act.wait_ge(s[f"yost{b}"], 16 * i)
                        nc.scalar.copy(yo[b][:], B[b][:]).then_inc(s["yo"], 1)
                sweep(act, PAIRS, body)

            @block.vector
            def _(dve):
                m = Marks(dve, s["dv"])

                def body(i):
                    m.step(i)
                    for b in SLOTS:
                        dve.wait_ge(s["th"], nth(i, b))
                        dve.wait_ge(s[f"lx{b}"], 16 * (i + 1))
                        if not first_step(i):
                            dve.wait_ge(s[f"xost{b}"], 16 * i)
                        nc.vector.tensor_tensor(xo[b][:], A[b][:], xr[b][:], ALU.add).then_inc(s["xo"], 1)

                    def ready(b):
                        dve.wait_ge(s["xo"], nth(i, b))
                        again(dve, s["tn"], i, b)
                    norm_on_dve(dve, m, i, T1, xo, nn, ready, s["var1"], s["std1"], s["nn"])
                sweep(dve, PAIRS, body)
        GIN_LAST_SEMS = (["w", "hT", "xo", "yo", "th", "tn", "fT", "nn", "y", "var1", "std1", "dv"]
                         + st("lt", "lx", "xost", "yost"))

        def fourth(ctx, block, s):
            def sb(name, shape, dt=F32):
                return ctx.enter_context(nc.sbuf_tensor(f"{stage[0]}_{name}", shape, dt))

            def pair(name):
                return [sb(f"{name}{b}", [P, GROUP]) for b in SLOTS]
            w = weight_tiles(ctx, ["w2"])
            ta, xr, hT, xo = (pair(n) for n in ("ta", "xr", "hT", "xo"))
            A, B = ([ctx.enter_context(nc.psum_tensor(f"{stage[0]}_{n}{b}", [P, GROUP], F32)) for b in SLOTS] for n in "AB")

            @block.sync
            def _(sp):
                sp.dma_start(w["w2"][:], t["L3_gnn_W2"]).then_inc(s["w"], 16)

                def loads(i):
                    for b in SLOTS:
                        again(sp, s["tr"], i, b)
                        sp.dma_start(ta[b][:], at(grouped(table[0]), 2 * i + b)).then_inc(s[f"lt{b}"], 16)
                        again(sp, s["xo"], i, b)
                        sp.dma_start(xr[b][:], at(grouped(xres[0]), 2 * i + b)).then_inc(s[f"lx{b}"], 16)

                def stores(i):
                    for b in SLOTS:
                        sp.wait_ge(s["xo"], nth(i, b))
                        if is_tail(i, b):
                            sp.dma_start(out_tail, xo[b][0:TAILP, :]).then_inc(s[f"xost{b}"], 16)
                        else:
                            sp.dma_start(at(out_groups, 2 * i + b), xo[b][:]).then_inc(s[f"xost{b}"], 16)
                load_and_store(sp, loads, stores)
                for b in SLOTS:
                    sp.wait_ge(s[f"xost{b}"], 16 * PAIRS)

            @block.tensor
            def _(pe):
                pe.wait_ge(s["w"], 16)

                def body(i):
                    for b in SLOTS:
                        pe.wait_ge(s[f"lt{b}"], 16 * (i + 1))
                        again(pe, s["hT"], i, b)
                        turn4(A[b], ta[b]).then_inc(s["tr"], 1)
                    for b in SLOTS:
                        pe.wait_ge(s["hT"], nth(i, b))
                        again(pe, s["xo"], i, b)
                        rows4(B[b], hT[b], w["w2"], "l3b2").then_inc(s["y"], 1)
                sweep(pe, PAIRS, body)

            @block.scalar
            def _(act):
                def body(i):
                    for b in SLOTS:
                        act.wait_ge(s["tr"], nth(i, b))
                        again(act, s["y"], i, b)
                        nc.scalar.activation(hT[b][:], A[b][:], ACT.Relu, bias=col("b1L3")).then_inc(s["hT"], 1)
                sweep(act, PAIRS, body)

            @block.vector
            def _(dve):
                def body(i):
                    for b in SLOTS:
                        dve.wait_ge(s["y"], nth(i, b))
                        dve.wait_ge(s[f"lx{b}"], 16 * (i + 1))
                        if not first_step(i):
                            dve.wait_ge(s[f"xost{b}"], 16 * i)
                        nc.vector.tensor_tensor(xo[b][:], B[b][:], xr[b][:], ALU.add).then_inc(s["xo"], 1)
                sweep(dve, PAIRS, body)
        FOURTH_SEMS = ["w", "tr", "hT", "y", "xo"] + st("lt", "lx", "xost")

        aggregate("gcn0", table[0], gcn_coef, table[0])
        run_block("att0", *attention(0))
        run_block("gcn0d", *gcn(0))
        aggregate("gcn1", table[0], gcn_coef, table[0])
        run_block("att1", *attention(1))
        run_block("gcn1d", *gcn(1))
        aggregate("gcn2", table[0], gcn_coef, table[0])
        run_block("join", JOIN_SEMS, join)
        run_block("attr", ATTR_SEMS, project_edge_attr)
        run_block("attr_a", *add_edges(table[0]), {"sw_added": 16 * TILES})
        run_block("second", SECOND_SEMS, second)
        for layer in range(3):
            aggregate(f"gin{layer}", table[0], edge_w, table[1])
            run_block(f"gin{layer}t", *gin_turn(layer))
            run_block(f"gin{layer}m", *gin_middle(layer))
            if layer < 2:
                run_block(f"gin{layer}n", *gin_next(layer))
        run_block("ginlast", GIN_LAST_SEMS, gin_last)
        aggregate("fourth", table[0], edge_w, table[0])
        run_block("out", FOURTH_SEMS, fourth)


_INS = ["x", "src", "dst", "edge_attr_128", "edge_weight",
        "L0_gnn_t_fc_w", "L0_gnn_t_fc_b", "L0_gnn_t_ln_g", "L0_gnn_t_ln_b", "L0_gnn_qkv_w",
        "L0_gnn_g_fc_w", "L0_gnn_g_fc_b", "L0_gnn_bn_g", "L0_gnn_bn_b", "L0_gnn_conv_w", "L0_gnn_conv_b",
        "L0_gnn_fc_w", "L0_gnn_fc_b",
        "L1_gnn_u", "L1_gnn_W1", "L1_gnn_b1", "L1_gnn_g1", "L1_gnn_be1", "L1_gnn_W2", "L1_gnn_b2",
        "L1_gnn_g2", "L1_gnn_be2", "L1_gnn_W3", "L1_gnn_b3",
        "L2_gnn_eps_list", "L2_gnn_W1", "L2_gnn_b1", "L2_gnn_g1", "L2_gnn_bt1", "L2_gnn_W2", "L2_gnn_b2",
        "L2_gnn_g2", "L2_gnn_bt2",
        "L3_gnn_W1", "L3_gnn_b1", "L3_gnn_W2", "L3_gnn_b2"]


def kernel(**inputs):
    import numpy as _np
    import concourse.bacc as _bacc
    from concourse import mybir as _mybir
    from concourse.bass_utils import run_bass_kernel_spmd as _run

    nc = _bacc.Bacc("TRN2", target_bir_lowering=False, num_devices=1)
    arrays, args = {}, {}
    for name in _INS:
        a = _np.ascontiguousarray(inputs[name])
        arrays[f"in_{name}_dram"] = a
        args[name] = nc.dram_tensor(f"in_{name}_dram", a.shape, _mybir.dt.from_np(a.dtype), kind="ExternalInput").ap()
    shape = inputs["x"].shape
    out = nc.dram_tensor("out_0_dram", shape, _mybir.dt.float32, kind="ExternalOutput").ap()
    build(nc, args, out)
    r = _run(nc, [arrays], core_ids=[0])
    return r.results[0]["out_0_dram"]
```

```python
from contextlib import ExitStack

import concourse.bass as bass
from concourse import mybir

F32 = mybir.dt.float32
BF16 = mybir.dt.bfloat16
I32 = mybir.dt.int32
ALU = mybir.AluOpType
ACT = mybir.ActivationFunctionType
AX = mybir.AxisListType

D = 128
P = 128
J = 4
GROUP = P * J
EP = 125
RING = 4
LN_EPS = 1e-5
GUARD = 1e6


class Marks:

    def __init__(self, eng, sem):
        self.eng, self.sem, self.n, self.per_step, self.i = eng, sem, 0, None, 0

    def step(self, i):
        if self.per_step is None and not (isinstance(i, int) and i == 0):
            self.per_step = self.n
        self.i, self.n = i, 0

    def up(self, instruction):
        instruction.then_inc(self.sem, 1)
        self.n += 1

    def wait(self):
        base = 0 if self.per_step is None else self.i * self.per_step
        self.eng.wait_ge(self.sem, base + self.n)

    def settle(self):
        self.wait()
        self.eng.sem_inc(self.sem, 1)
        self.n += 1


def sweep(eng, steps, body):
    body(0)
    if steps > 2:
        with eng.Fori(1, steps - 1) as i:
            body(i)
    body(steps - 1)


def build(nc, t, out):
    x_in = t["x"]
    N = x_in.shape[0]
    E = t["src"].shape[0]
    G = -(-N // GROUP)
    PAIRS = G // 2
    TAILP = (N - GROUP * (G - 1)) // J
    TILES = E // EP
    NPAD = G * GROUP
    assert G % 2 == 0 and TAILP * J == N - GROUP * (G - 1) and TILES * EP == E and TILES % RING == 0
    EITER = TILES // RING
    FOURS = TILES // 4
    assert TILES % 4 == 0

    def dram(name, shape):
        return nc.dram_tensor(name, shape, F32).ap()

    def grouped(buf):
        return buf[0:NPAD, :].rearrange("(g p j) d -> g p (j d)", p=P, j=J)

    full = (N // GROUP) * GROUP
    x_groups = x_in[0:full, :].rearrange("(g p j) d -> g p (j d)", p=P, j=J)
    x_tail = x_in[full:N, :].rearrange("(p j) d -> p (j d)", j=J)
    out_groups = out[0:full, :].rearrange("(g p j) d -> g p (j d)", p=P, j=J)
    out_tail = out[full:N, :].rearrange("(p j) d -> p (j d)", j=J)

    def at(view, g):
        return view[g, :, :] if isinstance(g, int) else view[bass.ds(g, 1), :, :].rearrange("a p f -> (a p) f")

    table = [dram(f"table{k}", [NPAD + P, D]) for k in range(2)]
    cur = [dram(f"cur{k}", [G, P, GROUP]) for k in range(2)]
    g_first = dram("g_first", [G, P, GROUP])
    xres = [dram(f"xres{k}", [NPAD, D]) for k in range(2)]
    degree = dram("degree", [NPAD + P, 1])
    attr_sum = dram("attr_sum", [NPAD + P, D])

    top = ExitStack()
    with top:
        def keep(name, shape, dt=F32):
            return top.enter_context(nc.sbuf_tensor(name, shape, dt))

        ident = keep("ident", [P, P])
        ones3 = keep("ones3", [3, P], BF16)
        onescol = keep("onescol", [P, 1])
        zrow = keep("zrow", [P, D])
        same = keep("same", [EP, TILES, EP], BF16)
        cross = keep("cross", [EP, TILES // 2, EP], BF16)
        src_i = keep("src_i", [EP, TILES], I32)
        dst_i = keep("dst_i", [EP, TILES], I32)
        put_i = keep("put_i", [EP, TILES], I32)
        gcn_coef = keep("gcn_coef", [EP, TILES])
        edge_w = keep("edge_w", [EP, TILES])
        dinv2 = keep("dinv2", [P, G * J])
        NCOL = 48
        cols = keep("cols", [P, NCOL])
        col_at = {}

        def col(name):
            if name not in col_at:
                col_at[name] = len(col_at)
                assert len(col_at) <= NCOL
            c = col_at[name]
            return cols[:, c:c + 1]
        BIASES = ["t_fc", "fc", "l1c", "l1b2", "l1b3", "l3b2"]
        bias3 = keep("bias3", [3, len(BIASES), GROUP], BF16)
        kvsum = keep("kvsum", [P, D + 1])
        bnstat = keep("bnstat", [P, (G + 1) * J, 6])

        def bias(name):
            return bias3[:, BIASES.index(name), :]

        stage = [""]
        pool_sems = {}
        base = {}

        def before_stage(k):
            return base.get(k, 0)

        def pool_dma_sem(k):
            if k not in pool_sems:
                pool_sems[k] = top.enter_context(nc.semaphore(k))
            return pool_sems[k]

        def run_block(name, sems, emit, sw_counts=None):
            stage[0] = name
            with ExitStack() as ctx:
                s = {k: pool_dma_sem(k) if k.startswith("sw_") else ctx.enter_context(nc.semaphore(f"{name}_{k}"))
                     for k in sems}
                with nc.Block() as block:
                    emit(ctx, block, s)
                nums = [v for k, v in s.items() if not k.startswith("sw_")]
                nc.all_engine_barrier()
                for k in sems:
                    if k.startswith("sw_"):
                        base[k] = base.get(k, 0) + sw_counts[k]
                for v in nums:
                    nc.gpsimd.sem_clear(v)
                nc.all_engine_barrier()

        COLS = {
            "bng0": t["L0_gnn_bn_g"][0], "bnb0": t["L0_gnn_bn_b"][0], "gfcb": t["L0_gnn_g_fc_b"],
            "b1L3": t["L3_gnn_b1"], "g1L1": t["L1_gnn_g1"], "be1L1": t["L1_gnn_be1"],
            "g2L1": t["L1_gnn_g2"], "be2L1": t["L1_gnn_be2"],
        }
        for k in range(3):
            COLS[f"lng{k}"] = t["L0_gnn_t_ln_g"][k]
            COLS[f"lnb{k}"] = t["L0_gnn_t_ln_b"][k]
            COLS[f"bng{k + 1}"] = t["L0_gnn_bn_g"][k + 1]
            COLS[f"bnb{k + 1}"] = t["L0_gnn_bn_b"][k + 1]
            COLS[f"cb{k}"] = t["L0_gnn_conv_b"][k]
            for n in ("b1", "b2", "g1", "bt1", "g2", "bt2"):
                COLS[f"{n}_{k}"] = t[f"L2_gnn_{n}"][k]
        for n in COLS:
            col(n)
        NCOLS_IN = len(COLS)
        eps1 = keep("eps1", [P, 3])
        bnsc = keep("bnsc", [P, 4])
        bnbi = keep("bnbi", [P, 4])

        def prepare(ctx, block, s):
            def sb(name, shape, dt=F32):
                return ctx.enter_context(nc.sbuf_tensor(f"{stage[0]}_{name}", shape, dt))
            brow = sb("brow", [3, len(BIASES), D])
            rest = sb("rest", [3, len(BIASES), D])
            hi = sb("hi", [3, len(BIASES), D], BF16)
            mid = sb("mid", [3, len(BIASES), D], BF16)
            lo = sb("lo", [3, len(BIASES), D], BF16)
            pick = sb("pick", [3, len(BIASES), D])
            pick2 = sb("pick2", [3, len(BIASES), D])
            ucol = sb("ucol", [16, 1])
            u3 = sb("u3", [16, 3])
            w1c = sb("w1c", [16, D])
            ones = sb("ones", [P, (NPAD + P) // P])
            psc = ctx.enter_context(nc.psum_tensor(f"{stage[0]}_psc", [P, D], F32))

            @block.gpsimd
            def _(pool):
                nc.gpsimd.memset(ident[:], 0.0).then_inc(s["pz"], 1)
                pool.wait_ge(s["pz"], 1)
                nc.gpsimd.affine_select(out=ident[:], in_=ident[:], compare_op=ALU.not_equal, fill=1.0,
                                        base=0, pattern=[[-1, P]], channel_multiplier=1).then_inc(s["pi"], 1)

            @block.sync
            def _(sp):
                n = 0
                for name, v in COLS.items():
                    sp.dma_start(col(name), v.rearrange("(p a) -> p a", a=1)).then_inc(s["ld"], 16)
                    n += 1
                rows = {"t_fc": t["L0_gnn_t_fc_b"], "fc": t["L0_gnn_fc_b"], "l1c": t["L1_gnn_b1"],
                        "l1b2": t["L1_gnn_b2"], "l1b3": t["L1_gnn_b3"], "l3b2": t["L3_gnn_b2"]}
                for name, v in rows.items():
                    for k in range(3):
                        sp.dma_start(brow[k:k + 1, BIASES.index(name), :],
                                     v.rearrange("(a d) -> a d", a=1)).then_inc(s["ld"], 16)
                        n += 1
                sp.dma_start(ucol[:], t["L1_gnn_u"].rearrange("a d -> d a")).then_inc(s["ld"], 16)
                sp.dma_start(w1c[:], t["L1_gnn_W1"][2 * D:2 * D + 16, :]).then_inc(s["ld"], 16)
                sp.dma_start(eps1[:], t["L2_gnn_eps_list"].partition_broadcast(P)).then_inc(s["ld"], 16)
                sp.dma_start(src_i[:], t["src"].rearrange("(p c) -> p c", p=EP)).then_inc(s["ld"], 16)
                sp.dma_start(dst_i[:], t["dst"].rearrange("(p c) -> p c", p=EP)).then_inc(s["ld"], 16)
                sp.dma_start(edge_w[:], t["edge_weight"].rearrange("(p c) -> p c", p=EP)).then_inc(s["ld"], 16)
                assert n + 6 == len(COLS) + 3 * len(BIASES) + 6
                sp.wait_ge(s["set"], 1)
                for k in range(2):
                    sp.dma_start(table[k][NPAD:NPAD + P, :], zrow[:]).then_inc(s["st"], 16)
                sp.dma_start(degree.rearrange("(p c) a -> p (c a)", p=P), ones[:]).then_inc(s["st"], 16)
                sp.wait_ge(s["st"], 48)

            LOADS = 16 * (len(COLS) + 3 * len(BIASES) + 6)

            @block.tensor
            def _(pe):
                pe.wait_ge(s["u3"], 1)
                nc.tensor.matmul(psc[0:3, :], u3[:], w1c[:], start=True, stop=True).then_inc(s["mm"], 1)

            @block.vector
            def _(dve):
                m = Marks(dve, s["dv"])

                def link(ins):
                    m.up(ins)
                    m.wait()
                nc.vector.memset(zrow[:], 0.0)
                nc.vector.memset(ones[:], 1.0).then_inc(s["set"], 1)
                nc.vector.memset(onescol[:], 1.0)
                link(nc.vector.memset(ones3[:], 1.0))
                dve.wait_ge(s["ld"], LOADS)
                nc.vector.tensor_copy(u3[:], ucol[:, 0:1].to_broadcast([16, 3])).then_inc(s["u3"], 1)
                dve.wait_ge(s["mm"], 1)
                c = BIASES.index("l1c")
                link(nc.vector.tensor_tensor(brow[:, c, :], psc[0:3, :], brow[:, c, :], ALU.add))
                link(nc.vector.tensor_scalar(eps1[:], eps1[:], 1.0, None, ALU.add))
                link(nc.vector.tensor_copy(hi[:], brow[:]))
                link(nc.vector.tensor_tensor(rest[:], brow[:], hi[:], ALU.subtract))
                link(nc.vector.tensor_copy(mid[:], rest[:]))
                link(nc.vector.tensor_tensor(rest[:], rest[:], mid[:], ALU.subtract))
                link(nc.vector.tensor_copy(lo[:], rest[:]))
                dve.wait_ge(s["pi"], 1)
                link(nc.vector.tensor_scalar(pick[:], hi[:], ident[0:3, 0:1], None, ALU.mult))
                link(nc.vector.scalar_tensor_tensor(out=pick2[:], in0=mid[:], scalar=ident[0:3, 1:2], in1=pick[:],
                                                    op0=ALU.mult, op1=ALU.add))
                link(nc.vector.scalar_tensor_tensor(out=pick[:], in0=lo[:], scalar=ident[0:3, 2:3], in1=pick2[:],
                                                    op0=ALU.mult, op1=ALU.add))
                for j in range(J):
                    link(nc.vector.tensor_copy(bias3[:, :, j * D:(j + 1) * D], pick[:]))
                for k in range(4):
                    b = col("gfcb") if k == 0 else col(f"cb{k - 1}")
                    link(nc.vector.tensor_scalar(bnsc[:, k:k + 1], col(f"bng{k}"), (1.0 + 1e-5) ** -0.5, None, ALU.mult))
                    link(nc.vector.scalar_tensor_tensor(out=bnbi[:, k:k + 1], in0=b, scalar=bnsc[:, k:k + 1],
                                                        in1=col(f"bnb{k}"), op0=ALU.mult, op1=ALU.add))
        run_block("prep", ["pz", "pi", "ld", "set", "st", "u3", "mm", "dv"], prepare)

        dstf = keep("dstf", [EP, TILES])
        count = keep("count", [EP, TILES])
        before = keep("before", [EP, TILES])

        def match_edges(ctx, block, s):
            def sb(name, shape, dt=F32):
                return ctx.enter_context(nc.sbuf_tensor(f"{stage[0]}_{name}", shape, dt))
            lower = sb("lower", [EP, EP])
            ZW = 4 * GROUP
            zeros = sb("zeros", [P, ZW])
            spare = sb("spare", [EP, TILES])
            tmp = sb("tmp", [EP, TILES])
            late = sb("late", [EP, TILES])
            wide = [sb(f"wide{r}", [EP, EP]) for r in range(RING)]
            eq = [sb(f"eq{r}", [EP, EP]) for r in range(RING)]
            odd_even = [sb(f"odd_even{r}", [EP, EP]) for r in range(0, RING, 2)]
            even_odd = [sb(f"even_odd{r}", [EP, EP]) for r in range(0, RING, 2)]
            more_count = sb("more_count", [EP, TILES])
            more_before = sb("more_before", [EP, TILES])
            low = [sb(f"low{r}", [EP, EP]) for r in range(RING)]
            ps = [ctx.enter_context(nc.psum_tensor(f"{stage[0]}_ps{r}", [P, 512], F32)) for r in range(RING)]

            HALF = RING // 2

            @block.gpsimd
            def _(pool):
                nc.gpsimd.memset(lower[:], 1.0).then_inc(s["pc"], 1)
                pool.wait_ge(s["pc"], 1)
                nc.gpsimd.affine_select(out=lower[:], in_=lower[:], compare_op=ALU.is_gt, fill=0.0,
                                        base=0, pattern=[[-1, EP]], channel_multiplier=1).then_inc(s["pc"], 1)
                nc.gpsimd.iota(spare[:], [[0, TILES]], base=NPAD, channel_multiplier=1,
                               allow_small_or_imprecise_dtypes=True).then_inc(s["pc"], 1)

            @block.sync
            def _(sp):
                flat = attr_sum.rearrange("(p n) d -> p (n d)", p=P)
                n = 0
                for a in range(0, NPAD + P, ZW):
                    c = min(ZW, NPAD + P - a)
                    sp.wait_ge(s["zero"], 1)
                    sp.dma_start(flat[:, a:a + c], zeros[:, 0:c]).then_inc(s["zst"], 16)
                    n += 1
                sp.wait_ge(s["zst"], 16 * n)

            @block.tensor
            def _(pe):
                def body(i):
                    for r in range(RING):
                        pe.wait_ge(s["wide"], RING * i + r + 1)
                        if not (isinstance(i, int) and i == 0):
                            pe.wait_ge(s["eqx"], HALF * i + r // 2 + 1 - HALF)
                        nc.tensor.transpose(ps[r][0:EP, 0:EP], wide[r][:], ident[0:EP, 0:EP]).then_inc(s["tr"], 1)
                sweep(pe, EITER, body)

            @block.vector
            def _(dve):
                m = Marks(dve, s["dv"])

                def link(ins):
                    m.up(ins)
                    m.wait()
                nc.vector.memset(zeros[:], 0.0).then_inc(s["zero"], 1)
                nc.vector.memset(more_count[:], 0.0)
                nc.vector.memset(more_before[:], 0.0)
                link(nc.vector.tensor_copy(dstf[:], dst_i[:]))
                dve.wait_ge(s["pc"], 3)

                def body(i):
                    for r in range(RING):
                        t_ = RING * i + r
                        if not (isinstance(i, int) and i == 0):
                            dve.wait_ge(s["tr"], RING * i + r + 1 - RING)
                        d = dstf[:, bass.ds(t_, 1)]
                        nc.vector.tensor_copy(wide[r][:], d.to_broadcast([EP, EP])).then_inc(s["wide"], 1)
                    for r in range(RING):
                        t_ = RING * i + r
                        dve.wait_ge(s["tr"], RING * i + r + 1)
                        nc.vector.tensor_scalar(eq[r][:], ps[r][0:EP, 0:EP], dstf[:, bass.ds(t_, 1)], None,
                                                ALU.is_equal).then_inc(s["eq"], 1)
                    for h in range(HALF):
                        even, odd = RING * i + 2 * h, RING * i + 2 * h + 1
                        nc.vector.tensor_scalar(odd_even[h][:], ps[2 * h][0:EP, 0:EP], dstf[:, bass.ds(odd, 1)], None,
                                                ALU.is_equal)
                        nc.vector.tensor_scalar(even_odd[h][:], ps[2 * h + 1][0:EP, 0:EP], dstf[:, bass.ds(even, 1)], None,
                                                ALU.is_equal).then_inc(s["eqx"], 1)
                    for r in range(RING):
                        t_ = RING * i + r
                        dve.wait_ge(s["eq"], RING * i + r + 1)
                        nc.vector.tensor_copy(same[:, bass.ds(t_, 1), :].rearrange("p a f -> p (a f)"), eq[r][:])
                        nc.vector.tensor_reduce(count[:, bass.ds(t_, 1)], eq[r][:], AX.X, ALU.add)
                        nc.vector.tensor_tensor(low[r][:], eq[r][:], lower[:], ALU.mult).then_inc(s["low"], 1)
                    for r in range(RING):
                        t_ = RING * i + r
                        dve.wait_ge(s["low"], RING * i + r + 1)
                        nc.vector.tensor_reduce(before[:, bass.ds(t_, 1)], low[r][:], AX.X, ALU.add).then_inc(s["red"], 1)
                    for h in range(HALF):
                        even, odd = RING * i + 2 * h, RING * i + 2 * h + 1
                        dve.wait_ge(s["eqx"], HALF * i + h + 1)
                        nc.vector.tensor_copy(cross[:, bass.ds(HALF * i + h, 1), :].rearrange("p a f -> p (a f)"),
                                              odd_even[h][:])
                        nc.vector.tensor_reduce(more_before[:, bass.ds(odd, 1)], odd_even[h][:], AX.X, ALU.add)
                        nc.vector.tensor_reduce(more_count[:, bass.ds(even, 1)], even_odd[h][:], AX.X, ALU.add
                                                ).then_inc(s["redx"], 1)
                sweep(dve, EITER, body)
                dve.wait_ge(s["red"], TILES)
                dve.wait_ge(s["redx"], TILES // 2)
                link(nc.vector.tensor_tensor(count[:], count[:], more_count[:], ALU.add))
                link(nc.vector.tensor_tensor(before[:], before[:], more_before[:], ALU.add))
                link(nc.vector.tensor_scalar(late[:], before[:], 0.5, None, ALU.is_gt))
                link(nc.vector.tensor_tensor(tmp[:], spare[:], dstf[:], ALU.subtract))
                link(nc.vector.tensor_tensor(tmp[:], tmp[:], late[:], ALU.mult))
                link(nc.vector.tensor_tensor(tmp[:], tmp[:], dstf[:], ALU.add))
                link(nc.vector.tensor_copy(put_i[:], tmp[:]))
        run_block("match", ["zero", "zst", "pc", "wide", "tr", "eq", "low", "red", "eqx", "redx", "dv"], match_edges)

        SLOTS = (0, 1)

        def first_step(i):
            return isinstance(i, int) and i == 0

        def last_step(i):
            return isinstance(i, int) and i == PAIRS - 1

        def is_tail(i, b):
            return last_step(i) and b == 1

        def nth(i, b):
            return 2 * i + b + 1

        def again(eng, sem, i, b):
            if not first_step(i):
                eng.wait_ge(sem, 2 * i + b - 1)

        def turn4(ps, src):
            for j in range(J):
                last = nc.tensor.transpose(ps[:, j * D:(j + 1) * D], src[:, j * D:(j + 1) * D], ident[:])
            return last

        def rows4(ps, feat, w, bias_name=None):
            if bias_name:
                nc.tensor.matmul(ps[:], ones3[:], bias(bias_name), start=True, stop=False)
            for j in range(J):
                last = nc.tensor.matmul(ps[:, j * D:(j + 1) * D], feat[:, j * D:(j + 1) * D], w[:],
                                        start=not bias_name, stop=True if not bias_name else j == J - 1)
            return last

        def norm_tiles(sb, name):
            return dict(st=[sb(f"{name}st{b}", [P, J, 6]) for b in SLOTS], mv=sb(f"{name}mv", [P, 2, J, 2]),
                        sd=sb(f"{name}sd", [P, 2, J]), rs=sb(f"{name}rs", [P, 2, J]))

        def norm_on_dve(dve, m, i, T, src, dst, ready, var, std, done):
            for b in SLOTS:
                ready(b)
                for j in range(J):
                    last = nc.vector.bn_stats(T["st"][b][:, j, :], src[b][:, j * D:(j + 1) * D])
                m.up(last)
            m.settle()
            for b in SLOTS:
                for j in range(J):
                    last = nc.vector.bn_aggr(T["mv"][:, b, j, :], T["st"][b][:, j, :])
            last.then_inc(var, 1)
            dve.wait_ge(std, i + 1)
            m.up(nc.vector.reciprocal(T["rs"][:], T["sd"][:]))
            m.wait()
            for b in SLOTS:
                for j in range(J):
                    last = nc.vector.tensor_scalar(dst[b][:, j * D:(j + 1) * D], src[b][:, j * D:(j + 1) * D],
                                                   T["mv"][:, b, j, 0:1], T["rs"][:, b, j:j + 1],
                                                   ALU.subtract, ALU.mult)
                last.then_inc(done, 1)

        def root_on_act(act, i, T, var, std, eps):
            act.wait_ge(var, i + 1)
            nc.scalar.activation(T["sd"][:], T["mv"][:, :, :, 1], ACT.Sqrt, bias=eps).then_inc(std, 1)

        epsc = keep("epsc", [P, 3])
        eps_ln, eps_half, eps_zero = epsc[:, 0:1], epsc[:, 1:2], epsc[:, 2:3]

        def weight_tiles(ctx, names):
            return {n: ctx.enter_context(nc.sbuf_tensor(f"{stage[0]}_w_{n}", [P, D], F32)) for n in names}

        def kv_tiles(sb):
            return dict(kc=[sb(f"kc{b}", [P, GROUP]) for b in SLOTS], kf=[sb(f"kf{b}", [P, GROUP]) for b in SLOTS],
                        sk=[sb(f"sk{b}", [P, GROUP]) for b in SLOTS], ss=sb("ss", [P, 2, J]),
                        nk=sb("nk", [P, 2, J]), rk=sb("rk", [P, 2, J]),
                        vs=[sb(f"vs{b}", [P, J, D + 1]) for b in SLOTS])

        KV_SEMS = ["kv", "kc", "kf", "sk", "ss", "nk", "vs", "acc"]

        def kv_on_act(act, s, i, T, k_ps):
            for b in SLOTS:
                act.wait_ge(s["kv"], nth(i, b))
                again(act, s["kf"], i, b)
                nc.scalar.copy(T["kc"][b][:], k_ps[b][:]).then_inc(s["kc"], 1)
            for b in SLOTS:
                act.wait_ge(s["kf"], nth(i, b))
                nc.scalar.activation(T["sk"][b][:], T["kf"][b][:], ACT.Square).then_inc(s["sk"], 1)
            act.wait_ge(s["ss"], i + 1)
            nc.scalar.activation(T["nk"][:], T["ss"][:], ACT.Sqrt).then_inc(s["nk"], 1)

        def kv_on_dve(dve, m, s, i, T, v_ps):
            for b in SLOTS:
                dve.wait_ge(s["kc"], nth(i, b))
                again(dve, s["acc"], i, b)
                nc.vector.scalar_tensor_tensor(out=T["kf"][b][:], in0=T["kc"][b][:], scalar=0.0, in1=T["kc"][b][:],
                                               op0=ALU.is_equal, op1=ALU.add).then_inc(s["kf"], 1)
            for b in SLOTS:
                dve.wait_ge(s["sk"], nth(i, b))
                last = nc.vector.tensor_reduce(T["ss"][:, b, :], T["sk"][b][:].rearrange("p (j d) -> p j d", j=J),
                                               AX.X, ALU.add)
            last.then_inc(s["ss"], 1)
            dve.wait_ge(s["nk"], i + 1)
            m.up(nc.vector.reciprocal(T["rk"][:], T["nk"][:]))
            m.wait()
            for b in SLOTS:
                r = T["rk"][:, b, :]
                nc.vector.tensor_tensor(T["vs"][b][:, :, 0:D], v_ps[b][:].rearrange("p (j d) -> p j d", j=J),
                                        r.unsqueeze(2).to_broadcast([P, J, D]), ALU.mult)
                nc.vector.tensor_copy(T["vs"][b][:, :, D:D + 1], r.unsqueeze(2)).then_inc(s["vs"], 1)

        def kv_on_pe(pe, s, i, T, acc_ps):
            for b in SLOTS:
                pe.wait_ge(s["vs"], nth(i, b))
                rows = TAILP if is_tail(i, b) else P
                for j in range(J):
                    last = nc.tensor.matmul(acc_ps[:, 0:D + 1], T["kf"][b][0:rows, j * D:(j + 1) * D],
                                            T["vs"][b][0:rows, j, :],
                                            start=first_step(i) and b == 0 and j == 0,
                                            stop=is_tail(i, b) and j == J - 1, skip_group_check=True)
                last.then_inc(s["acc"], 1)

        def kv_end(act, s, acc_ps):
            act.wait_ge(s["acc"], G)
            nc.scalar.mul(kvsum[:], acc_ps[:, 0:D + 1], 1.0 / N).then_inc(s["kvdone"], 1)

        def load_and_store(sp, loads, stores):
            def body(i):
                loads(i)
                if not first_step(i):
                    stores(i - 1)
            sweep(sp, PAIRS, body)
            stores(PAIRS - 1)

        W = t["L0_gnn_qkv_w"]

        def st(*names):
            return [f"{n}{b}" for n in names for b in SLOTS]

        def set_eps(ctx, block, s):
            @block.vector
            def _(dve):
                nc.vector.memset(eps_ln, LN_EPS)
                nc.vector.memset(eps_half, 4 * LN_EPS)
                nc.vector.memset(eps_zero, 0.0)
        run_block("eps", [], set_eps)

        class Ring:

            def __init__(self, sb, name, width, dt=F32):
                self.t = [sb(f"{name}{r}", [EP, width], dt) for r in range(RING)]

        def degree_tiles(sb):
            return dict(put=Ring(sb, "put", 1, I32).t, num=Ring(sb, "num", 1).t, si=Ring(sb, "si", 1, I32).t,
                        di=Ring(sb, "di", 1, I32).t, gs=Ring(sb, "gs", 1).t, gd=Ring(sb, "gd", 1).t,
                        deg_s=sb("deg_s", [EP, TILES]), deg_d=sb("deg_d", [EP, TILES]), deg_n=sb("deg_n", [P, G, J]),
                        ratio=sb("ratio", [EP, TILES]))
        DEGREE_SEMS = ["dcopy", "sw_added", "sw_dn", "icopy", "back", "ratio", "rdeg", "pace"] + [f"sw_got{r}" for r in range(RING)]

        def degrees_on_pool(pool, s, T):
            def add_counts(i):
                for r in range(RING):
                    tile = RING * i + r
                    nc.gpsimd.tensor_copy(T["put"][r][:], put_i[:, bass.ds(tile, 1)])
                    nc.gpsimd.tensor_copy(T["num"][r][:], count[:, bass.ds(tile, 1)]).then_inc(s["dcopy"], 1)
                    pool.wait_ge(s["dcopy"], tile + 1)
                    if r % 2 == 0 and not (first_step(i) and r == 0):
                        pool.wait_ge(s["sw_added"], before_stage("sw_added") + 16 * tile)
                    pool.sem_inc(s["pace"], 1)
                    nc.gpsimd.indirect_dma_start(degree, bass.IndirectOffsetOnAxis(T["put"][r][:, 0:1], 0), T["num"][r][:],
                                                 None, compute_op=ALU.add).then_inc(s["sw_added"], 16)
            sweep(pool, EITER, add_counts)
            pool.wait_ge(s["sw_added"], before_stage("sw_added") + 16 * TILES)
            pool.dma_start(T["deg_n"][:], degree[0:NPAD, :].rearrange("(g p j) a -> p g (j a)", p=P, j=J)).then_inc(s["sw_dn"], 16)

            def copy_back(i):
                for r in range(RING):
                    tile = RING * i + r
                    pool.wait_ge(s[f"sw_got{r}"], before_stage(f"sw_got{r}") + 32 * (i + 1))
                    pool.sem_inc(s["pace"], 1)
                    nc.gpsimd.tensor_copy(T["deg_s"][:, bass.ds(tile, 1)], T["gs"][r][:])
                    nc.gpsimd.tensor_copy(T["deg_d"][:, bass.ds(tile, 1)], T["gd"][r][:]).then_inc(s["back"], 1)

            def read_degrees(i):
                if not first_step(i):
                    copy_back(i - 1)
                for r in range(RING):
                    tile = RING * i + r
                    if not first_step(i):
                        pool.wait_ge(s["back"], tile + 1 - RING)
                        pool.sem_inc(s["pace"], 1)
                    nc.gpsimd.tensor_copy(T["si"][r][:], src_i[:, bass.ds(tile, 1)])
                    nc.gpsimd.tensor_copy(T["di"][r][:], dst_i[:, bass.ds(tile, 1)]).then_inc(s["icopy"], 1)
                    pool.wait_ge(s["icopy"], tile + 1)
                    pool.sem_inc(s["pace"], 1)
                    nc.gpsimd.indirect_dma_start(T["gs"][r][:], None, degree, bass.IndirectOffsetOnAxis(T["si"][r][:, 0:1], 0)
                                                 ).then_inc(s[f"sw_got{r}"], 16)
                    nc.gpsimd.indirect_dma_start(T["gd"][r][:], None, degree, bass.IndirectOffsetOnAxis(T["di"][r][:, 0:1], 0)
                                                 ).then_inc(s[f"sw_got{r}"], 16)
            read_degrees(0)
            with pool.Fori(1, EITER) as i:
                read_degrees(i)
            copy_back(EITER - 1)

        def degrees_on_dve(dve, s, T):
            dve.wait_ge(s["sw_dn"], before_stage("sw_dn") + 16)
            nc.vector.reciprocal(dinv2[:], T["deg_n"][:].rearrange("p g j -> p (g j)"))
            dve.wait_ge(s["back"], TILES)
            nc.vector.reciprocal(T["ratio"][:], T["deg_s"][:]).then_inc(s["rdeg"], 1)
            dve.wait_ge(s["rdeg"], 1)
            nc.vector.tensor_tensor(T["ratio"][:], T["ratio"][:], T["deg_d"][:], ALU.mult).then_inc(s["ratio"], 1)

        def degrees_on_act(act, s, T):
            act.wait_ge(s["ratio"], 1)
            nc.scalar.activation(gcn_coef[:], T["ratio"][:], ACT.Sqrt)

        def add_tiles(sb):
            return dict(idx=Ring(sb, "aidx", 1, I32).t, msg=Ring(sb, "amsg", D).t)

        def add_on_pool(pool, s, T, rows, done):
            before = before_stage("sw_added") + 16 * done

            def body(i):
                for r in range(RING):
                    tile = RING * i + r
                    nc.gpsimd.tensor_copy(T["idx"][r][:], put_i[:, bass.ds(tile, 1)])
                    nc.gpsimd.tensor_copy(T["msg"][r][:], added[:, bass.ds(tile, 1), :].rearrange("p a f -> p (a f)")
                                          ).then_inc(s["acopy"], 1)
                    pool.wait_ge(s["acopy"], tile + 1)
                    if r % 2 == 0 and not (first_step(i) and r == 0):
                        pool.wait_ge(s["sw_added"], before + 16 * tile)
                    pool.sem_inc(s["pace"], 1)
                    nc.gpsimd.indirect_dma_start(rows, bass.IndirectOffsetOnAxis(T["idx"][r][:, 0:1], 0), T["msg"][r][:], None,
                                                 compute_op=ALU.add).then_inc(s["sw_added"], 16)
            sweep(pool, EITER, body)
            pool.wait_ge(s["sw_added"], before + 16 * TILES)

        QUAD = 4

        def edge_tiles(ctx, sb):
            return dict(gidx=[sb(f"gidx{r}", [EP, 1], I32) for r in range(QUAD)],
                        pidx=[sb(f"pidx{r}", [EP, 1], I32) for r in range(QUAD)],
                        got=[sb(f"egot{r}", [EP, D]) for r in range(QUAD)],
                        mix=[sb(f"emix{r}", [EP, EP]) for r in range(QUAD)],
                        mixx=[sb(f"emixx{h}", [EP, EP]) for h in range(QUAD // 2)], msg=sb("emsg", [EP, QUAD, D]),
                        ps=ctx.enter_context(nc.psum_tensor(f"{stage[0]}_edge_ps", [P, QUAD * D], F32)))
        EDGE_SEMS = ["emix", "emm", "emsg", "gidx", "pidx", "epace", "sw_added"] + [f"sw_got{r}" for r in range(QUAD)]
        EDGE_COUNTS = {"sw_added": 16 * TILES, **{f"sw_got{r}": 16 * FOURS for r in range(QUAD)}}

        def edges_on_pool(pool, s, Q, source, target):
            def get(i, r):
                tile = QUAD * i + r
                if not first_step(i):
                    pool.wait_ge(s["emm"], i)
                    pool.sem_inc(s["epace"], 1)
                nc.gpsimd.tensor_copy(Q["gidx"][r][:], src_i[:, bass.ds(tile, 1)]).then_inc(s["gidx"], 1)
                pool.wait_ge(s["gidx"], tile + 1)
                pool.sem_inc(s["epace"], 1)
                nc.gpsimd.indirect_dma_start(Q["got"][r][:], None, source, bass.IndirectOffsetOnAxis(Q["gidx"][r][:, 0:1], 0)
                                             ).then_inc(s[f"sw_got{r}"], 16)

            def put(i, r):
                tile = QUAD * i + r
                nc.gpsimd.tensor_copy(Q["pidx"][r][:], put_i[:, bass.ds(tile, 1)]).then_inc(s["pidx"], 1)
                pool.wait_ge(s["pidx"], tile + 1)
                pool.wait_ge(s["emsg"], i + 1)
                if r % 2 == 0 and not (first_step(i) and r == 0):
                    pool.wait_ge(s["sw_added"], before_stage("sw_added") + 16 * tile)
                pool.sem_inc(s["epace"], 1)
                nc.gpsimd.indirect_dma_start(target, bass.IndirectOffsetOnAxis(Q["pidx"][r][:, 0:1], 0), Q["msg"][:, r, :], None,
                                             compute_op=ALU.add).then_inc(s["sw_added"], 16)

            def body(i):
                for r in range(0, QUAD, 2):
                    get(i, r)
                    get(i, r + 1)
                    if not first_step(i):
                        put(i - 1, r)
                        put(i - 1, r + 1)
            body(0)
            body(1)
            with pool.Fori(2, FOURS) as i:
                body(i)
            for r in range(QUAD):
                put(FOURS - 1, r)
            pool.wait_ge(s["sw_added"], before_stage("sw_added") + 16 * TILES)

        def edges_on_dve(dve, s, Q, coef):
            def part(i):
                if not first_step(i):
                    dve.wait_ge(s["emm"], i)
                for r in range(QUAD):
                    tile = QUAD * i + r
                    last = nc.vector.tensor_scalar(Q["mix"][r][:], same[:, bass.ds(tile, 1), :].rearrange("p a f -> p (a f)"),
                                                   coef[:, bass.ds(tile, 1)], None, ALU.mult)
                for h in range(QUAD // 2):
                    last = nc.vector.tensor_scalar(
                        Q["mixx"][h][:], cross[:, bass.ds(QUAD // 2 * i + h, 1), :].rearrange("p a f -> p (a f)"),
                        coef[:, bass.ds(QUAD * i + 2 * h + 1, 1)], None, ALU.mult)
                last.then_inc(s["emix"], 1)
            return part

        def edges_on_pe(pe, s, Q):
            def part(i):
                pe.wait_ge(s["emix"], i + 1)
                if not first_step(i):
                    pe.wait_ge(s["emsg"], i)
                for r in range(QUAD):
                    pe.wait_ge(s[f"sw_got{r}"], before_stage(f"sw_got{r}") + 16 * (i + 1))
                    if r % 2 == 1:
                        even = Q["ps"][0:EP, (r - 1) * D:r * D]
                        nc.tensor.matmul(even, Q["mix"][r - 1][:], Q["got"][r - 1][:], start=True, stop=False)
                        nc.tensor.matmul(even, Q["mixx"][r // 2][:], Q["got"][r][:], start=False, stop=True)
                        last = nc.tensor.matmul(Q["ps"][0:EP, r * D:(r + 1) * D], Q["mix"][r][:], Q["got"][r][:],
                                                start=True, stop=True)
                last.then_inc(s["emm"], 1)
            return part

        def edges_on_act(act, s, Q):
            def part(i):
                act.wait_ge(s["emm"], i + 1)
                if not first_step(i):
                    act.wait_ge(s["sw_added"], before_stage("sw_added") + 16 * QUAD * i)
                nc.scalar.copy(Q["msg"][:], Q["ps"][0:EP, :].rearrange("p (r d) -> p r d", r=QUAD)).then_inc(s["emsg"], 1)
            return part

        def there(g, pairs=PAIRS):
            return not isinstance(g, int) or 0 <= g < 2 * pairs

        def ran(eng, sem, g):
            eng.wait_ge(sem, g + 1)

        def free1(eng, sem, g):
            if not (isinstance(g, int) and g < 1):
                eng.wait_ge(sem, g)

        def free2(eng, sem, g):
            if not (isinstance(g, int) and g < 2):
                eng.wait_ge(sem, g - 1)

        def landed(eng, sems, g, i, b, per_group=1):
            eng.wait_ge(sems[b], 16 * per_group * (i + 1))

        def stored(eng, sems, g, i, b, per_group=1):
            if not (isinstance(g, int) and g < 2):
                eng.wait_ge(sems[b], 16 * per_group * i)

        def step_sweep(eng, step, lag, pairs=PAIRS, edges=None):
            peel = (lag + 3) // 2
            more = (lag + 1) // 2

            def pair(i):
                for b in SLOTS:
                    if not isinstance(i, int) or 2 * i + b < 2 * pairs + lag:
                        step(2 * i + b, i, b)
                if edges and (not isinstance(i, int) or i < FOURS):
                    edges(i)

            for i in range(peel):
                pair(i)
            with_edges = min(FOURS, pairs - 1) if edges else peel
            if with_edges > peel:
                with eng.Fori(peel, with_edges) as i:
                    pair(i)
            else:
                with_edges = peel
            if pairs - 1 > with_edges:
                with eng.Fori(with_edges, pairs - 1) as i:
                    for b in SLOTS:
                        step(2 * i + b, i, b)
            for i in range(pairs - 1, max(pairs + more, FOURS if edges else 0)):
                pair(i)

        def tail_of(g):
            return isinstance(g, int) and g == G - 1

        def rows_of(g):
            return TAILP if tail_of(g) else P

        def stats4(tiles, src):
            for j in range(J):
                last = nc.vector.bn_stats(tiles["st"][:, j, :], src[:, j * D:(j + 1) * D])
            return last

        def aggr4(tiles):
            for j in range(J):
                last = nc.vector.bn_aggr(tiles["mv"][:, j, :], tiles["st"][:, j, :])
            return last

        def apply4(tiles, dst, src):
            for j in range(J):
                js = slice(j * D, (j + 1) * D)
                last = nc.vector.tensor_scalar(dst[:, js], src[:, js], tiles["mv"][:, j, 0:1], tiles["rs"][:, j:j + 1],
                                               ALU.subtract, ALU.mult)
            return last

        def norm1_tiles(sb, name):
            return dict(st=sb(f"{name}st", [P, J, 6]), mv=sb(f"{name}mv", [P, J, 2]), sd=sb(f"{name}sd", [P, J]),
                        rs=sb(f"{name}rs", [P, J]))

        def norm_sems(k):
            return [f"{n}{k}" for n in ("stats", "var", "std", "rstd", "nn")]

        def norm_stats(dve, s, k, T, src, g):
            stats4(T, src).then_inc(s[f"stats{k}"], 1)

        def norm_vars(dve, s, k, T, g):
            ran(dve, s[f"stats{k}"], g)
            dve.sem_inc(s["pace"], 1)
            aggr4(T).then_inc(s[f"var{k}"], 1)

        def norm_root(act, s, k, T, g, eps):
            ran(act, s[f"var{k}"], g)
            nc.scalar.activation(T["sd"][:], T["mv"][:, :, 1], ACT.Sqrt, bias=eps).then_inc(s[f"std{k}"], 1)

        def norm_recip(dve, s, k, T, g):
            ran(dve, s[f"std{k}"], g)
            nc.vector.reciprocal(T["rs"][:], T["sd"][:]).then_inc(s[f"rstd{k}"], 1)

        def norm_apply(dve, s, k, T, dst, src, g):
            ran(dve, s[f"rstd{k}"], g)
            apply4(T, dst, src).then_inc(s[f"nn{k}"], 1)

        def kv1_tiles(sb):
            return dict(kc=sb("kc", [P, GROUP]), kf=[sb(f"kf{b}", [P, GROUP]) for b in SLOTS], sk=sb("sk", [P, GROUP]),
                        ss=sb("ss", [P, J]), nk=sb("nk", [P, J]), rk=sb("rk", [P, J]),
                        vs=[sb(f"vs{b}", [P, J, D + 1]) for b in SLOTS])
        KV1_SEMS = ["k", "v2", "kc", "kf", "sk", "ss", "nk", "rk", "vs", "acc"]

        def pair_of(sb, name):
            return [sb(f"{name}{b}", [P, GROUP]) for b in SLOTS]

        def kv_copy(act, s, T, k_ps, g):
            ran(act, s["k"], g)
            free1(act, s["kf"], g)
            nc.scalar.copy(T["kc"][:], k_ps[:]).then_inc(s["kc"], 1)

        def kv_fix(dve, s, T, g, b):
            ran(dve, s["kc"], g)
            free2(dve, s["acc"], g)
            nc.vector.scalar_tensor_tensor(out=T["kf"][b][:], in0=T["kc"][:], scalar=0.0, in1=T["kc"][:],
                                           op0=ALU.is_equal, op1=ALU.add).then_inc(s["kf"], 1)

        def kv_square(act, s, T, g, b):
            ran(act, s["kf"], g)
            free1(act, s["ss"], g)
            nc.scalar.activation(T["sk"][:], T["kf"][b][:], ACT.Square).then_inc(s["sk"], 1)

        def kv_length(dve, s, T, g):
            ran(dve, s["sk"], g)
            nc.vector.tensor_reduce(T["ss"][:], T["sk"][:].rearrange("p (j d) -> p j d", j=J), AX.X, ALU.add
                                    ).then_inc(s["ss"], 1)

        def kv_root(act, s, T, g):
            ran(act, s["ss"], g)
            nc.scalar.activation(T["nk"][:], T["ss"][:], ACT.Sqrt).then_inc(s["nk"], 1)

        def kv_scale(dve, s, T, v_ps, g, b):
            ran(dve, s["nk"], g)
            nc.vector.reciprocal(T["rk"][:], T["nk"][:]).then_inc(s["rk"], 1)
            ran(dve, s["rk"], g)
            ran(dve, s["v2"], g)
            free2(dve, s["acc"], g)
            r = T["rk"][:, :]
            nc.vector.tensor_tensor(T["vs"][b][:, :, 0:D], v_ps[:].rearrange("p (j d) -> p j d", j=J),
                                    r.unsqueeze(2).to_broadcast([P, J, D]), ALU.mult)
            nc.vector.tensor_copy(T["vs"][b][:, :, D:D + 1], r.unsqueeze(2)).then_inc(s["vs"], 1)

        def kv_product(pe, s, T, acc_ps, g, b):
            ran(pe, s["vs"], g)
            rows = rows_of(g)
            for j in range(J):
                last = nc.tensor.matmul(acc_ps[:, 0:D + 1], T["kf"][b][0:rows, j * D:(j + 1) * D], T["vs"][b][0:rows, j, :],
                                        start=isinstance(g, int) and g == 0 and j == 0,
                                        stop=tail_of(g) and j == J - 1, skip_group_check=True)
            last.then_inc(s["acc"], 1)

        def pass_first(ctx, block, s):
            def sb(name, shape, dt=F32):
                return ctx.enter_context(nc.sbuf_tensor(f"{stage[0]}_{name}", shape, dt))
            w = weight_tiles(ctx, ["fc", "g", "conv", "k", "v"])
            xt, xn, h0, zn, hT, g0, yo = (pair_of(sb, n) for n in ("xt", "xn", "h0", "zn", "hT", "g0", "yo"))
            T1, T2, TK = norm1_tiles(sb, "n1"), norm1_tiles(sb, "n2"), kv1_tiles(sb)
            tr_ps, z_ps, g_ps, y_ps, tz_ps, k_ps, v_ps, acc_ps = (
                ctx.enter_context(nc.psum_tensor(f"{stage[0]}_ps{n}", [P, GROUP], F32)) for n in range(8))
            ld, g0st, hTst, yost = ([s[f"{n}{b}"] for b in SLOTS] for n in ("ld", "g0st", "hTst", "yost"))
            TD, TA = degree_tiles(sb), add_tiles(sb)

            @block.gpsimd
            def _(pool):
                degrees_on_pool(pool, s, TD)
                add_on_pool(pool, s, TA, attr_sum, TILES)

            @block.sync
            def _(sp):
                for n, v in (("fc", t["L0_gnn_t_fc_w"]), ("g", t["L0_gnn_g_fc_w"]), ("conv", t["L0_gnn_conv_w"][0]),
                             ("k", W[0, 1]), ("v", W[0, 2])):
                    sp.dma_start(w[n][:], v).then_inc(s["w"], 16)

                def step(g, i, b):
                    if there(g):
                        free2(sp, s["nn1"], g)
                        if tail_of(g):
                            sp.dma_start(xt[b][0:TAILP, :], x_tail).then_inc(ld[b], 16)
                        else:
                            sp.dma_start(xt[b][:], at(x_groups, g)).then_inc(ld[b], 16)
                    if there(g - 2):
                        ran(sp, s["g0"], g - 2)
                        sp.dma_start(at(g_first, g - 2), g0[b][:]).then_inc(g0st[b], 16)
                        ran(sp, s["yo"], g - 2)
                        sp.dma_start(at(grouped(table[0]), g - 2), yo[b][:]).then_inc(yost[b], 16)
                        sp.dma_start(at(grouped(table[1]), g - 2), yo[b][:]).then_inc(yost[b], 16)
                    if there(g - 3):
                        ran(sp, s["hT"], g - 3)
                        sp.dma_start(at(cur[0], g - 3), hT[1 - b][:]).then_inc(hTst[1 - b], 16)
                step_sweep(sp, step, 3)
                for sem in g0st + yost + hTst:
                    sp.wait_ge(sem, (32 if sem in yost else 16) * PAIRS)

            @block.tensor
            def _(pe):
                pe.wait_ge(s["w"], 80)
                pe.wait_ge(s["wk"], 1)

                def step(g, i, b):
                    c = 1 - b
                    if there(g - 1):
                        ran(pe, s["h0"], g - 1)
                        free1(pe, s["g0"], g - 1)
                        nc.tensor.matmul(g_ps[:], w["g"][:], h0[c][:], start=True, stop=True).then_inc(s["g"], 1)
                    if there(g - 4):
                        kv_product(pe, s, TK, acc_ps, g - 4, b)
                    if there(g - 3):
                        ran(pe, s["hT"], g - 3)
                        free1(pe, s["kc"], g - 3)
                        rows4(k_ps, hT[c], w["k"]).then_inc(s["k"], 1)
                        free1(pe, s["vs"], g - 3)
                        rows4(v_ps, hT[c], w["v"]).then_inc(s["v2"], 1)
                    if there(g):
                        ran(pe, s["nn1"], g)
                        free1(pe, s["h0"], g)
                        turn4(tr_ps, xn[b]).then_inc(s["tr"], 1)
                    if there(g - 1):
                        ran(pe, s["g0"], g - 1)
                        free1(pe, s["yo"], g - 1)
                        rows4(y_ps, g0[c], w["conv"]).then_inc(s["y"], 1)
                    if there(g - 2):
                        ran(pe, s["nn2"], g - 2)
                        free1(pe, s["hT"], g - 2)
                        turn4(tz_ps, zn[b]).then_inc(s["tz"], 1)
                    if there(g - 1):
                        free1(pe, s["nn2"], g - 1)
                        rows4(z_ps, h0[c], w["fc"], "t_fc").then_inc(s["z"], 1)
                step_sweep(pe, step, 4)

            @block.scalar
            def _(act):
                def step(g, i, b):
                    c = 1 - b
                    if there(g - 1):
                        ran(act, s["g"], g - 1)
                        stored(act, g0st, g - 1, i if b else i - 1, c)
                        free2(act, s["y"], g - 1)
                        nc.scalar.activation(g0[c][:], g_ps[:], ACT.Relu, bias=bnbi[:, 0:1],
                                             scale=bnsc[:, 0:1]).then_inc(s["g0"], 1)
                    if there(g):
                        norm_root(act, s, 1, T1, g, eps_ln)
                    if there(g - 3):
                        kv_copy(act, s, TK, k_ps, g - 3)
                    if there(g - 2):
                        norm_root(act, s, 2, T2, g - 2, eps_ln)
                    if there(g - 3):
                        kv_square(act, s, TK, g - 3, c)
                    if there(g):
                        ran(act, s["tr"], g)
                        free2(act, s["z"], g)
                        nc.scalar.activation(h0[b][:], tr_ps[:], ACT.Relu).then_inc(s["h0"], 1)
                    if there(g - 3):
                        kv_root(act, s, TK, g - 3)
                    if there(g - 1):
                        ran(act, s["y"], g - 1)
                        stored(act, yost, g - 1, i if b else i - 1, c, 2)
                        nc.scalar.copy(yo[c][:], y_ps[:]).then_inc(s["yo"], 1)
                    if there(g - 2):
                        ran(act, s["tz"], g - 2)
                        stored(act, hTst, g - 2, i - 1, b)
                        free2(act, s["v2"], g - 2)
                        nc.scalar.activation(hT[b][:], tz_ps[:], ACT.Relu, bias=col("lnb0"),
                                             scale=col("lng0")).then_inc(s["hT"], 1)
                step_sweep(act, step, 3)
                kv_end(act, s, acc_ps)
                act.wait_ge(s["kvdone"], 1)
                degrees_on_act(act, s, TD)

            @block.vector
            def _(dve):
                dve.wait_ge(s["w"], 80)
                nc.vector.tensor_scalar(w["k"][:], w["k"][:], GUARD, None, ALU.mult).then_inc(s["wk"], 1)

                def step(g, i, b):
                    c = 1 - b
                    if there(g):
                        landed(dve, ld, g, i, b)
                        norm_stats(dve, s, 1, T1, xt[b], g)
                    if there(g - 2):
                        ran(dve, s["z"], g - 2)
                        norm_stats(dve, s, 2, T2, z_ps, g - 2)
                    if there(g):
                        norm_vars(dve, s, 1, T1, g)
                    if there(g - 2):
                        norm_vars(dve, s, 2, T2, g - 2)
                    if there(g - 3):
                        kv_fix(dve, s, TK, g - 3, c)
                    if there(g):
                        norm_recip(dve, s, 1, T1, g)
                    if there(g - 2):
                        norm_recip(dve, s, 2, T2, g - 2)
                    if there(g):
                        free2(dve, s["tr"], g)
                        norm_apply(dve, s, 1, T1, xn[b], xt[b], g)
                    if there(g - 2):
                        free2(dve, s["tz"], g - 2)
                        norm_apply(dve, s, 2, T2, zn[b], z_ps, g - 2)
                    if there(g - 3):
                        kv_length(dve, s, TK, g - 3)
                        kv_scale(dve, s, TK, v_ps, g - 3, c)
                step_sweep(dve, step, 3)
                degrees_on_dve(dve, s, TD)
        FIRST_SEMS = (["acopy"] + [x for x in DEGREE_SEMS if x != "pace"] + ["w", "wk", "h0", "z", "g", "g0", "yo", "y", "hT", "tr", "tz", "kvdone", "pace"] + KV1_SEMS
                      + norm_sems(1) + norm_sems(2) + ["ppace"] + st("ld", "g0st", "hTst", "yost"))
        FIRST_COUNTS = {"sw_added": 32 * TILES, "sw_dn": 16, **{f"sw_got{r}": 32 * EITER for r in range(RING)}}

        def attention(layer, pairs=(0, PAIRS)):
            source, dest, more = cur[layer], cur[1 - layer], layer == 0
            g0, NP = 2 * pairs[0], pairs[1] - pairs[0]

            def here(g):
                return there(g, NP)

            def emit(ctx, block, s):
                def sb(name, shape, dt=F32):
                    return ctx.enter_context(nc.sbuf_tensor(f"{stage[0]}_{name}", shape, dt))
                w = weight_tiles(ctx, ["q", "v"] + (["k2", "v2"] if more else []))
                hT, hn, qc, qf, sq, t1, su, nn, cT = (pair_of(sb, n) for n in (
                    "hT", "hn", "qc", "qf", "sq", "t1", "su", "nn", "cT"))
                nq, rq, cr, den, beta, alpha = (sb(n, [P, J]) for n in ("nq", "rq", "cr", "den", "beta", "alpha"))
                T1, TK = norm1_tiles(sb, "n1"), kv1_tiles(sb)
                th_ps, v_ps, p_ps, small_ps, tc_ps, v2_ps, acc_ps = (
                    ctx.enter_context(nc.psum_tensor(f"{stage[0]}_ps{n}", [P, GROUP], F32)) for n in range(7))
                q_ps = th_ps
                Q = edge_tiles(ctx, sb)
                ld, cTst = ([s[f"{n}{b}"] for b in SLOTS] for n in ("ld", "cTst"))

                @block.sync
                def _(sp):
                    for n, v in (("q", W[layer, 0]), ("v", W[layer, 2])) + ((("k2", W[1, 1]), ("v2", W[1, 2])) if more else ()):
                        sp.dma_start(w[n][:], v).then_inc(s["w"], 16)

                    def step(g, i, b):
                        if here(g):
                            free2(sp, s["v"], g)
                            sp.dma_start(hT[b][:], at(source, g + g0)).then_inc(ld[b], 16)
                        if here(g - 3):
                            ran(sp, s["cT"], g - 3)
                            sp.dma_start(at(dest, g + (g0 - 3)), cT[1 - b][:]).then_inc(cTst[1 - b], 16)
                    step_sweep(sp, step, 3, NP)
                    for sem in cTst:
                        sp.wait_ge(sem, 16 * NP)

                @block.gpsimd
                def _(pool):
                    edges_on_pool(pool, s, Q, table[0], table[1])

                @block.tensor
                def _(pe):
                    pe.wait_ge(s["w"], 64 if more else 32)
                    pe.wait_ge(s["wk"], 1)

                    def step(g, i, b):
                        c = 1 - b
                        if here(g):
                            landed(pe, ld, g, i, b)
                            free1(pe, s["qc"], g)
                            turn4(th_ps, hT[b]).then_inc(s["th"], 1)
                        if more and here(g - 4):
                            kv_product(pe, s, TK, acc_ps, g - 4, b)
                        if here(g):
                            ran(pe, s["hn"], g)
                            nc.tensor.matmul(q_ps[:], w["q"][:], hT[b][:], start=True, stop=True).then_inc(s["q"], 1)
                        if more and here(g - 3):
                            ran(pe, s["cT"], g - 3)
                            rows4(tc_ps, cT[c], w["k2"]).then_inc(s["k"], 1)
                        if here(g):
                            free1(pe, s["su"], g)
                            rows4(v_ps, hT[b], w["v"]).then_inc(s["v"], 1)
                        if more and here(g - 3):
                            free1(pe, s["vs"], g - 3)
                            rows4(v2_ps, cT[c], w["v2"]).then_inc(s["v2"], 1)
                        if here(g):
                            ran(pe, s["qf"], g)
                            free1(pe, s["t1"], g)
                            for j in range(J):
                                last = nc.tensor.matmul(p_ps[:, j * D:(j + 1) * D], qf[b][:, j * D:(j + 1) * D],
                                                        kvsum[:, 0:D], start=True, stop=True)
                            last.then_inc(s["p1"], 1)
                        if here(g - 2):
                            ran(pe, s["nn1"], g - 2)
                            if more:
                                free1(pe, s["kc"], g - 2)
                            else:
                                free1(pe, s["cT"], g - 2)
                            turn4(tc_ps, nn[b]).then_inc(s["tc"], 1)
                        if here(g):
                            ran(pe, s["sq"], g)
                            free1(pe, s["cr"], g)
                            for j in range(J):
                                nc.tensor.matmul(small_ps[:, j:j + 1], qf[b][:, j * D:(j + 1) * D], kvsum[:, D:D + 1],
                                                 start=True, stop=True)
                            for j in range(J):
                                last = nc.tensor.matmul(small_ps[:, J + j:J + j + 1], sq[b][:, j * D:(j + 1) * D], onescol[:],
                                                        start=True, stop=True)
                            last.then_inc(s["n2"], 1)
                    step_sweep(pe, step, 4 if more else 2, NP, edges_on_pe(pe, s, Q))

                @block.scalar
                def _(act):
                    def step(g, i, b):
                        c = 1 - b
                        if here(g):
                            ran(act, s["th"], g)
                            free2(act, s["t1"], g)
                            nc.scalar.copy(hn[b][:], th_ps[:]).then_inc(s["hn"], 1)
                            ran(act, s["q"], g)
                            free2(act, s["qf"], g)
                            nc.scalar.copy(qc[b][:], q_ps[:]).then_inc(s["qc"], 1)
                        if more and here(g - 3):
                            kv_copy(act, s, TK, tc_ps, g - 3)
                            kv_square(act, s, TK, g - 3, c)
                        if here(g):
                            ran(act, s["qf"], g)
                            free2(act, s["n2"], g)
                            nc.scalar.activation(sq[b][:], qf[b][:], ACT.Square).then_inc(s["sq"], 1)
                        if here(g - 2):
                            norm_root(act, s, 1, T1, g - 2, eps_half)
                        if more and here(g - 3):
                            kv_root(act, s, TK, g - 3)
                        if here(g - 2):
                            ran(act, s["tc"], g - 2)
                            stored(act, cTst, g - 2, i - 1, b)
                            if more:
                                free2(act, s["v2"], g - 2)
                            nc.scalar.activation(cT[b][:], tc_ps[:], ACT.Relu, bias=col(f"lnb{layer + 1}"),
                                                 scale=col(f"lng{layer + 1}")).then_inc(s["cT"], 1)
                        if here(g):
                            ran(act, s["n2"], g)
                            free1(act, s["rq"], g)
                            nc.scalar.activation(nq[:], small_ps[:, J:2 * J], ACT.Sqrt).then_inc(s["nq"], 1)
                    step_sweep(act, step, 3 if more else 2, NP, edges_on_act(act, s, Q))
                    if more:
                        kv_end(act, s, acc_ps)
                        act.wait_ge(s["kvdone"], 1)

                @block.vector
                def _(dve):
                    dve.wait_ge(s["w"], 64 if more else 32)
                    if more:
                        nc.vector.tensor_scalar(w["k2"][:], w["k2"][:], GUARD, None, ALU.mult)
                    nc.vector.tensor_scalar(w["q"][:], w["q"][:], GUARD, None, ALU.mult).then_inc(s["wk"], 1)

                    def step(g, i, b):
                        c = 1 - b
                        if here(g - 1):
                            ran(dve, s["nq"], g - 1)
                            nc.vector.reciprocal(rq[:], nq[:]).then_inc(s["rq"], 1)
                            ran(dve, s["rq"], g - 1)
                            nc.vector.tensor_tensor(cr[:], small_ps[:, 0:J], rq[:], ALU.mult).then_inc(s["cr"], 1)
                            ran(dve, s["cr"], g - 1)
                            nc.vector.tensor_scalar(den[:], cr[:], 1.0, None, ALU.add).then_inc(s["den"], 1)
                            ran(dve, s["den"], g - 1)
                            nc.vector.reciprocal(beta[:], den[:]).then_inc(s["beta"], 1)
                            ran(dve, s["beta"], g - 1)
                            nc.vector.tensor_tensor(alpha[:], beta[:], rq[:], ALU.mult).then_inc(s["alpha"], 1)
                            ran(dve, s["alpha"], g - 1)
                            ran(dve, s["hn"], g - 1)
                            for j in range(J):
                                js = slice(j * D, (j + 1) * D)
                                last = nc.vector.scalar_tensor_tensor(out=t1[c][:, js], in0=p_ps[:, js], scalar=alpha[:, j:j + 1],
                                                                      in1=hn[c][:, js], op0=ALU.mult, op1=ALU.add)
                            last.then_inc(s["t1"], 1)
                            ran(dve, s["t1"], g - 1)
                            for j in range(J):
                                js = slice(j * D, (j + 1) * D)
                                last = nc.vector.scalar_tensor_tensor(out=su[c][:, js], in0=v_ps[:, js], scalar=beta[:, j:j + 1],
                                                                      in1=t1[c][:, js], op0=ALU.mult, op1=ALU.add)
                            last.then_inc(s["su"], 1)
                        if here(g - 2):
                            ran(dve, s["su"], g - 2)
                            norm_stats(dve, s, 1, T1, su[b], g - 2)
                        if more and here(g - 3):
                            kv_fix(dve, s, TK, g - 3, c)
                        if here(g - 2):
                            norm_vars(dve, s, 1, T1, g - 2)
                        if here(g):
                            ran(dve, s["qc"], g)
                            free2(dve, s["n2"], g)
                            nc.vector.scalar_tensor_tensor(out=qf[b][:], in0=qc[b][:], scalar=0.0, in1=qc[b][:],
                                                           op0=ALU.is_equal, op1=ALU.add).then_inc(s["qf"], 1)
                        if more and here(g - 3):
                            kv_length(dve, s, TK, g - 3)
                        if here(g - 2):
                            norm_recip(dve, s, 1, T1, g - 2)
                            free2(dve, s["tc"], g - 2)
                            norm_apply(dve, s, 1, T1, nn[b], su[b], g - 2)
                        if more and here(g - 3):
                            kv_scale(dve, s, TK, v2_ps, g - 3, c)
                    step_sweep(dve, step, 3 if more else 2, NP, edges_on_dve(dve, s, Q, gcn_coef))
            return (["w", "wk", "v", "cT", "th", "q", "hn", "qf", "p1", "sq", "n2", "tc", "qc", "nq", "rq", "cr", "den",
                     "beta", "alpha", "t1", "su", "kvdone", "pace"] + EDGE_SEMS + KV1_SEMS + norm_sems(1) + st("ld", "cTst")), emit

        def norm_shift(dve, s, k, T, g):
            ran(dve, s[f"rstd{k}"], g)
            nc.vector.scalar_tensor_tensor(out=T["nb"][:], in0=T["mv"][:, :, 0], scalar=-1.0, in1=T["rs"][:],
                                           op0=ALU.mult, op1=ALU.mult).then_inc(s[f"shift{k}"], 1)

        def norm_apply_act(act, s, k, T, dst, src, g):
            ran(act, s[f"shift{k}"], g)
            for j in range(J):
                js = slice(j * D, (j + 1) * D)
                last = nc.scalar.activation(dst[:, js], src[:, js], ACT.Identity, bias=T["nb"][:, j:j + 1],
                                            scale=T["rs"][:, j:j + 1])
            last.then_inc(s[f"nn{k}"], 1)

        def back(i, b, k):
            return i - (k - b + 1) // 2

        def middle(ctx, block, s):
            def sb(name, shape, dt=F32):
                return ctx.enter_context(nc.sbuf_tensor(f"{stage[0]}_{name}", shape, dt))
            w = weight_tiles(ctx, ["out", "w1", "w2", "w3", "gin"])
            (ta, gf, x1, xr, ag, xb, sc, gr, gx, mT, xo, n0, h0, za, r1, n1, h1, r2, n2, h2, x2, n3, h3, yo, ye) = (
                pair_of(sb, n) for n in ("ta gf x1 xr ag xb sc gr gx mT xo n0 h0 za r1 n1 h1 r2 n2 h2 x2 n3 h3 yo ye").split())
            T = [norm1_tiles(sb, f"t{k}") for k in range(4)]
            for k in (2, 3):
                T[k]["nb"] = sb(f"t{k}nb", [P, J])
            tr_ps, o_ps, t01_ps, z1_ps, z2_ps, t23_ps, z3_ps, y_ps = (
                ctx.enter_context(nc.psum_tensor(f"{stage[0]}_ps{n}", [P, GROUP], F32)) for n in range(8))
            lt, lg, lx, la, lb, xost, x2st, yost = ([s[f"{n}{b}"] for b in SLOTS] for n in (
                "lt", "lg", "lx", "la", "lb", "xost", "x2st", "yost"))
            LAG = 7

            @block.sync
            def _(sp):
                for n, v in (("out", t["L0_gnn_fc_w"]), ("w1", t["L1_gnn_W1"][0:D, :]), ("w2", t["L1_gnn_W2"]),
                             ("w3", t["L1_gnn_W3"]), ("gin", t["L2_gnn_W1"][0])):
                    sp.dma_start(w[n][:], v).then_inc(s["w"], 16)

                def step(g, i, b):
                    c = 1 - b
                    if there(g):
                        free2(sp, s["sc"], g)
                        sp.dma_start(ta[b][:], at(grouped(table[1]), g)).then_inc(lt[b], 16)
                        free2(sp, s["gx"], g)
                        sp.dma_start(gf[b][:], at(g_first, g)).then_inc(lg[b], 16)
                        sp.dma_start(x1[b][:], at(cur[0], g)).then_inc(lg[b], 16)
                        free2(sp, s["xo"], g)
                        if tail_of(g):
                            sp.dma_start(xr[b][0:TAILP, :], x_tail).then_inc(lx[b], 16)
                        else:
                            sp.dma_start(xr[b][:], at(x_groups, g)).then_inc(lx[b], 16)
                    if there(g - 1):
                        free2(sp, s["za"], g - 1)
                        sp.dma_start(ag[c][:], at(grouped(attr_sum), g - 1)).then_inc(la[c], 16)
                    if there(g - 2):
                        ran(sp, s["xo"], g - 2)
                        sp.dma_start(at(grouped(xres[0]), g - 2), xo[b][:]).then_inc(xost[b], 16)
                    if there(g - 6):
                        ran(sp, s["x2"], g - 6)
                        sp.dma_start(at(grouped(xres[1]), g - 6), x2[b][:]).then_inc(x2st[b], 16)
                    if there(g - 4):
                        sp.wait_ge(xost[b], 16 * (i - 1))
                        sp.dma_start(xb[b][:], at(grouped(xres[0]), g - 4)).then_inc(lb[b], 16)
                    if there(g - 7):
                        ran(sp, s["ye"], g - 7)
                        sp.dma_start(at(grouped(table[0]), g - 7), yo[c][:]).then_inc(yost[c], 16)
                        sp.dma_start(at(grouped(table[1]), g - 7), ye[c][:]).then_inc(yost[c], 16)
                step_sweep(sp, step, LAG)
                for sem in xost + x2st:
                    sp.wait_ge(sem, 16 * PAIRS)
                for sem in yost:
                    sp.wait_ge(sem, 32 * PAIRS)

            @block.gpsimd
            def _(pool):
                def step(g, i, b):
                    c = 1 - b
                    if there(g):
                        landed(pool, lg, g, i, b, 2)
                        free2(pool, s["mT"], g)
                        nc.gpsimd.tensor_tensor(gx[b][:], gf[b][:], x1[b][:], ALU.add).then_inc(s["gx"], 1)
                    if there(g - 2):
                        ran(pool, s["za"], g - 2)
                        free2(pool, s["nn1"], g - 2)
                        pool.sem_inc(s["ppace"], 1)
                        nc.gpsimd.tensor_scalar(r1[b][:], za[b][:], 0.0, None, ALU.max).then_inc(s["r1"], 1)
                    if there(g):
                        ran(pool, s["gr"], g)
                        ran(pool, s["gx"], g)
                        free2(pool, s["o"], g)
                        nc.gpsimd.tensor_tensor(mT[b][:], gr[b][:], gx[b][:], ALU.add).then_inc(s["mT"], 1)
                    if there(g - 6):
                        ran(pool, s["yo"], g - 6)
                        if not (isinstance(g, int) and g - 6 < 2):
                            pool.wait_ge(yost[b], 32 * (i - 3))
                        pool.sem_inc(s["ppace"], 1)
                        nc.gpsimd.tensor_scalar(ye[b][:], yo[b][:], eps1[:, 0:1], None, ALU.mult).then_inc(s["ye"], 1)
                step_sweep(pool, step, 6)

            @block.tensor
            def _(pe):
                pe.wait_ge(s["w"], 80)
                pe.wait_ge(s["wh"], 1)

                def step(g, i, b):
                    c = 1 - b
                    if there(g):
                        ran(pe, s["sc"], g)
                        free1(pe, s["gr"], g)
                        turn4(tr_ps, sc[b]).then_inc(s["tr"], 1)
                    if there(g - 1):
                        ran(pe, s["nn0"], g - 1)
                        free1(pe, s["h1"], g - 3)
                        turn4(t01_ps, n0[c]).then_inc(s["tn0"], 1)
                    if there(g):
                        ran(pe, s["mT"], g)
                        free1(pe, s["xo"], g)
                        rows4(o_ps, mT[b], w["out"], "fc").then_inc(s["o"], 1)
                    if there(g - 1):
                        ran(pe, s["h0"], g - 1)
                        free1(pe, s["za"], g - 1)
                        rows4(z1_ps, h0[c], w["w1"], "l1c").then_inc(s["z1"], 1)
                    if there(g - 3):
                        ran(pe, s["nn1"], g - 3)
                        turn4(t01_ps, n1[c]).then_inc(s["tn1"], 1)
                        ran(pe, s["h1"], g - 3)
                        free1(pe, s["r2"], g - 3)
                        rows4(z2_ps, h1[c], w["w2"], "l1b2").then_inc(s["z2"], 1)
                    if there(g - 4):
                        ran(pe, s["nn2"], g - 4)
                        free1(pe, s["h3"], g - 5)
                        turn4(t23_ps, n2[b]).then_inc(s["tn2"], 1)
                        ran(pe, s["h2"], g - 4)
                        free1(pe, s["x2"], g - 4)
                        rows4(z3_ps, h2[b], w["w3"], "l1b3").then_inc(s["z3"], 1)
                    if there(g - 5):
                        ran(pe, s["nn3"], g - 5)
                        turn4(t23_ps, n3[c]).then_inc(s["tn3"], 1)
                        ran(pe, s["h3"], g - 5)
                        free1(pe, s["yo"], g - 5)
                        rows4(y_ps, h3[c], w["gin"]).then_inc(s["y"], 1)
                step_sweep(pe, step, 5)

            @block.scalar
            def _(act):
                def evac(k, dst, ps, g, fn, **kw):
                    ran(act, s[f"tn{k}"], g)
                    nc.scalar.activation(dst[:], ps[:], fn, **kw).then_inc(s[f"h{k}"], 1)

                def step(g, i, b):
                    c = 1 - b
                    if there(g - 4):
                        ran(act, s["z2"], g - 4)
                        free2(act, s["nn2"], g - 4)
                        nc.scalar.activation(r2[b][:], z2_ps[:], ACT.Relu).then_inc(s["r2"], 1)
                    if there(g):
                        ran(act, s["tr"], g)
                        free2(act, s["mT"], g)
                        nc.scalar.activation(gr[b][:], tr_ps[:], ACT.Relu, bias=bnbi[:, 3:4],
                                             scale=bnsc[:, 3:4]).then_inc(s["gr"], 1)
                    if there(g - 1):
                        norm_root(act, s, 0, T[0], g - 1, eps_ln)
                    if there(g - 6):
                        ran(act, s["y"], g - 6)
                        free2(act, s["ye"], g - 6)
                        if not (isinstance(g, int) and g - 6 < 2):
                            act.wait_ge(yost[b], 32 * (i - 3))
                        nc.scalar.copy(yo[b][:], y_ps[:]).then_inc(s["yo"], 1)
                    if there(g - 3):
                        norm_root(act, s, 1, T[1], g - 3, eps_ln)
                    if there(g - 1):
                        free2(act, s["z1"], g - 1)
                        evac(0, h0[c], t01_ps, g - 1, ACT.Relu)
                    if there(g - 4):
                        norm_root(act, s, 2, T[2], g - 4, eps_ln)
                    if there(g - 3):
                        free2(act, s["z2"], g - 3)
                        evac(1, h1[c], t01_ps, g - 3, ACT.Identity, bias=col("be1L1"), scale=col("g1L1"))
                    if there(g - 5):
                        norm_root(act, s, 3, T[3], g - 5, eps_ln)
                    if there(g - 4):
                        free2(act, s["tn2"], g - 4)
                        norm_apply_act(act, s, 2, T[2], n2[b], r2[b], g - 4)
                    if there(g - 5):
                        free2(act, s["tn3"], g - 5)
                        norm_apply_act(act, s, 3, T[3], n3[c], x2[c], g - 5)
                    if there(g - 4):
                        free2(act, s["z3"], g - 4)
                        evac(2, h2[b], t23_ps, g - 4, ACT.Identity, bias=col("be2L1"), scale=col("g2L1"))
                    if there(g - 5):
                        free2(act, s["y"], g - 5)
                        evac(3, h3[c], t23_ps, g - 5, ACT.Relu)
                step_sweep(act, step, 6)

            @block.vector
            def _(dve):
                dve.wait_ge(s["w"], 80)
                nc.vector.tensor_scalar(w["out"][:], w["out"][:], 0.5, None, ALU.mult).then_inc(s["wh"], 1)

                def step(g, i, b):
                    c = 1 - b
                    if there(g):
                        landed(dve, lt, g, i, b)
                        free2(dve, s["tr"], g)
                        for j in range(J):
                            js = slice(j * D, (j + 1) * D)
                            last = nc.vector.tensor_scalar(sc[b][:, js], ta[b][:, js],
                                                           dinv2[:, bass.ds(g * J + j, 1)], None, ALU.mult)
                        last.then_inc(s["sc"], 1)
                    if there(g - 1):
                        ran(dve, s["o"], g - 1)
                        dve.wait_ge(lx[c], 16 * (back(i, b, 1) + 1))
                        if not (isinstance(g, int) and g - 1 < 2):
                            dve.wait_ge(xost[c], 16 * back(i, b, 1))
                        nc.vector.tensor_tensor(xo[c][:], o_ps[:], xr[c][:], ALU.add).then_inc(s["xo"], 1)
                    if there(g - 2):
                        ran(dve, s["z1"], g - 2)
                        dve.wait_ge(la[b], 16 * i)
                        free2(dve, s["r1"], g - 2)
                        nc.vector.tensor_tensor(za[b][:], z1_ps[:], ag[b][:], ALU.add).then_inc(s["za"], 1)
                    if there(g - 5):
                        ran(dve, s["z3"], g - 5)
                        dve.wait_ge(lb[c], 16 * (back(i, b, 5) + 1))
                        free2(dve, s["nn3"], g - 5)
                        if not (isinstance(g, int) and g - 5 < 2):
                            dve.wait_ge(x2st[c], 16 * back(i, b, 5))
                        nc.vector.tensor_tensor(x2[c][:], z3_ps[:], xb[c][:], ALU.add).then_inc(s["x2"], 1)
                    if there(g - 1):
                        ran(dve, s["xo"], g - 1)
                        norm_stats(dve, s, 0, T[0], xo[c], g - 1)
                    if there(g - 4):
                        ran(dve, s["r2"], g - 4)
                        norm_stats(dve, s, 2, T[2], r2[b], g - 4)
                    if there(g - 1):
                        norm_vars(dve, s, 0, T[0], g - 1)
                    if there(g - 3):
                        ran(dve, s["r1"], g - 3)
                        norm_stats(dve, s, 1, T[1], r1[c], g - 3)
                    if there(g - 4):
                        norm_vars(dve, s, 2, T[2], g - 4)
                    if there(g - 1):
                        norm_recip(dve, s, 0, T[0], g - 1)
                    if there(g - 3):
                        norm_vars(dve, s, 1, T[1], g - 3)
                    if there(g - 1):
                        free2(dve, s["tn0"], g - 1)
                        norm_apply(dve, s, 0, T[0], n0[c], xo[c], g - 1)
                    if there(g - 5):
                        ran(dve, s["x2"], g - 5)
                        norm_stats(dve, s, 3, T[3], x2[c], g - 5)
                    if there(g - 3):
                        norm_recip(dve, s, 1, T[1], g - 3)
                    if there(g - 4):
                        norm_recip(dve, s, 2, T[2], g - 4)
                        norm_shift(dve, s, 2, T[2], g - 4)
                    if there(g - 5):
                        norm_vars(dve, s, 3, T[3], g - 5)
                    if there(g - 3):
                        free2(dve, s["tn1"], g - 3)
                        norm_apply(dve, s, 1, T[1], n1[c], r1[c], g - 3)
                    if there(g - 5):
                        norm_recip(dve, s, 3, T[3], g - 5)
                        norm_shift(dve, s, 3, T[3], g - 5)
                step_sweep(dve, step, 5)
        MIDDLE_SEMS = (["w", "wh", "sc", "tr", "gr", "gx", "mT", "o", "xo", "tn0", "h0", "z1", "za", "r1", "tn1", "h1",
                        "z2", "r2", "tn2", "h2", "z3", "x2", "tn3", "h3", "y", "yo", "ye", "shift2", "shift3", "pace", "ppace"]
                       + norm_sems(0) + norm_sems(1) + norm_sems(2) + norm_sems(3)
                       + st("lt", "lg", "lx", "la", "lb", "xost", "x2st", "yost"))

        def project_edge_attr(ctx, block, s):
            def sb(name, shape, dt=F32):
                return ctx.enter_context(nc.sbuf_tensor(f"{stage[0]}_{name}", shape, dt))
            w = sb("w_edge", [P, D])
            ea = [sb(f"ea{r}", [EP, D]) for r in range(RING)]
            mix = [sb(f"mix{r}", [EP, EP]) for r in range(RING)]
            mixx = [sb(f"mixx{h}", [EP, EP]) for h in range(RING // 2)]
            sumT = [sb(f"sumT{r}", [P, EP]) for r in range(RING)]
            ps = [ctx.enter_context(nc.psum_tensor(f"{stage[0]}_ps{r}", [P, 512], F32)) for r in range(RING)]
            attr = t["edge_attr_128"].rearrange("(p c) d -> p c d", p=EP)

            @block.sync
            def _(sp):
                sp.dma_start(w[:], t["L1_gnn_W1"][D:2 * D, :]).then_inc(s["w"], 16)

                def body(i):
                    for r in range(RING):
                        if not first_step(i):
                            sp.wait_ge(s["sum"], RING * i + r + 1 - RING)
                        sp.dma_start(ea[r][:], attr[:, bass.ds(RING * i + r, 1), :].rearrange("p a f -> p (a f)")
                                     ).then_inc(s[f"got{r}"], 16)
                sweep(sp, EITER, body)

            @block.vector
            def _(dve):
                def body(i):
                    for r in range(RING):
                        if not first_step(i):
                            dve.wait_ge(s["sum"], RING * i + r + 1 - RING)
                        if r % 2 == 0:
                            nc.vector.tensor_copy(
                                mixx[r // 2][:], cross[:, bass.ds(RING // 2 * i + r // 2, 1), :].rearrange("p a f -> p (a f)"))
                        nc.vector.tensor_copy(mix[r][:], same[:, bass.ds(RING * i + r, 1), :].rearrange("p a f -> p (a f)")
                                              ).then_inc(s["mix"], 1)
                sweep(dve, EITER, body)

            @block.tensor
            def _(pe):
                pe.wait_ge(s["w"], 16)

                def body(i):
                    for r in range(RING):
                        pe.wait_ge(s["mix"], RING * i + r + 1)
                        pe.wait_ge(s[f"got{r}"], 16 * (i + 1))
                        if not first_step(i):
                            pe.wait_ge(s["out"], RING * i + r + 1 - RING)
                        if r % 2 == 1:
                            nc.tensor.matmul(ps[r - 1][:, 0:EP], ea[r - 1][:], mix[r - 1][:], start=True, stop=False)
                            nc.tensor.matmul(ps[r - 1][:, 0:EP], ea[r][:], mixx[r // 2][:], start=False, stop=True
                                             ).then_inc(s["sum"], 1)
                            nc.tensor.matmul(ps[r][:, 0:EP], ea[r][:], mix[r][:], start=True, stop=True).then_inc(s["sum"], 1)
                    for r in range(RING):
                        pe.wait_ge(s["sumT"], RING * i + r + 1)
                        nc.tensor.matmul(ps[r][0:EP, 128:128 + D], sumT[r][:], w[:], start=True, stop=True).then_inc(s["mm"], 1)
                sweep(pe, EITER, body)

            @block.scalar
            def _(act):
                def body(i):
                    for r in range(RING):
                        act.wait_ge(s["sum"], RING * i + r + 1)
                        if not first_step(i):
                            act.wait_ge(s["mm"], RING * i + r + 1 - RING)
                        nc.scalar.copy(sumT[r][:], ps[r][:, 0:EP]).then_inc(s["sumT"], 1)
                    for r in range(RING):
                        act.wait_ge(s["mm"], RING * i + r + 1)
                        nc.scalar.copy(added[:, bass.ds(RING * i + r, 1), :].rearrange("p a f -> p (a f)"),
                                       ps[r][0:EP, 128:128 + D]).then_inc(s["out"], 1)
                sweep(act, EITER, body)
        ATTR_SEMS = ["w", "sum", "mix", "sumT", "mm", "out"] + [f"got{r}" for r in range(RING)]

        def aggregate():
            def emit(ctx, block, s):
                def sb(name, shape, dt=F32):
                    return ctx.enter_context(nc.sbuf_tensor(f"{stage[0]}_{name}", shape, dt))
                Q = edge_tiles(ctx, sb)

                def fours(eng, part):
                    part(0)
                    with eng.Fori(1, FOURS) as i:
                        part(i)

                @block.gpsimd
                def _(pool):
                    edges_on_pool(pool, s, Q, table[0], table[1])

                @block.vector
                def _(dve):
                    fours(dve, edges_on_dve(dve, s, Q, edge_w))

                @block.tensor
                def _(pe):
                    fours(pe, edges_on_pe(pe, s, Q))

                @block.scalar
                def _(act):
                    fours(act, edges_on_act(act, s, Q))
            return EDGE_SEMS, emit

        def gcn(layer):
            def emit(ctx, block, s):
                def sb(name, shape, dt=F32):
                    return ctx.enter_context(nc.sbuf_tensor(f"{stage[0]}_{name}", shape, dt))

                def pair(name):
                    return [sb(f"{name}{b}", [P, GROUP]) for b in SLOTS]
                w = weight_tiles(ctx, ["conv"])
                ta, gf, sc, gr, gT, yo = (pair(n) for n in ("ta", "gf", "sc", "gr", "gT", "yo"))
                A, B = ([ctx.enter_context(nc.psum_tensor(f"{stage[0]}_{n}{b}", [P, GROUP], F32)) for b in SLOTS] for n in "AB")

                @block.sync
                def _(sp):
                    sp.dma_start(w["conv"][:], t["L0_gnn_conv_w"][layer + 1]).then_inc(s["w"], 16)

                    def loads(i):
                        for b in SLOTS:
                            again(sp, s["sc"], i, b)
                            sp.dma_start(ta[b][:], at(grouped(table[1]), 2 * i + b)).then_inc(s[f"lt{b}"], 16)
                            again(sp, s["gT"], i, b)
                            sp.dma_start(gf[b][:], at(g_first, 2 * i + b)).then_inc(s[f"lg{b}"], 16)

                    def stores(i):
                        for b in SLOTS:
                            sp.wait_ge(s["yo"], nth(i, b))
                            sp.dma_start(at(grouped(table[0]), 2 * i + b), yo[b][:]).then_inc(s[f"yost{b}"], 16)
                            sp.dma_start(at(grouped(table[1]), 2 * i + b), yo[b][:]).then_inc(s[f"yost{b}"], 16)
                    load_and_store(sp, loads, stores)
                    for b in SLOTS:
                        sp.wait_ge(s[f"yost{b}"], 32 * PAIRS)

                @block.vector
                def _(dve):
                    def body(i):
                        for b in SLOTS:
                            dve.wait_ge(s[f"lt{b}"], 16 * (i + 1))
                            again(dve, s["tr"], i, b)
                            for j in range(J):
                                js = slice(j * D, (j + 1) * D)
                                last = nc.vector.tensor_scalar(sc[b][:, js], ta[b][:, js],
                                                               dinv2[:, bass.ds((2 * i + b) * J + j, 1)], None, ALU.mult)
                            last.then_inc(s["sc"], 1)
                    sweep(dve, PAIRS, body)

                @block.gpsimd
                def _(pool):
                    def body(i):
                        for b in SLOTS:
                            pool.wait_ge(s["gr"], nth(i, b))
                            pool.wait_ge(s[f"lg{b}"], 16 * (i + 1))
                            again(pool, s["y"], i, b)
                            nc.gpsimd.tensor_tensor(gT[b][:], gr[b][:], gf[b][:], ALU.add).then_inc(s["gT"], 1)
                    sweep(pool, PAIRS, body)

                @block.scalar
                def _(act):
                    def body(i):
                        for b in SLOTS:
                            act.wait_ge(s["tr"], nth(i, b))
                            again(act, s["gT"], i, b)
                            nc.scalar.activation(gr[b][:], A[b][:], ACT.Relu, bias=bnbi[:, layer + 1:layer + 2],
                                                 scale=bnsc[:, layer + 1:layer + 2]).then_inc(s["gr"], 1)
                        for b in SLOTS:
                            act.wait_ge(s["y"], nth(i, b))
                            if not first_step(i):
                                act.wait_ge(s[f"yost{b}"], 32 * i)
                            nc.scalar.copy(yo[b][:], B[b][:]).then_inc(s["yo"], 1)
                    sweep(act, PAIRS, body)

                @block.tensor
                def _(pe):
                    pe.wait_ge(s["w"], 16)

                    def body(i):
                        for b in SLOTS:
                            pe.wait_ge(s["sc"], nth(i, b))
                            again(pe, s["gr"], i, b)
                            turn4(A[b], sc[b]).then_inc(s["tr"], 1)
                        for b in SLOTS:
                            pe.wait_ge(s["gT"], nth(i, b))
                            again(pe, s["yo"], i, b)
                            rows4(B[b], gT[b], w["conv"]).then_inc(s["y"], 1)
                    sweep(pe, PAIRS, body)
            return ["w", "sc", "tr", "gr", "gT", "y", "yo"] + st("lt", "lg", "yost"), emit

        bnmv = keep("bnmv", [P, 2])
        bnsd = keep("bnsd", [P, 1])
        gsc = keep("gsc", [P, 1])
        gbi = keep("gbi", [P, 1])
        gtmp = keep("gtmp", [P, 1])

        def batch_stats(dve, i, b, src):
            rows = TAILP if is_tail(i, b) else P
            if rows == P:
                return nc.vector.bn_stats(bnstat[:, bass.ds(2 * i + b, 1), :].rearrange("p a f -> p (a f)"), src[:])
            for j in range(J):
                last = nc.vector.bn_stats(bnstat[:, G - 1 + j, :], src[:, j * D:j * D + rows])
            return last

        def gin_turn(layer):
            def emit(ctx, block, s):
                def sb(name, shape, dt=F32):
                    return ctx.enter_context(nc.sbuf_tensor(f"{stage[0]}_{name}", shape, dt))
                ta = [sb(f"ta{b}", [P, GROUP]) for b in SLOTS]
                zT = [sb(f"zT{b}", [P, GROUP]) for b in SLOTS]
                A = [ctx.enter_context(nc.psum_tensor(f"{stage[0]}_A{b}", [P, GROUP], F32)) for b in SLOTS]

                @block.sync
                def _(sp):
                    def loads(i):
                        for b in SLOTS:
                            again(sp, s["tr"], i, b)
                            sp.dma_start(ta[b][:], at(grouped(table[1]), 2 * i + b)).then_inc(s[f"lt{b}"], 16)

                    def stores(i):
                        for b in SLOTS:
                            sp.wait_ge(s["zT"], nth(i, b))
                            sp.dma_start(at(cur[0], 2 * i + b), zT[b][:]).then_inc(s[f"zst{b}"], 16)
                    load_and_store(sp, loads, stores)
                    for b in SLOTS:
                        sp.wait_ge(s[f"zst{b}"], 16 * PAIRS)

                @block.tensor
                def _(pe):
                    def body(i):
                        for b in SLOTS:
                            pe.wait_ge(s[f"lt{b}"], 16 * (i + 1))
                            again(pe, s["zT"], i, b)
                            turn4(A[b], ta[b]).then_inc(s["tr"], 1)
                    sweep(pe, PAIRS, body)

                @block.scalar
                def _(act):
                    def body(i):
                        for b in SLOTS:
                            act.wait_ge(s["tr"], nth(i, b))
                            again(act, s["bs"], i, b)
                            if not first_step(i):
                                act.wait_ge(s[f"zst{b}"], 16 * i)
                            nc.scalar.activation(zT[b][:], A[b][:], ACT.Identity, bias=col(f"b1_{layer}")).then_inc(s["zT"], 1)
                    sweep(act, PAIRS, body)
                    batch_root(act, s)

                @block.vector
                def _(dve):
                    def body(i):
                        for b in SLOTS:
                            dve.wait_ge(s["zT"], nth(i, b))
                            batch_stats(dve, i, b, zT[b]).then_inc(s["bs"], 1)
                    sweep(dve, PAIRS, body)
                    batch_scale(dve, s, col(f"g1_{layer}"), col(f"bt1_{layer}"))
            return ["tr", "zT", "bs", "dv", "bvar", "bstd"] + st("lt", "zst"), emit

        def batch_root(act, s):
            act.wait_ge(s["bvar"], 1)
            nc.scalar.activation(bnsd[:], bnmv[:, 1:2], ACT.Sqrt, bias=eps_ln).then_inc(s["bstd"], 1)

        def batch_scale(dve, s, g, b):
            dve.wait_ge(s["bs"], G)
            nc.vector.bn_aggr(bnmv[:], bnstat[:, 0:G - 1 + J, :].rearrange("p a f -> p (a f)")).then_inc(s["bvar"], 1)
            dve.wait_ge(s["bstd"], 1)
            nc.vector.reciprocal(gtmp[:], bnsd[:]).then_inc(s["dv"], 1)
            dve.wait_ge(s["dv"], 1)
            nc.vector.tensor_tensor(gsc[:], gtmp[:], g, ALU.mult).then_inc(s["dv"], 1)
            dve.wait_ge(s["dv"], 2)
            nc.vector.tensor_tensor(gtmp[:], bnmv[:, 0:1], gsc[:], ALU.mult).then_inc(s["dv"], 1)
            dve.wait_ge(s["dv"], 3)
            nc.vector.tensor_tensor(gbi[:], b, gtmp[:], ALU.subtract)

        def gin_middle(layer):
            def emit(ctx, block, s):
                def sb(name, shape, dt=F32):
                    return ctx.enter_context(nc.sbuf_tensor(f"{stage[0]}_{name}", shape, dt))

                def pair(name):
                    return [sb(f"{name}{b}", [P, GROUP]) for b in SLOTS]
                w = weight_tiles(ctx, ["w2"])
                zT, tT, uT = pair("zT"), pair("tT"), pair("uT")
                A = [ctx.enter_context(nc.psum_tensor(f"{stage[0]}_A{b}", [P, GROUP], F32)) for b in SLOTS]

                @block.sync
                def _(sp):
                    sp.dma_start(w["w2"][:], t["L2_gnn_W2"][layer]).then_inc(s["w"], 16)

                    def loads(i):
                        for b in SLOTS:
                            again(sp, s["tT"], i, b)
                            sp.dma_start(zT[b][:], at(cur[0], 2 * i + b)).then_inc(s[f"lt{b}"], 16)

                    def stores(i):
                        for b in SLOTS:
                            sp.wait_ge(s["uT"], nth(i, b))
                            sp.dma_start(at(cur[1], 2 * i + b), uT[b][:]).then_inc(s[f"ust{b}"], 16)
                    load_and_store(sp, loads, stores)
                    for b in SLOTS:
                        sp.wait_ge(s[f"ust{b}"], 16 * PAIRS)

                @block.tensor
                def _(pe):
                    pe.wait_ge(s["w"], 16)

                    def body(i):
                        for b in SLOTS:
                            pe.wait_ge(s["tT"], nth(i, b))
                            again(pe, s["uT"], i, b)
                            nc.tensor.matmul(A[b][:], w["w2"][:], tT[b][:], start=True, stop=True).then_inc(s["mm"], 1)
                    sweep(pe, PAIRS, body)

                @block.scalar
                def _(act):
                    def body(i):
                        for b in SLOTS:
                            act.wait_ge(s[f"lt{b}"], 16 * (i + 1))
                            again(act, s["mm"], i, b)
                            nc.scalar.activation(tT[b][:], zT[b][:], ACT.Relu, bias=gsc_bias[0], scale=gsc_bias[1]
                                                 ).then_inc(s["tT"], 1)
                        for b in SLOTS:
                            act.wait_ge(s["mm"], nth(i, b))
                            again(act, s["bs"], i, b)
                            if not first_step(i):
                                act.wait_ge(s[f"ust{b}"], 16 * i)
                            nc.scalar.activation(uT[b][:], A[b][:], ACT.Relu, bias=col(f"b2_{layer}")).then_inc(s["uT"], 1)
                    sweep(act, PAIRS, body)
                    batch_root(act, s)

                @block.vector
                def _(dve):
                    def body(i):
                        for b in SLOTS:
                            dve.wait_ge(s["uT"], nth(i, b))
                            batch_stats(dve, i, b, uT[b]).then_inc(s["bs"], 1)
                    sweep(dve, PAIRS, body)
                    dve.wait_ge(s["tT"], G)
                    batch_scale(dve, s, col(f"g2_{layer}"), col(f"bt2_{layer}"))
            return ["w", "tT", "uT", "mm", "bs", "dv", "bvar", "bstd"] + st("lt", "ust"), emit
        gsc_bias = (gbi[:, 0:1], gsc[:, 0:1])

        def gin_next(layer):
            def emit(ctx, block, s):
                def sb(name, shape, dt=F32):
                    return ctx.enter_context(nc.sbuf_tensor(f"{stage[0]}_{name}", shape, dt))

                def pair(name):
                    return [sb(f"{name}{b}", [P, GROUP]) for b in SLOTS]
                w = weight_tiles(ctx, ["w1"])
                uT, hT, yo, ye = pair("uT"), pair("hT"), pair("yo"), pair("ye")
                A = [ctx.enter_context(nc.psum_tensor(f"{stage[0]}_A{b}", [P, GROUP], F32)) for b in SLOTS]

                @block.sync
                def _(sp):
                    sp.dma_start(w["w1"][:], t["L2_gnn_W1"][layer + 1]).then_inc(s["w"], 16)

                    def loads(i):
                        for b in SLOTS:
                            again(sp, s["hT"], i, b)
                            sp.dma_start(uT[b][:], at(cur[1], 2 * i + b)).then_inc(s[f"lt{b}"], 16)

                    def stores(i):
                        for b in SLOTS:
                            sp.wait_ge(s["yo"], nth(i, b))
                            sp.dma_start(at(grouped(table[0]), 2 * i + b), yo[b][:]).then_inc(s[f"yost{b}"], 16)
                            sp.wait_ge(s["ye"], nth(i, b))
                            sp.dma_start(at(grouped(table[1]), 2 * i + b), ye[b][:]).then_inc(s[f"yest{b}"], 16)
                    load_and_store(sp, loads, stores)
                    for b in SLOTS:
                        sp.wait_ge(s[f"yost{b}"], 16 * PAIRS)
                        sp.wait_ge(s[f"yest{b}"], 16 * PAIRS)

                @block.tensor
                def _(pe):
                    pe.wait_ge(s["w"], 16)

                    def body(i):
                        for b in SLOTS:
                            pe.wait_ge(s["hT"], nth(i, b))
                            again(pe, s["yo"], i, b)
                            rows4(A[b], hT[b], w["w1"]).then_inc(s["mm"], 1)
                    sweep(pe, PAIRS, body)

                @block.scalar
                def _(act):
                    def body(i):
                        for b in SLOTS:
                            act.wait_ge(s[f"lt{b}"], 16 * (i + 1))
                            again(act, s["mm"], i, b)
                            nc.scalar.activation(hT[b][:], uT[b][:], ACT.Relu, bias=gsc_bias[0], scale=gsc_bias[1]
                                                 ).then_inc(s["hT"], 1)
                        for b in SLOTS:
                            act.wait_ge(s["mm"], nth(i, b))
                            again(act, s["ye"], i, b)
                            if not first_step(i):
                                act.wait_ge(s[f"yost{b}"], 16 * i)
                            nc.scalar.copy(yo[b][:], A[b][:]).then_inc(s["yo"], 1)
                    sweep(act, PAIRS, body)

                @block.vector
                def _(dve):
                    def body(i):
                        for b in SLOTS:
                            dve.wait_ge(s["yo"], nth(i, b))
                            if not first_step(i):
                                dve.wait_ge(s[f"yest{b}"], 16 * i)
                            nc.vector.tensor_scalar(ye[b][:], yo[b][:], eps1[:, layer + 1:layer + 2], None, ALU.mult
                                                    ).then_inc(s["ye"], 1)
                    sweep(dve, PAIRS, body)
            return ["w", "hT", "mm", "yo", "ye"] + st("lt", "yost", "yest"), emit

        def gin_last(ctx, block, s):
            def sb(name, shape, dt=F32):
                return ctx.enter_context(nc.sbuf_tensor(f"{stage[0]}_{name}", shape, dt))
            w = weight_tiles(ctx, ["w1"])
            uT, hT, xr, xo, nn, fT, yo = (pair_of(sb, n) for n in ("uT", "hT", "xr", "xo", "nn", "fT", "yo"))
            T1 = norm1_tiles(sb, "n1")
            th_ps, tn_ps, y_ps = ([ctx.enter_context(nc.psum_tensor(f"{stage[0]}_{n}{b}", [P, GROUP], F32)) for b in SLOTS]
                                  for n in ("th", "tn", "y"))
            lt, lx, xost, yost = ([s[f"{n}{b}"] for b in SLOTS] for n in ("lt", "lx", "xost", "yost"))

            @block.sync
            def _(sp):
                sp.dma_start(w["w1"][:], t["L3_gnn_W1"]).then_inc(s["w"], 16)

                def step(g, i, b):
                    c = 1 - b
                    if there(g):
                        free2(sp, s["hT"], g)
                        sp.dma_start(uT[b][:], at(cur[1], g)).then_inc(lt[b], 16)
                        free2(sp, s["xo"], g)
                        sp.dma_start(xr[b][:], at(grouped(xres[1]), g)).then_inc(lx[b], 16)
                    if there(g - 1):
                        ran(sp, s["xo"], g - 1)
                        sp.dma_start(at(grouped(xres[0]), g - 1), xo[c][:]).then_inc(xost[c], 16)
                    if there(g - 4):
                        ran(sp, s["yo"], g - 4)
                        sp.dma_start(at(grouped(table[0]), g - 4), yo[b][:]).then_inc(yost[b], 16)
                        sp.dma_start(at(grouped(table[1]), g - 4), yo[b][:]).then_inc(yost[b], 16)
                step_sweep(sp, step, 4)
                for sem in xost:
                    sp.wait_ge(sem, 16 * PAIRS)
                for sem in yost:
                    sp.wait_ge(sem, 32 * PAIRS)

            @block.tensor
            def _(pe):
                pe.wait_ge(s["w"], 16)

                def step(g, i, b):
                    c = 1 - b
                    if there(g):
                        ran(pe, s["hT"], g)
                        free2(pe, s["xo"], g)
                        turn4(th_ps[b], hT[b]).then_inc(s["th"], 1)
                    if there(g - 2):
                        ran(pe, s["nn1"], g - 2)
                        free2(pe, s["fT"], g - 2)
                        turn4(tn_ps[b], nn[b]).then_inc(s["tn"], 1)
                    if there(g - 3):
                        ran(pe, s["fT"], g - 3)
                        free2(pe, s["yo"], g - 3)
                        rows4(y_ps[c], fT[c], w["w1"]).then_inc(s["y"], 1)
                step_sweep(pe, step, 3)

            @block.scalar
            def _(act):
                def step(g, i, b):
                    c = 1 - b
                    if there(g):
                        landed(act, lt, g, i, b)
                        free2(act, s["th"], g)
                        nc.scalar.activation(hT[b][:], uT[b][:], ACT.Relu, bias=gsc_bias[0], scale=gsc_bias[1]
                                             ).then_inc(s["hT"], 1)
                    if there(g - 1):
                        norm_root(act, s, 1, T1, g - 1, eps_ln)
                    if there(g - 2):
                        ran(act, s["tn"], g - 2)
                        free2(act, s["y"], g - 2)
                        nc.scalar.activation(fT[b][:], tn_ps[b][:], ACT.Relu).then_inc(s["fT"], 1)
                    if there(g - 3):
                        ran(act, s["y"], g - 3)
                        if not (isinstance(g, int) and g - 3 < 2):
                            act.wait_ge(yost[c], 32 * (i - 2 + b))
                        nc.scalar.copy(yo[c][:], y_ps[c][:]).then_inc(s["yo"], 1)
                step_sweep(act, step, 3)

            @block.vector
            def _(dve):
                def step(g, i, b):
                    c = 1 - b
                    if there(g):
                        ran(dve, s["th"], g)
                        landed(dve, lx, g, i, b)
                        stored(dve, xost, g, i, b)
                        nc.vector.tensor_tensor(xo[b][:], th_ps[b][:], xr[b][:], ALU.add).then_inc(s["xo"], 1)
                    if there(g - 1):
                        norm_recip(dve, s, 1, T1, g - 1)
                        free2(dve, s["tn"], g - 1)
                        norm_apply(dve, s, 1, T1, nn[c], xo[c], g - 1)
                    if there(g):
                        ran(dve, s["xo"], g)
                        norm_stats(dve, s, 1, T1, xo[b], g)
                        norm_vars(dve, s, 1, T1, g)
                step_sweep(dve, step, 1)
        GIN_LAST_SEMS = (["w", "hT", "xo", "yo", "th", "tn", "fT", "y", "pace"] + norm_sems(1)
                         + st("lt", "lx", "xost", "yost"))

        def fourth(ctx, block, s):
            def sb(name, shape, dt=F32):
                return ctx.enter_context(nc.sbuf_tensor(f"{stage[0]}_{name}", shape, dt))

            def pair(name):
                return [sb(f"{name}{b}", [P, GROUP]) for b in SLOTS]
            w = weight_tiles(ctx, ["w2"])
            ta, xr, hT, xo = (pair(n) for n in ("ta", "xr", "hT", "xo"))
            A, B = ([ctx.enter_context(nc.psum_tensor(f"{stage[0]}_{n}{b}", [P, GROUP], F32)) for b in SLOTS] for n in "AB")

            @block.sync
            def _(sp):
                sp.dma_start(w["w2"][:], t["L3_gnn_W2"]).then_inc(s["w"], 16)

                def loads(i):
                    for b in SLOTS:
                        again(sp, s["tr"], i, b)
                        sp.dma_start(ta[b][:], at(grouped(table[1]), 2 * i + b)).then_inc(s[f"lt{b}"], 16)
                        again(sp, s["xo"], i, b)
                        sp.dma_start(xr[b][:], at(grouped(xres[0]), 2 * i + b)).then_inc(s[f"lx{b}"], 16)

                def stores(i):
                    for b in SLOTS:
                        sp.wait_ge(s["xo"], nth(i, b))
                        if is_tail(i, b):
                            sp.dma_start(out_tail, xo[b][0:TAILP, :]).then_inc(s[f"xost{b}"], 16)
                        else:
                            sp.dma_start(at(out_groups, 2 * i + b), xo[b][:]).then_inc(s[f"xost{b}"], 16)
                load_and_store(sp, loads, stores)
                for b in SLOTS:
                    sp.wait_ge(s[f"xost{b}"], 16 * PAIRS)

            @block.tensor
            def _(pe):
                pe.wait_ge(s["w"], 16)

                def body(i):
                    for b in SLOTS:
                        pe.wait_ge(s[f"lt{b}"], 16 * (i + 1))
                        again(pe, s["hT"], i, b)
                        turn4(A[b], ta[b]).then_inc(s["tr"], 1)
                    for b in SLOTS:
                        pe.wait_ge(s["hT"], nth(i, b))
                        again(pe, s["xo"], i, b)
                        rows4(B[b], hT[b], w["w2"], "l3b2").then_inc(s["y"], 1)
                sweep(pe, PAIRS, body)

            @block.scalar
            def _(act):
                def body(i):
                    for b in SLOTS:
                        act.wait_ge(s["tr"], nth(i, b))
                        again(act, s["y"], i, b)
                        nc.scalar.activation(hT[b][:], A[b][:], ACT.Relu, bias=col("b1L3")).then_inc(s["hT"], 1)
                sweep(act, PAIRS, body)

            @block.vector
            def _(dve):
                def body(i):
                    for b in SLOTS:
                        dve.wait_ge(s["y"], nth(i, b))
                        dve.wait_ge(s[f"lx{b}"], 16 * (i + 1))
                        if not first_step(i):
                            dve.wait_ge(s[f"xost{b}"], 16 * i)
                        nc.vector.tensor_tensor(xo[b][:], B[b][:], xr[b][:], ALU.add).then_inc(s["xo"], 1)
                sweep(dve, PAIRS, body)
        FOURTH_SEMS = ["w", "tr", "hT", "y", "xo"] + st("lt", "lx", "xost")

        with nc.sbuf_tensor("added", [EP, TILES, D], F32) as added:
            run_block("attr", ATTR_SEMS, project_edge_attr)
            run_block("first", FIRST_SEMS, pass_first, FIRST_COUNTS)
        run_block("att0", *attention(0), EDGE_COUNTS)
        run_block("gcn0", *gcn(0))
        run_block("att1a", *attention(1, (0, -(-PAIRS // 2))), EDGE_COUNTS)
        run_block("gcn1", *gcn(1))
        run_block("att1b", *attention(1, (-(-PAIRS // 2), PAIRS)), EDGE_COUNTS)
        run_block("middle", MIDDLE_SEMS, middle)
        for layer in range(3):
            run_block(f"gin{layer}e", *aggregate(), EDGE_COUNTS)
            run_block(f"gin{layer}t", *gin_turn(layer))
            run_block(f"gin{layer}m", *gin_middle(layer))
            if layer < 2:
                run_block(f"gin{layer}n", *gin_next(layer))
        run_block("ginlast", GIN_LAST_SEMS, gin_last)
        run_block("fourth", *aggregate(), EDGE_COUNTS)
        run_block("out", FOURTH_SEMS, fourth)


_INS = ["x", "src", "dst", "edge_attr_128", "edge_weight",
        "L0_gnn_t_fc_w", "L0_gnn_t_fc_b", "L0_gnn_t_ln_g", "L0_gnn_t_ln_b", "L0_gnn_qkv_w",
        "L0_gnn_g_fc_w", "L0_gnn_g_fc_b", "L0_gnn_bn_g", "L0_gnn_bn_b", "L0_gnn_conv_w", "L0_gnn_conv_b",
        "L0_gnn_fc_w", "L0_gnn_fc_b",
        "L1_gnn_u", "L1_gnn_W1", "L1_gnn_b1", "L1_gnn_g1", "L1_gnn_be1", "L1_gnn_W2", "L1_gnn_b2",
        "L1_gnn_g2", "L1_gnn_be2", "L1_gnn_W3", "L1_gnn_b3",
        "L2_gnn_eps_list", "L2_gnn_W1", "L2_gnn_b1", "L2_gnn_g1", "L2_gnn_bt1", "L2_gnn_W2", "L2_gnn_b2",
        "L2_gnn_g2", "L2_gnn_bt2",
        "L3_gnn_W1", "L3_gnn_b1", "L3_gnn_W2", "L3_gnn_b2"]


def kernel(**inputs):
    import numpy as _np
    import concourse.bacc as _bacc
    from concourse import mybir as _mybir
    from concourse.bass_utils import run_bass_kernel_spmd as _run

    nc = _bacc.Bacc("TRN2", target_bir_lowering=False, num_devices=1)
    arrays, args = {}, {}
    for name in _INS:
        a = _np.ascontiguousarray(inputs[name])
        arrays[f"in_{name}_dram"] = a
        args[name] = nc.dram_tensor(f"in_{name}_dram", a.shape, _mybir.dt.from_np(a.dtype), kind="ExternalInput").ap()
    shape = inputs["x"].shape
    out = nc.dram_tensor("out_0_dram", shape, _mybir.dt.float32, kind="ExternalOutput").ap()
    build(nc, args, out)
    r = _run(nc, [arrays], core_ids=[0])
    return r.results[0]["out_0_dram"]
```

```python
from contextlib import ExitStack

import concourse.bass as bass
from concourse import mybir

F32 = mybir.dt.float32
BF16 = mybir.dt.bfloat16
I32 = mybir.dt.int32
ALU = mybir.AluOpType
ACT = mybir.ActivationFunctionType
AX = mybir.AxisListType

D = 128
P = 128
J = 4
GROUP = P * J
EP = 125
RING = 4
LN_EPS = 1e-5
GUARD = 1e6


class Chain:

    def __init__(self, eng, sem):
        self.eng, self.sem, self.n = eng, sem, 0

    def link(self, instruction):
        instruction.then_inc(self.sem, 1)
        self.n += 1
        self.eng.wait_ge(self.sem, self.n)


def sweep(eng, steps, body):
    body(0)
    if steps > 2:
        with eng.Fori(1, steps - 1) as i:
            body(i)
    body(steps - 1)


def build(nc, t, out):
    x_in = t["x"]
    N = x_in.shape[0]
    E = t["src"].shape[0]
    G = -(-N // GROUP)
    PAIRS = G // 2
    TAILP = (N - GROUP * (G - 1)) // J
    TILES = E // EP
    NPAD = G * GROUP
    assert G % 2 == 0 and TAILP * J == N - GROUP * (G - 1) and TILES * EP == E and TILES % RING == 0
    EITER = TILES // RING
    FOURS = TILES // 4
    assert TILES % 4 == 0

    def dram(name, shape):
        return nc.dram_tensor(name, shape, F32).ap()

    def grouped(buf):
        return buf[0:NPAD, :].rearrange("(g p j) d -> g p (j d)", p=P, j=J)

    full = (N // GROUP) * GROUP
    x_groups = x_in[0:full, :].rearrange("(g p j) d -> g p (j d)", p=P, j=J)
    x_tail = x_in[full:N, :].rearrange("(p j) d -> p (j d)", j=J)
    out_groups = out[0:full, :].rearrange("(g p j) d -> g p (j d)", p=P, j=J)
    out_tail = out[full:N, :].rearrange("(p j) d -> p (j d)", j=J)

    def at(view, g):
        return view[g, :, :] if isinstance(g, int) else view[bass.ds(g, 1), :, :].rearrange("a p f -> (a p) f")

    table = [dram(f"table{k}", [NPAD + P, D]) for k in range(2)]
    cur = [dram(f"cur{k}", [G, P, GROUP]) for k in range(2)]
    g_first = dram("g_first", [G, P, GROUP])
    xres = [dram(f"xres{k}", [NPAD, D]) for k in range(2)]
    degree = dram("degree", [NPAD + P, 1])
    attr_sum = dram("attr_sum", [NPAD + P, D])

    top = ExitStack()
    with top:
        def keep(name, shape, dt=F32):
            return top.enter_context(nc.sbuf_tensor(name, shape, dt))

        ident = keep("ident", [P, P])
        ones3 = keep("ones3", [3, P], BF16)
        onescol = keep("onescol", [P, 1])
        zrow = keep("zrow", [P, D])
        same = keep("same", [EP, TILES, EP], BF16)
        cross = keep("cross", [EP, TILES // 2, EP], BF16)
        src_i = keep("src_i", [EP, TILES], I32)
        dst_i = keep("dst_i", [EP, TILES], I32)
        put_i = keep("put_i", [EP, TILES], I32)
        gcn_coef = keep("gcn_coef", [EP, TILES])
        edge_w = keep("edge_w", [EP, TILES])
        dinv2 = keep("dinv2", [P, G * J])
        NCOL = 48
        cols = keep("cols", [P, NCOL])
        col_at = {}

        def col(name):
            if name not in col_at:
                col_at[name] = len(col_at)
                assert len(col_at) <= NCOL
            c = col_at[name]
            return cols[:, c:c + 1]
        BIASES = ["t_fc", "fc", "l1c", "l1b2", "l1b3", "l3b2"]
        bias3 = keep("bias3", [3, len(BIASES), GROUP], BF16)
        kvsum = keep("kvsum", [P, D + 1])
        bnstat = keep("bnstat", [P, (G + 1) * J, 6])

        def bias(name):
            return bias3[:, BIASES.index(name), :]

        stage = [""]
        pool_sems = {}
        base = {}

        def before_stage(k):
            return base.get(k, 0)

        def pool_dma_sem(k):
            if k not in pool_sems:
                pool_sems[k] = top.enter_context(nc.semaphore(k))
            return pool_sems[k]

        def run_block(name, sems, emit, sw_counts=None):
            stage[0] = name
            with ExitStack() as ctx:
                s = {k: pool_dma_sem(k) if k.startswith("sw_") else ctx.enter_context(nc.semaphore(f"{name}_{k}"))
                     for k in sems}
                with nc.Block() as block:
                    emit(ctx, block, s)
                nums = [v for k, v in s.items() if not k.startswith("sw_")]
                nc.all_engine_barrier()
                for k in sems:
                    if k.startswith("sw_"):
                        base[k] = base.get(k, 0) + sw_counts[k]
                for v in nums:
                    nc.gpsimd.sem_clear(v)
                nc.all_engine_barrier()

        COLS = {
            "bng0": t["L0_gnn_bn_g"][0], "bnb0": t["L0_gnn_bn_b"][0], "gfcb": t["L0_gnn_g_fc_b"],
            "b1L3": t["L3_gnn_b1"], "g1L1": t["L1_gnn_g1"], "be1L1": t["L1_gnn_be1"],
            "g2L1": t["L1_gnn_g2"], "be2L1": t["L1_gnn_be2"],
        }
        for k in range(3):
            COLS[f"lng{k}"] = t["L0_gnn_t_ln_g"][k]
            COLS[f"lnb{k}"] = t["L0_gnn_t_ln_b"][k]
            COLS[f"bng{k + 1}"] = t["L0_gnn_bn_g"][k + 1]
            COLS[f"bnb{k + 1}"] = t["L0_gnn_bn_b"][k + 1]
            COLS[f"cb{k}"] = t["L0_gnn_conv_b"][k]
            for n in ("b1", "b2", "g1", "bt1", "g2", "bt2"):
                COLS[f"{n}_{k}"] = t[f"L2_gnn_{n}"][k]
        for n in COLS:
            col(n)
        eps1 = keep("eps1", [P, 3])
        bnsc = keep("bnsc", [P, 4])
        bnbi = keep("bnbi", [P, 4])

        def prepare(ctx, block, s):
            def sb(name, shape, dt=F32):
                return ctx.enter_context(nc.sbuf_tensor(f"{stage[0]}_{name}", shape, dt))
            brow = sb("brow", [3, len(BIASES), D])
            rest = sb("rest", [3, len(BIASES), D])
            hi = sb("hi", [3, len(BIASES), D], BF16)
            mid = sb("mid", [3, len(BIASES), D], BF16)
            lo = sb("lo", [3, len(BIASES), D], BF16)
            pick = sb("pick", [3, len(BIASES), D])
            pick2 = sb("pick2", [3, len(BIASES), D])
            ucol = sb("ucol", [16, 1])
            u3 = sb("u3", [16, 3])
            w1c = sb("w1c", [16, D])
            ones = sb("ones", [P, (NPAD + P) // P])
            psc = ctx.enter_context(nc.psum_tensor(f"{stage[0]}_psc", [P, D], F32))

            @block.gpsimd
            def _(pool):
                nc.gpsimd.memset(ident[:], 0.0).then_inc(s["pz"], 1)
                pool.wait_ge(s["pz"], 1)
                nc.gpsimd.affine_select(out=ident[:], in_=ident[:], compare_op=ALU.not_equal, fill=1.0,
                                        base=0, pattern=[[-1, P]], channel_multiplier=1).then_inc(s["pi"], 1)

            @block.sync
            def _(sp):
                n = 0
                for name, v in COLS.items():
                    sp.dma_start(col(name), v.rearrange("(p a) -> p a", a=1)).then_inc(s["ld"], 16)
                    n += 1
                rows = {"t_fc": t["L0_gnn_t_fc_b"], "fc": t["L0_gnn_fc_b"], "l1c": t["L1_gnn_b1"],
                        "l1b2": t["L1_gnn_b2"], "l1b3": t["L1_gnn_b3"], "l3b2": t["L3_gnn_b2"]}
                for name, v in rows.items():
                    for k in range(3):
                        sp.dma_start(brow[k:k + 1, BIASES.index(name), :],
                                     v.rearrange("(a d) -> a d", a=1)).then_inc(s["ld"], 16)
                        n += 1
                sp.dma_start(ucol[:], t["L1_gnn_u"].rearrange("a d -> d a")).then_inc(s["ld"], 16)
                sp.dma_start(w1c[:], t["L1_gnn_W1"][2 * D:2 * D + 16, :]).then_inc(s["ld"], 16)
                sp.dma_start(eps1[:], t["L2_gnn_eps_list"].partition_broadcast(P)).then_inc(s["ld"], 16)
                sp.dma_start(src_i[:], t["src"].rearrange("(p c) -> p c", p=EP)).then_inc(s["ld"], 16)
                sp.dma_start(dst_i[:], t["dst"].rearrange("(p c) -> p c", p=EP)).then_inc(s["ld"], 16)
                sp.dma_start(edge_w[:], t["edge_weight"].rearrange("(p c) -> p c", p=EP)).then_inc(s["ld"], 16)
                assert n + 6 == len(COLS) + 3 * len(BIASES) + 6
                sp.wait_ge(s["set"], 1)
                for k in range(2):
                    sp.dma_start(table[k][NPAD:NPAD + P, :], zrow[:]).then_inc(s["st"], 16)
                sp.dma_start(degree.rearrange("(p c) a -> p (c a)", p=P), ones[:]).then_inc(s["st"], 16)
                sp.wait_ge(s["st"], 48)

            LOADS = 16 * (len(COLS) + 3 * len(BIASES) + 6)

            @block.tensor
            def _(pe):
                pe.wait_ge(s["u3"], 1)
                nc.tensor.matmul(psc[0:3, :], u3[:], w1c[:], start=True, stop=True).then_inc(s["mm"], 1)

            @block.vector
            def _(dve):
                link = Chain(dve, s["dv"]).link
                nc.vector.memset(zrow[:], 0.0)
                nc.vector.memset(ones[:], 1.0).then_inc(s["set"], 1)
                nc.vector.memset(onescol[:], 1.0)
                link(nc.vector.memset(ones3[:], 1.0))
                dve.wait_ge(s["ld"], LOADS)
                nc.vector.tensor_copy(u3[:], ucol[:, 0:1].to_broadcast([16, 3])).then_inc(s["u3"], 1)
                dve.wait_ge(s["mm"], 1)
                c = BIASES.index("l1c")
                link(nc.vector.tensor_tensor(brow[:, c, :], psc[0:3, :], brow[:, c, :], ALU.add))
                link(nc.vector.tensor_scalar(eps1[:], eps1[:], 1.0, None, ALU.add))
                link(nc.vector.tensor_copy(hi[:], brow[:]))
                link(nc.vector.tensor_tensor(rest[:], brow[:], hi[:], ALU.subtract))
                link(nc.vector.tensor_copy(mid[:], rest[:]))
                link(nc.vector.tensor_tensor(rest[:], rest[:], mid[:], ALU.subtract))
                link(nc.vector.tensor_copy(lo[:], rest[:]))
                dve.wait_ge(s["pi"], 1)
                link(nc.vector.tensor_scalar(pick[:], hi[:], ident[0:3, 0:1], None, ALU.mult))
                link(nc.vector.scalar_tensor_tensor(out=pick2[:], in0=mid[:], scalar=ident[0:3, 1:2], in1=pick[:],
                                                    op0=ALU.mult, op1=ALU.add))
                link(nc.vector.scalar_tensor_tensor(out=pick[:], in0=lo[:], scalar=ident[0:3, 2:3], in1=pick2[:],
                                                    op0=ALU.mult, op1=ALU.add))
                for j in range(J):
                    link(nc.vector.tensor_copy(bias3[:, :, j * D:(j + 1) * D], pick[:]))
                for k in range(4):
                    b = col("gfcb") if k == 0 else col(f"cb{k - 1}")
                    link(nc.vector.tensor_scalar(bnsc[:, k:k + 1], col(f"bng{k}"), (1.0 + 1e-5) ** -0.5, None, ALU.mult))
                    link(nc.vector.scalar_tensor_tensor(out=bnbi[:, k:k + 1], in0=b, scalar=bnsc[:, k:k + 1],
                                                        in1=col(f"bnb{k}"), op0=ALU.mult, op1=ALU.add))
        run_block("prep", ["pz", "pi", "ld", "set", "st", "u3", "mm", "dv"], prepare)

        dstf = keep("dstf", [EP, TILES])
        count = keep("count", [EP, TILES])
        before = keep("before", [EP, TILES])

        def match_edges(ctx, block, s):
            def sb(name, shape, dt=F32):
                return ctx.enter_context(nc.sbuf_tensor(f"{stage[0]}_{name}", shape, dt))
            lower = sb("lower", [EP, EP])
            ZW = 4 * GROUP
            zeros = sb("zeros", [P, ZW])
            spare = sb("spare", [EP, TILES])
            tmp = sb("tmp", [EP, TILES])
            late = sb("late", [EP, TILES])
            wide = [sb(f"wide{r}", [EP, EP]) for r in range(RING)]
            eq = [sb(f"eq{r}", [EP, EP]) for r in range(RING)]
            odd_even = [sb(f"odd_even{r}", [EP, EP]) for r in range(0, RING, 2)]
            even_odd = [sb(f"even_odd{r}", [EP, EP]) for r in range(0, RING, 2)]
            more_count = sb("more_count", [EP, TILES])
            more_before = sb("more_before", [EP, TILES])
            low = [sb(f"low{r}", [EP, EP]) for r in range(RING)]
            ps = [ctx.enter_context(nc.psum_tensor(f"{stage[0]}_ps{r}", [P, 512], F32)) for r in range(RING)]

            HALF = RING // 2

            @block.gpsimd
            def _(pool):
                nc.gpsimd.memset(lower[:], 1.0).then_inc(s["pc"], 1)
                pool.wait_ge(s["pc"], 1)
                nc.gpsimd.affine_select(out=lower[:], in_=lower[:], compare_op=ALU.is_gt, fill=0.0,
                                        base=0, pattern=[[-1, EP]], channel_multiplier=1).then_inc(s["pc"], 1)
                nc.gpsimd.iota(spare[:], [[0, TILES]], base=NPAD, channel_multiplier=1,
                               allow_small_or_imprecise_dtypes=True).then_inc(s["pc"], 1)

                def keep_matches(i):
                    for r in range(RING):
                        pool.wait_ge(s["eq"], RING * i + r + 1)
                        pool.sem_inc(s["pace"], 1)
                        nc.gpsimd.tensor_copy(same[:, bass.ds(RING * i + r, 1), :].rearrange("p a f -> p (a f)"), eq[r][:]
                                              ).then_inc(s["kept"], 1)
                    for h in range(HALF):
                        pool.wait_ge(s["eqx"], HALF * i + h + 1)
                        pool.sem_inc(s["pace"], 1)
                        nc.gpsimd.tensor_copy(cross[:, bass.ds(HALF * i + h, 1), :].rearrange("p a f -> p (a f)"),
                                              odd_even[h][:]).then_inc(s["kept"], 1)
                sweep(pool, EITER, keep_matches)

            @block.sync
            def _(sp):
                flat = attr_sum.rearrange("(p n) d -> p (n d)", p=P)
                n = 0
                for a in range(0, NPAD + P, ZW):
                    c = min(ZW, NPAD + P - a)
                    sp.wait_ge(s["zero"], 1)
                    sp.dma_start(flat[:, a:a + c], zeros[:, 0:c]).then_inc(s["zst"], 16)
                    n += 1
                sp.wait_ge(s["zst"], 16 * n)

            @block.tensor
            def _(pe):
                def body(i):
                    for r in range(RING):
                        pe.wait_ge(s["wide"], RING * i + r + 1)
                        if not (isinstance(i, int) and i == 0):
                            pe.wait_ge(s["eqx"], HALF * i + r // 2 + 1 - HALF)
                        nc.tensor.transpose(ps[r][0:EP, 0:EP], wide[r][:], ident[0:EP, 0:EP]).then_inc(s["tr"], 1)
                sweep(pe, EITER, body)

            @block.vector
            def _(dve):
                link = Chain(dve, s["dv"]).link
                nc.vector.memset(zeros[:], 0.0).then_inc(s["zero"], 1)
                nc.vector.memset(more_count[:], 0.0)
                nc.vector.memset(more_before[:], 0.0)
                link(nc.vector.tensor_copy(dstf[:], dst_i[:]))
                dve.wait_ge(s["pc"], 3)

                def body(i):
                    for r in range(RING):
                        t_ = RING * i + r
                        if not (isinstance(i, int) and i == 0):
                            dve.wait_ge(s["tr"], RING * i + r + 1 - RING)
                        d = dstf[:, bass.ds(t_, 1)]
                        nc.vector.tensor_copy(wide[r][:], d.to_broadcast([EP, EP])).then_inc(s["wide"], 1)
                    if not (isinstance(i, int) and i == 0):
                        dve.wait_ge(s["kept"], (RING + HALF) * i)
                    for r in range(RING):
                        t_ = RING * i + r
                        dve.wait_ge(s["tr"], RING * i + r + 1)
                        nc.vector.tensor_scalar(eq[r][:], ps[r][0:EP, 0:EP], dstf[:, bass.ds(t_, 1)], None,
                                                ALU.is_equal).then_inc(s["eq"], 1)
                    for h in range(HALF):
                        even, odd = RING * i + 2 * h, RING * i + 2 * h + 1
                        nc.vector.tensor_scalar(odd_even[h][:], ps[2 * h][0:EP, 0:EP], dstf[:, bass.ds(odd, 1)], None,
                                                ALU.is_equal)
                        nc.vector.tensor_scalar(even_odd[h][:], ps[2 * h + 1][0:EP, 0:EP], dstf[:, bass.ds(even, 1)], None,
                                                ALU.is_equal).then_inc(s["eqx"], 1)
                    for r in range(RING):
                        t_ = RING * i + r
                        dve.wait_ge(s["eq"], RING * i + r + 1)
                        nc.vector.tensor_reduce(count[:, bass.ds(t_, 1)], eq[r][:], AX.X, ALU.add)
                        nc.vector.tensor_tensor(low[r][:], eq[r][:], lower[:], ALU.mult).then_inc(s["low"], 1)
                    for r in range(RING):
                        t_ = RING * i + r
                        dve.wait_ge(s["low"], RING * i + r + 1)
                        nc.vector.tensor_reduce(before[:, bass.ds(t_, 1)], low[r][:], AX.X, ALU.add).then_inc(s["red"], 1)
                    for h in range(HALF):
                        even, odd = RING * i + 2 * h, RING * i + 2 * h + 1
                        dve.wait_ge(s["eqx"], HALF * i + h + 1)
                        nc.vector.tensor_reduce(more_before[:, bass.ds(odd, 1)], odd_even[h][:], AX.X, ALU.add)
                        nc.vector.tensor_reduce(more_count[:, bass.ds(even, 1)], even_odd[h][:], AX.X, ALU.add
                                                ).then_inc(s["redx"], 1)
                sweep(dve, EITER, body)
                dve.wait_ge(s["red"], TILES)
                dve.wait_ge(s["redx"], TILES // 2)
                link(nc.vector.tensor_tensor(count[:], count[:], more_count[:], ALU.add))
                link(nc.vector.tensor_tensor(before[:], before[:], more_before[:], ALU.add))
                link(nc.vector.tensor_scalar(late[:], before[:], 0.5, None, ALU.is_gt))
                link(nc.vector.tensor_tensor(tmp[:], spare[:], dstf[:], ALU.subtract))
                link(nc.vector.tensor_tensor(tmp[:], tmp[:], late[:], ALU.mult))
                link(nc.vector.tensor_tensor(tmp[:], tmp[:], dstf[:], ALU.add))
                link(nc.vector.tensor_copy(put_i[:], tmp[:]))
        run_block("match", ["zero", "zst", "pc", "wide", "tr", "eq", "low", "red", "eqx", "redx", "kept", "pace", "dv"], match_edges)

        SLOTS = (0, 1)

        def first_step(i):
            return isinstance(i, int) and i == 0

        def nth(i, b):
            return 2 * i + b + 1

        def again(eng, sem, i, b):
            if not first_step(i):
                eng.wait_ge(sem, 2 * i + b - 1)

        def turn4(ps, src):
            for j in range(J):
                last = nc.tensor.transpose(ps[:, j * D:(j + 1) * D], src[:, j * D:(j + 1) * D], ident[:])
            return last

        def rows4(ps, feat, w, bias_name=None):
            if bias_name:
                nc.tensor.matmul(ps[:], ones3[:], bias(bias_name), start=True, stop=False)
            for j in range(J):
                last = nc.tensor.matmul(ps[:, j * D:(j + 1) * D], feat[:, j * D:(j + 1) * D], w[:],
                                        start=not bias_name, stop=True if not bias_name else j == J - 1)
            return last

        epsc = keep("epsc", [P, 2])
        eps_ln, eps_half = epsc[:, 0:1], epsc[:, 1:2]

        def weight_tiles(ctx, names):
            return {n: ctx.enter_context(nc.sbuf_tensor(f"{stage[0]}_w_{n}", [P, D], F32)) for n in names}

        def kv_end(act, s, acc_ps):
            act.wait_ge(s["acc"], G)
            nc.scalar.mul(kvsum[:], acc_ps[:, 0:D + 1], 1.0 / N).then_inc(s["kvdone"], 1)

        def load_and_store(sp, loads, stores):
            def body(i):
                loads(i)
                if not first_step(i):
                    stores(i - 1)
            sweep(sp, PAIRS, body)
            stores(PAIRS - 1)

        W = t["L0_gnn_qkv_w"]

        def st(*names):
            return [f"{n}{b}" for n in names for b in SLOTS]

        def set_eps(ctx, block, s):
            @block.vector
            def _(dve):
                nc.vector.memset(eps_ln, LN_EPS)
                nc.vector.memset(eps_half, 4 * LN_EPS)
        run_block("eps", [], set_eps)

        class Ring:

            def __init__(self, sb, name, width, dt=F32):
                self.t = [sb(f"{name}{r}", [EP, width], dt) for r in range(RING)]

        def degree_tiles(sb):
            return dict(put=Ring(sb, "put", 1, I32).t, num=Ring(sb, "num", 1).t, si=Ring(sb, "si", 1, I32).t,
                        di=Ring(sb, "di", 1, I32).t, gs=Ring(sb, "gs", 1).t, gd=Ring(sb, "gd", 1).t,
                        deg_s=sb("deg_s", [EP, TILES]), deg_d=sb("deg_d", [EP, TILES]), deg_n=sb("deg_n", [P, G, J]),
                        ratio=sb("ratio", [EP, TILES]))
        DEGREE_SEMS = ["dcopy", "sw_added", "sw_dn", "icopy", "back", "ratio", "rdeg", "pace"] + [f"sw_got{r}" for r in range(RING)]

        def degrees_on_pool(pool, s, T):
            def add_counts(i):
                for r in range(RING):
                    tile = RING * i + r
                    nc.gpsimd.tensor_copy(T["put"][r][:], put_i[:, bass.ds(tile, 1)])
                    nc.gpsimd.tensor_copy(T["num"][r][:], count[:, bass.ds(tile, 1)]).then_inc(s["dcopy"], 1)
                    pool.wait_ge(s["dcopy"], tile + 1)
                    if r % 2 == 0 and not (first_step(i) and r == 0):
                        pool.wait_ge(s["sw_added"], before_stage("sw_added") + 16 * tile)
                    pool.sem_inc(s["pace"], 1)
                    nc.gpsimd.indirect_dma_start(degree, bass.IndirectOffsetOnAxis(T["put"][r][:, 0:1], 0), T["num"][r][:],
                                                 None, compute_op=ALU.add).then_inc(s["sw_added"], 16)
            sweep(pool, EITER, add_counts)
            pool.wait_ge(s["sw_added"], before_stage("sw_added") + 16 * TILES)
            pool.dma_start(T["deg_n"][:], degree[0:NPAD, :].rearrange("(g p j) a -> p g (j a)", p=P, j=J)).then_inc(s["sw_dn"], 16)

            def copy_back(i):
                for r in range(RING):
                    tile = RING * i + r
                    pool.wait_ge(s[f"sw_got{r}"], before_stage(f"sw_got{r}") + 32 * (i + 1))
                    pool.sem_inc(s["pace"], 1)
                    nc.gpsimd.tensor_copy(T["deg_s"][:, bass.ds(tile, 1)], T["gs"][r][:])
                    nc.gpsimd.tensor_copy(T["deg_d"][:, bass.ds(tile, 1)], T["gd"][r][:]).then_inc(s["back"], 1)

            def read_degrees(i):
                if not first_step(i):
                    copy_back(i - 1)
                for r in range(RING):
                    tile = RING * i + r
                    if not first_step(i):
                        pool.wait_ge(s["back"], tile + 1 - RING)
                        pool.sem_inc(s["pace"], 1)
                    nc.gpsimd.tensor_copy(T["si"][r][:], src_i[:, bass.ds(tile, 1)])
                    nc.gpsimd.tensor_copy(T["di"][r][:], dst_i[:, bass.ds(tile, 1)]).then_inc(s["icopy"], 1)
                    pool.wait_ge(s["icopy"], tile + 1)
                    pool.sem_inc(s["pace"], 1)
                    nc.gpsimd.indirect_dma_start(T["gs"][r][:], None, degree, bass.IndirectOffsetOnAxis(T["si"][r][:, 0:1], 0)
                                                 ).then_inc(s[f"sw_got{r}"], 16)
                    nc.gpsimd.indirect_dma_start(T["gd"][r][:], None, degree, bass.IndirectOffsetOnAxis(T["di"][r][:, 0:1], 0)
                                                 ).then_inc(s[f"sw_got{r}"], 16)
            read_degrees(0)
            with pool.Fori(1, EITER) as i:
                read_degrees(i)
            copy_back(EITER - 1)

        def degrees_on_dve(dve, s, T):
            dve.wait_ge(s["sw_dn"], before_stage("sw_dn") + 16)
            nc.vector.reciprocal(dinv2[:], T["deg_n"][:].rearrange("p g j -> p (g j)"))
            dve.wait_ge(s["back"], TILES)
            nc.vector.reciprocal(T["ratio"][:], T["deg_s"][:]).then_inc(s["rdeg"], 1)
            dve.wait_ge(s["rdeg"], 1)
            nc.vector.tensor_tensor(T["ratio"][:], T["ratio"][:], T["deg_d"][:], ALU.mult).then_inc(s["ratio"], 1)

        def degrees_on_act(act, s, T):
            act.wait_ge(s["ratio"], 1)
            nc.scalar.activation(gcn_coef[:], T["ratio"][:], ACT.Sqrt)

        def add_tiles(sb):
            return dict(idx=Ring(sb, "aidx", 1, I32).t, msg=Ring(sb, "amsg", D).t)

        def add_on_pool(pool, s, T, rows, done):
            before = before_stage("sw_added") + 16 * done

            def body(i):
                for r in range(RING):
                    tile = RING * i + r
                    nc.gpsimd.tensor_copy(T["idx"][r][:], put_i[:, bass.ds(tile, 1)])
                    nc.gpsimd.tensor_copy(T["msg"][r][:], added[:, bass.ds(tile, 1), :].rearrange("p a f -> p (a f)")
                                          ).then_inc(s["acopy"], 1)
                    pool.wait_ge(s["acopy"], tile + 1)
                    if r % 2 == 0 and not (first_step(i) and r == 0):
                        pool.wait_ge(s["sw_added"], before + 16 * tile)
                    pool.sem_inc(s["pace"], 1)
                    nc.gpsimd.indirect_dma_start(rows, bass.IndirectOffsetOnAxis(T["idx"][r][:, 0:1], 0), T["msg"][r][:], None,
                                                 compute_op=ALU.add).then_inc(s["sw_added"], 16)
            sweep(pool, EITER, body)
            pool.wait_ge(s["sw_added"], before + 16 * TILES)

        QUAD = 4

        def edge_tiles(ctx, sb):
            return dict(gidx=[sb(f"gidx{h}", [EP, 2], I32) for h in range(QUAD // 2)],
                        pidx=[sb(f"pidx{h}", [EP, 2], I32) for h in range(QUAD // 2)],
                        got=[sb(f"egot{r}", [EP, D]) for r in range(QUAD)],
                        mix=[sb(f"emix{r}", [EP, EP]) for r in range(QUAD)],
                        mixx=[sb(f"emixx{h}", [EP, EP]) for h in range(QUAD // 2)], msg=sb("emsg", [EP, QUAD, D]),
                        ps=ctx.enter_context(nc.psum_tensor(f"{stage[0]}_edge_ps", [P, QUAD * D], F32)))
        EDGE_SEMS = ["emix", "emm", "emsg", "gidx", "pidx", "epace", "sw_added"] + [f"sw_got{r}" for r in range(QUAD)]
        EDGE_COUNTS = {"sw_added": 16 * TILES, **{f"sw_got{r}": 16 * FOURS for r in range(QUAD)}}

        def edges_on_pool(pool, s, Q, source, target):
            def get(i, h):
                pair = QUAD // 2 * i + h
                if not first_step(i):
                    pool.wait_ge(s["emm"], i)
                    pool.sem_inc(s["epace"], 1)
                nc.gpsimd.tensor_copy(Q["gidx"][h][:], src_i[:, bass.ds(2 * pair, 2)]).then_inc(s["gidx"], 1)
                pool.wait_ge(s["gidx"], pair + 1)
                pool.sem_inc(s["epace"], 1)
                for r in (0, 1):
                    nc.gpsimd.indirect_dma_start(Q["got"][2 * h + r][:], None, source,
                                                 bass.IndirectOffsetOnAxis(Q["gidx"][h][:, r:r + 1], 0)
                                                 ).then_inc(s[f"sw_got{2 * h + r}"], 16)

            def put(i, h):
                pair = QUAD // 2 * i + h
                nc.gpsimd.tensor_copy(Q["pidx"][h][:], put_i[:, bass.ds(2 * pair, 2)]).then_inc(s["pidx"], 1)
                pool.wait_ge(s["pidx"], pair + 1)
                pool.wait_ge(s["emsg"], i + 1)
                if not (first_step(i) and h == 0):
                    pool.wait_ge(s["sw_added"], before_stage("sw_added") + 32 * pair)
                pool.sem_inc(s["epace"], 1)
                for r in (0, 1):
                    nc.gpsimd.indirect_dma_start(target, bass.IndirectOffsetOnAxis(Q["pidx"][h][:, r:r + 1], 0),
                                                 Q["msg"][:, 2 * h + r, :], None, compute_op=ALU.add
                                                 ).then_inc(s["sw_added"], 16)

            def body(i):
                for h in range(QUAD // 2):
                    get(i, h)
                    if not first_step(i):
                        put(i - 1, h)
            body(0)
            body(1)
            with pool.Fori(2, FOURS) as i:
                body(i)
            for h in range(QUAD // 2):
                put(FOURS - 1, h)
            pool.wait_ge(s["sw_added"], before_stage("sw_added") + 16 * TILES)

        def edges_on_dve(dve, s, Q, coef):
            def part(i):
                if not first_step(i):
                    dve.wait_ge(s["emm"], i)
                for r in range(QUAD):
                    tile = QUAD * i + r
                    last = nc.vector.tensor_scalar(Q["mix"][r][:], same[:, bass.ds(tile, 1), :].rearrange("p a f -> p (a f)"),
                                                   coef[:, bass.ds(tile, 1)], None, ALU.mult)
                for h in range(QUAD // 2):
                    last = nc.vector.tensor_scalar(
                        Q["mixx"][h][:], cross[:, bass.ds(QUAD // 2 * i + h, 1), :].rearrange("p a f -> p (a f)"),
                        coef[:, bass.ds(QUAD * i + 2 * h + 1, 1)], None, ALU.mult)
                last.then_inc(s["emix"], 1)
            return part

        def edges_on_pe(pe, s, Q):
            def part(i):
                pe.wait_ge(s["emix"], i + 1)
                if not first_step(i):
                    pe.wait_ge(s["emsg"], i)
                for r in range(QUAD):
                    pe.wait_ge(s[f"sw_got{r}"], before_stage(f"sw_got{r}") + 16 * (i + 1))
                    if r % 2 == 1:
                        even = Q["ps"][0:EP, (r - 1) * D:r * D]
                        nc.tensor.matmul(even, Q["mix"][r - 1][:], Q["got"][r - 1][:], start=True, stop=False)
                        nc.tensor.matmul(even, Q["mixx"][r // 2][:], Q["got"][r][:], start=False, stop=True)
                        last = nc.tensor.matmul(Q["ps"][0:EP, r * D:(r + 1) * D], Q["mix"][r][:], Q["got"][r][:],
                                                start=True, stop=True)
                last.then_inc(s["emm"], 1)
            return part

        def edges_on_act(act, s, Q):
            def part(i):
                act.wait_ge(s["emm"], i + 1)
                if not first_step(i):
                    act.wait_ge(s["sw_added"], before_stage("sw_added") + 16 * QUAD * i)
                nc.scalar.copy(Q["msg"][:], Q["ps"][0:EP, :].rearrange("p (r d) -> p r d", r=QUAD)).then_inc(s["emsg"], 1)
            return part

        def there(g, pairs=PAIRS):
            return not isinstance(g, int) or 0 <= g < 2 * pairs

        def ran(eng, sem, g):
            eng.wait_ge(sem, g + 1)

        def free1(eng, sem, g):
            if not (isinstance(g, int) and g < 1):
                eng.wait_ge(sem, g)

        def free2(eng, sem, g):
            if not (isinstance(g, int) and g < 2):
                eng.wait_ge(sem, g - 1)

        def landed(eng, sems, g, i, b, per_group=1):
            eng.wait_ge(sems[b], 16 * per_group * (i + 1))

        def stored(eng, sems, g, i, b, per_group=1):
            if not (isinstance(g, int) and g < 2):
                eng.wait_ge(sems[b], 16 * per_group * i)

        def step_sweep(eng, step, lag, pairs=PAIRS, edges=None):
            peel = (lag + 3) // 2
            more = (lag + 1) // 2

            def pair(i):
                for b in SLOTS:
                    if not isinstance(i, int) or 2 * i + b < 2 * pairs + lag:
                        step(2 * i + b, i, b)
                if edges and (not isinstance(i, int) or i < FOURS):
                    edges(i)

            for i in range(peel):
                pair(i)
            with_edges = min(FOURS, pairs - 1) if edges else peel
            if with_edges > peel:
                with eng.Fori(peel, with_edges) as i:
                    pair(i)
            else:
                with_edges = peel
            if pairs - 1 > with_edges:
                with eng.Fori(with_edges, pairs - 1) as i:
                    for b in SLOTS:
                        step(2 * i + b, i, b)
            for i in range(pairs - 1, max(pairs + more, FOURS if edges else 0)):
                pair(i)

        def tail_of(g):
            return isinstance(g, int) and g == G - 1

        def rows_of(g):
            return TAILP if tail_of(g) else P

        def stats4(tiles, src):
            for j in range(J):
                last = nc.vector.bn_stats(tiles["st"][:, j, :], src[:, j * D:(j + 1) * D])
            return last

        def aggr4(tiles):
            for j in range(J):
                last = nc.vector.bn_aggr(tiles["mv"][:, j, :], tiles["st"][:, j, :])
            return last

        def apply4(tiles, dst, src):
            for j in range(J):
                js = slice(j * D, (j + 1) * D)
                last = nc.vector.tensor_scalar(dst[:, js], src[:, js], tiles["mv"][:, j, 0:1], tiles["rs"][:, j:j + 1],
                                               ALU.subtract, ALU.mult)
            return last

        def norm1_tiles(sb, name):
            return dict(st=sb(f"{name}st", [P, J, 6]), mv=sb(f"{name}mv", [P, J, 2]), sd=sb(f"{name}sd", [P, J]),
                        rs=sb(f"{name}rs", [P, J]))

        def norm_sems(k):
            return [f"{n}{k}" for n in ("stats", "var", "std", "rstd", "nn")]

        def norm_stats(dve, s, k, T, src, g):
            stats4(T, src).then_inc(s[f"stats{k}"], 1)

        def norm_vars(dve, s, k, T, g):
            ran(dve, s[f"stats{k}"], g)
            dve.sem_inc(s["pace"], 1)
            aggr4(T).then_inc(s[f"var{k}"], 1)

        def norm_root(act, s, k, T, g, eps):
            ran(act, s[f"var{k}"], g)
            nc.scalar.activation(T["sd"][:], T["mv"][:, :, 1], ACT.Sqrt, bias=eps).then_inc(s[f"std{k}"], 1)

        def norm_recip(dve, s, k, T, g):
            ran(dve, s[f"std{k}"], g)
            nc.vector.reciprocal(T["rs"][:], T["sd"][:]).then_inc(s[f"rstd{k}"], 1)

        def norm_apply(dve, s, k, T, dst, src, g):
            ran(dve, s[f"rstd{k}"], g)
            apply4(T, dst, src).then_inc(s[f"nn{k}"], 1)

        def kv1_tiles(sb):
            return dict(kc=sb("kc", [P, GROUP]), kf=[sb(f"kf{b}", [P, GROUP]) for b in SLOTS], sk=sb("sk", [P, GROUP]),
                        ss=sb("ss", [P, J]), nk=sb("nk", [P, J]), rk=sb("rk", [P, J]),
                        vs=[sb(f"vs{b}", [P, J, D + 1]) for b in SLOTS])
        KV1_SEMS = ["k", "v2", "kc", "kf", "sk", "ss", "nk", "rk", "vs", "acc"]

        def pair_of(sb, name):
            return [sb(f"{name}{b}", [P, GROUP]) for b in SLOTS]

        def kv_copy(act, s, T, k_ps, g):
            ran(act, s["k"], g)
            free1(act, s["kf"], g)
            nc.scalar.copy(T["kc"][:], k_ps[:]).then_inc(s["kc"], 1)

        def kv_fix(dve, s, T, g, b):
            ran(dve, s["kc"], g)
            free2(dve, s["acc"], g)
            nc.vector.scalar_tensor_tensor(out=T["kf"][b][:], in0=T["kc"][:], scalar=0.0, in1=T["kc"][:],
                                           op0=ALU.is_equal, op1=ALU.add).then_inc(s["kf"], 1)

        def kv_square(act, s, T, g, b):
            ran(act, s["kf"], g)
            free1(act, s["ss"], g)
            nc.scalar.activation(T["sk"][:], T["kf"][b][:], ACT.Square).then_inc(s["sk"], 1)

        def kv_length(dve, s, T, g):
            ran(dve, s["sk"], g)
            nc.vector.tensor_reduce(T["ss"][:], T["sk"][:].rearrange("p (j d) -> p j d", j=J), AX.X, ALU.add
                                    ).then_inc(s["ss"], 1)

        def kv_root(act, s, T, g):
            ran(act, s["ss"], g)
            nc.scalar.activation(T["nk"][:], T["ss"][:], ACT.Sqrt).then_inc(s["nk"], 1)

        def kv_scale(dve, s, T, v_ps, g, b):
            ran(dve, s["nk"], g)
            nc.vector.reciprocal(T["rk"][:], T["nk"][:]).then_inc(s["rk"], 1)
            ran(dve, s["rk"], g)
            ran(dve, s["v2"], g)
            free2(dve, s["acc"], g)
            r = T["rk"][:, :]
            nc.vector.tensor_tensor(T["vs"][b][:, :, 0:D], v_ps[:].rearrange("p (j d) -> p j d", j=J),
                                    r.unsqueeze(2).to_broadcast([P, J, D]), ALU.mult)
            nc.vector.tensor_copy(T["vs"][b][:, :, D:D + 1], r.unsqueeze(2)).then_inc(s["vs"], 1)

        def kv_product(pe, s, T, acc_ps, g, b):
            ran(pe, s["vs"], g)
            rows = rows_of(g)
            for j in range(J):
                last = nc.tensor.matmul(acc_ps[:, 0:D + 1], T["kf"][b][0:rows, j * D:(j + 1) * D], T["vs"][b][0:rows, j, :],
                                        start=isinstance(g, int) and g == 0 and j == 0,
                                        stop=tail_of(g) and j == J - 1, skip_group_check=True)
            last.then_inc(s["acc"], 1)

        def pass_first(ctx, block, s):
            def sb(name, shape, dt=F32):
                return ctx.enter_context(nc.sbuf_tensor(f"{stage[0]}_{name}", shape, dt))
            w = weight_tiles(ctx, ["fc", "g", "conv", "k", "v"])
            xt, xn, h0, zn, hT, g0, yo = (pair_of(sb, n) for n in ("xt", "xn", "h0", "zn", "hT", "g0", "yo"))
            T1, T2, TK = norm1_tiles(sb, "n1"), norm1_tiles(sb, "n2"), kv1_tiles(sb)
            tr_ps, z_ps, g_ps, y_ps, tz_ps, k_ps, v_ps, acc_ps = (
                ctx.enter_context(nc.psum_tensor(f"{stage[0]}_ps{n}", [P, GROUP], F32)) for n in range(8))
            ld, g0st, hTst, yost = ([s[f"{n}{b}"] for b in SLOTS] for n in ("ld", "g0st", "hTst", "yost"))
            TD = degree_tiles(sb)

            @block.gpsimd
            def _(pool):
                degrees_on_pool(pool, s, TD)

            @block.sync
            def _(sp):
                for n, v in (("fc", t["L0_gnn_t_fc_w"]), ("g", t["L0_gnn_g_fc_w"]), ("conv", t["L0_gnn_conv_w"][0]),
                             ("k", W[0, 1]), ("v", W[0, 2])):
                    sp.dma_start(w[n][:], v).then_inc(s["w"], 16)

                def step(g, i, b):
                    if there(g):
                        free2(sp, s["nn1"], g)
                        if tail_of(g):
                            sp.dma_start(xt[b][0:TAILP, :], x_tail).then_inc(ld[b], 16)
                        else:
                            sp.dma_start(xt[b][:], at(x_groups, g)).then_inc(ld[b], 16)
                    if there(g - 2):
                        ran(sp, s["g0"], g - 2)
                        sp.dma_start(at(g_first, g - 2), g0[b][:]).then_inc(g0st[b], 16)
                        ran(sp, s["yo"], g - 2)
                        sp.dma_start(at(grouped(table[0]), g - 2), yo[b][:]).then_inc(yost[b], 16)
                        sp.dma_start(at(grouped(table[1]), g - 2), yo[b][:]).then_inc(yost[b], 16)
                    if there(g - 3):
                        ran(sp, s["hT"], g - 3)
                        sp.dma_start(at(cur[0], g - 3), hT[1 - b][:]).then_inc(hTst[1 - b], 16)
                step_sweep(sp, step, 3)
                for sem in g0st + yost + hTst:
                    sp.wait_ge(sem, (32 if sem in yost else 16) * PAIRS)

            @block.tensor
            def _(pe):
                pe.wait_ge(s["w"], 80)
                pe.wait_ge(s["wk"], 1)

                def step(g, i, b):
                    c = 1 - b
                    if there(g - 1):
                        ran(pe, s["h0"], g - 1)
                        free1(pe, s["g0"], g - 1)
                        nc.tensor.matmul(g_ps[:], w["g"][:], h0[c][:], start=True, stop=True).then_inc(s["g"], 1)
                    if there(g - 3):
                        ran(pe, s["hT"], g - 3)
                        free1(pe, s["kc"], g - 3)
                        rows4(k_ps, hT[c], w["k"]).then_inc(s["k"], 1)
                    if there(g - 5):
                        kv_product(pe, s, TK, acc_ps, g - 5, c)
                    if there(g - 4):
                        free1(pe, s["vs"], g - 4)
                        rows4(v_ps, hT[b], w["v"]).then_inc(s["v2"], 1)
                    if there(g):
                        ran(pe, s["nn1"], g)
                        free1(pe, s["h0"], g)
                        turn4(tr_ps, xn[b]).then_inc(s["tr"], 1)
                    if there(g - 1):
                        ran(pe, s["g0"], g - 1)
                        free1(pe, s["yo"], g - 1)
                        rows4(y_ps, g0[c], w["conv"]).then_inc(s["y"], 1)
                    if there(g - 2):
                        ran(pe, s["nn2"], g - 2)
                        free1(pe, s["hT"], g - 2)
                        turn4(tz_ps, zn[b]).then_inc(s["tz"], 1)
                    if there(g - 1):
                        free1(pe, s["nn2"], g - 1)
                        rows4(z_ps, h0[c], w["fc"], "t_fc").then_inc(s["z"], 1)
                step_sweep(pe, step, 5)

            @block.scalar
            def _(act):
                def step(g, i, b):
                    c = 1 - b
                    if there(g - 5):
                        kv_root(act, s, TK, g - 5)
                    if there(g - 1):
                        ran(act, s["g"], g - 1)
                        stored(act, g0st, g - 1, i if b else i - 1, c)
                        free2(act, s["y"], g - 1)
                        nc.scalar.activation(g0[c][:], g_ps[:], ACT.Relu, bias=bnbi[:, 0:1],
                                             scale=bnsc[:, 0:1]).then_inc(s["g0"], 1)
                    if there(g - 4):
                        kv_square(act, s, TK, g - 4, b)
                    if there(g):
                        norm_root(act, s, 1, T1, g, eps_ln)
                    if there(g - 2):
                        norm_root(act, s, 2, T2, g - 2, eps_ln)
                    if there(g - 3):
                        kv_copy(act, s, TK, k_ps, g - 3)
                    if there(g):
                        ran(act, s["tr"], g)
                        free2(act, s["z"], g)
                        nc.scalar.activation(h0[b][:], tr_ps[:], ACT.Relu).then_inc(s["h0"], 1)
                    if there(g - 1):
                        ran(act, s["y"], g - 1)
                        stored(act, yost, g - 1, i if b else i - 1, c, 2)
                        nc.scalar.copy(yo[c][:], y_ps[:]).then_inc(s["yo"], 1)
                    if there(g - 2):
                        ran(act, s["tz"], g - 2)
                        stored(act, hTst, g - 2, i - 1, b)
                        free2(act, s["v2"], g - 2)
                        nc.scalar.activation(hT[b][:], tz_ps[:], ACT.Relu, bias=col("lnb0"),
                                             scale=col("lng0")).then_inc(s["hT"], 1)
                step_sweep(act, step, 5)
                kv_end(act, s, acc_ps)
                act.wait_ge(s["kvdone"], 1)
                degrees_on_act(act, s, TD)

            @block.vector
            def _(dve):
                dve.wait_ge(s["w"], 80)
                nc.vector.tensor_scalar(w["k"][:], w["k"][:], GUARD, None, ALU.mult).then_inc(s["wk"], 1)

                def step(g, i, b):
                    c = 1 - b
                    if there(g):
                        landed(dve, ld, g, i, b)
                        norm_stats(dve, s, 1, T1, xt[b], g)
                    if there(g - 4):
                        kv_fix(dve, s, TK, g - 4, b)
                    if there(g - 5):
                        kv_scale(dve, s, TK, v_ps, g - 5, c)
                    if there(g - 2):
                        ran(dve, s["z"], g - 2)
                        norm_stats(dve, s, 2, T2, z_ps, g - 2)
                    if there(g):
                        norm_vars(dve, s, 1, T1, g)
                    if there(g - 2):
                        norm_vars(dve, s, 2, T2, g - 2)
                    if there(g):
                        norm_recip(dve, s, 1, T1, g)
                    if there(g - 2):
                        norm_recip(dve, s, 2, T2, g - 2)
                    if there(g):
                        free2(dve, s["tr"], g)
                        norm_apply(dve, s, 1, T1, xn[b], xt[b], g)
                    if there(g - 2):
                        free2(dve, s["tz"], g - 2)
                        norm_apply(dve, s, 2, T2, zn[b], z_ps, g - 2)
                    if there(g - 4):
                        kv_length(dve, s, TK, g - 4)
                step_sweep(dve, step, 5)
                degrees_on_dve(dve, s, TD)
        FIRST_SEMS = ([x for x in DEGREE_SEMS if x != "pace"] + ["w", "wk", "h0", "z", "g", "g0", "yo", "y", "hT", "tr", "tz", "kvdone", "pace"] + KV1_SEMS
                      + norm_sems(1) + norm_sems(2) + st("ld", "g0st", "hTst", "yost"))
        FIRST_COUNTS = {"sw_added": 16 * TILES, "sw_dn": 16, **{f"sw_got{r}": 32 * EITER for r in range(RING)}}

        def attention(layer, pairs=(0, PAIRS)):
            source, dest, more = cur[layer], cur[1 - layer], layer == 0
            g0, NP = 2 * pairs[0], pairs[1] - pairs[0]

            def here(g):
                return there(g, NP)

            def emit(ctx, block, s):
                def sb(name, shape, dt=F32):
                    return ctx.enter_context(nc.sbuf_tensor(f"{stage[0]}_{name}", shape, dt))
                w = weight_tiles(ctx, ["q", "v"] + (["k2", "v2"] if more else []))
                hT, hn, qc, qf, sq, t1, su, nn, cT = (pair_of(sb, n) for n in (
                    "hT", "hn", "qc", "qf", "sq", "t1", "su", "nn", "cT"))
                nq, rq, cr, den, beta, alpha = (sb(n, [P, J]) for n in ("nq", "rq", "cr", "den", "beta", "alpha"))
                T1, TK = norm1_tiles(sb, "n1"), kv1_tiles(sb)
                th_ps, v_ps, p_ps, small_ps, tc_ps, v2_ps, acc_ps = (
                    ctx.enter_context(nc.psum_tensor(f"{stage[0]}_ps{n}", [P, GROUP], F32)) for n in range(7))
                q_ps = th_ps
                Q = edge_tiles(ctx, sb)
                TA = add_tiles(sb) if more else None
                first3 = p_ps[:, 0:(J - 1) * (D + 1)].rearrange("p (j d) -> p j d", j=J - 1)
                lengths = small_ps[:, D + 1:D + 1 + J]

                def by_kv(j):
                    return p_ps[:, j * (D + 1):(j + 1) * (D + 1)] if j < J - 1 else small_ps[:, 0:D + 1]
                ld, cTst = ([s[f"{n}{b}"] for b in SLOTS] for n in ("ld", "cTst"))

                @block.sync
                def _(sp):
                    for n, v in (("q", W[layer, 0]), ("v", W[layer, 2])) + ((("k2", W[1, 1]), ("v2", W[1, 2])) if more else ()):
                        sp.dma_start(w[n][:], v).then_inc(s["w"], 16)

                    def step(g, i, b):
                        if here(g):
                            free2(sp, s["v"], g)
                            sp.dma_start(hT[b][:], at(source, g + g0)).then_inc(ld[b], 16)
                        if here(g - 5):
                            ran(sp, s["cT"], g - 5)
                            sp.dma_start(at(dest, g + (g0 - 5)), cT[1 - b][:]).then_inc(cTst[1 - b], 16)
                    step_sweep(sp, step, 5, NP)
                    for sem in cTst:
                        sp.wait_ge(sem, 16 * NP)

                @block.gpsimd
                def _(pool):
                    edges_on_pool(pool, s, Q, table[0], table[1])
                    if more:
                        add_on_pool(pool, s, TA, attr_sum, TILES)

                @block.tensor
                def _(pe):
                    pe.wait_ge(s["w"], 64 if more else 32)
                    pe.wait_ge(s["wk"], 1)

                    def step(g, i, b):
                        c = 1 - b
                        if more and here(g - 7):
                            kv_product(pe, s, TK, acc_ps, g - 7, c)
                        if here(g - 4):
                            ran(pe, s["nn1"], g - 4)
                            if more:
                                free1(pe, s["kc"], g - 4)
                            else:
                                free1(pe, s["cT"], g - 4)
                            turn4(tc_ps, nn[b]).then_inc(s["tc"], 1)
                        if here(g):
                            landed(pe, ld, g, i, b)
                            free1(pe, s["qc"], g)
                            turn4(th_ps, hT[b]).then_inc(s["th"], 1)
                        if more and here(g - 4):
                            ran(pe, s["cT"], g - 4)
                            rows4(tc_ps, cT[b], w["k2"]).then_inc(s["k"], 1)
                        if more and here(g - 5):
                            free1(pe, s["vs"], g - 5)
                            rows4(v2_ps, cT[c], w["v2"]).then_inc(s["v2"], 1)
                        if here(g - 1):
                            ran(pe, s["sq"], g - 1)
                            free1(pe, s["t1"], g - 1)
                            for j in range(J):
                                js = slice(j * D, (j + 1) * D)
                                nc.tensor.matmul(by_kv(j), qf[c][:, js], kvsum[:], start=True, stop=True)
                                last = nc.tensor.matmul(lengths[:, j:j + 1], sq[c][:, js], onescol[:], start=True, stop=True)
                            last.then_inc(s["p1"], 1)
                        if here(g):
                            ran(pe, s["hn"], g)
                            nc.tensor.matmul(q_ps[:], w["q"][:], hT[b][:], start=True, stop=True).then_inc(s["q"], 1)
                        if here(g - 1):
                            free1(pe, s["su"], g - 1)
                            rows4(v_ps, hT[c], w["v"]).then_inc(s["v"], 1)
                    step_sweep(pe, step, 7 if more else 4, NP, edges_on_pe(pe, s, Q))

                @block.scalar
                def _(act):
                    def step(g, i, b):
                        c = 1 - b
                        if here(g - 3):
                            norm_root(act, s, 1, T1, g - 3, eps_half)
                        if more and here(g - 6):
                            kv_root(act, s, TK, g - 6)
                        if here(g - 4):
                            ran(act, s["tc"], g - 4)
                            stored(act, cTst, g - 4, i - 2, b)
                            if more:
                                free2(act, s["v2"], g - 4)
                            nc.scalar.activation(cT[b][:], tc_ps[:], ACT.Relu, bias=col(f"lnb{layer + 1}"),
                                                 scale=col(f"lng{layer + 1}")).then_inc(s["cT"], 1)
                        if here(g - 1):
                            ran(act, s["qf"], g - 1)
                            free2(act, s["p1"], g - 1)
                            nc.scalar.activation(sq[c][:], qf[c][:], ACT.Square).then_inc(s["sq"], 1)
                        if more and here(g - 5):
                            kv_square(act, s, TK, g - 5, c)
                        if here(g):
                            ran(act, s["th"], g)
                            free2(act, s["t1"], g)
                            nc.scalar.copy(hn[b][:], th_ps[:]).then_inc(s["hn"], 1)
                        if more and here(g - 4):
                            kv_copy(act, s, TK, tc_ps, g - 4)
                        if here(g - 1):
                            ran(act, s["p1"], g - 1)
                            free1(act, s["rq"], g - 1)
                            nc.scalar.activation(nq[:], lengths, ACT.Sqrt).then_inc(s["nq"], 1)
                        if here(g):
                            ran(act, s["q"], g)
                            free2(act, s["qf"], g)
                            nc.scalar.copy(qc[b][:], q_ps[:]).then_inc(s["qc"], 1)
                    step_sweep(act, step, 6 if more else 4, NP, edges_on_act(act, s, Q))
                    if more:
                        kv_end(act, s, acc_ps)
                        act.wait_ge(s["kvdone"], 1)

                @block.vector
                def _(dve):
                    dve.wait_ge(s["w"], 64 if more else 32)
                    if more:
                        nc.vector.tensor_scalar(w["k2"][:], w["k2"][:], GUARD, None, ALU.mult)
                    nc.vector.tensor_scalar(w["q"][:], w["q"][:], GUARD, None, ALU.mult).then_inc(s["wk"], 1)

                    def step(g, i, b):
                        c = 1 - b
                        if here(g - 2):
                            ran(dve, s["nq"], g - 2)
                            nc.vector.reciprocal(rq[:], nq[:]).then_inc(s["rq"], 1)
                        if here(g - 1):
                            ran(dve, s["qc"], g - 1)
                            free2(dve, s["p1"], g - 1)
                            nc.vector.scalar_tensor_tensor(out=qf[c][:], in0=qc[c][:], scalar=0.0, in1=qc[c][:],
                                                           op0=ALU.is_equal, op1=ALU.add).then_inc(s["qf"], 1)
                        if here(g - 2):
                            ran(dve, s["rq"], g - 2)
                            nc.vector.tensor_tensor(cr[:, 0:J - 1], first3[:, :, D], rq[:, 0:J - 1], ALU.mult)
                            nc.vector.tensor_tensor(cr[:, J - 1:J], small_ps[:, D:D + 1], rq[:, J - 1:J], ALU.mult
                                                    ).then_inc(s["cr"], 1)
                        if more and here(g - 5):
                            kv_fix(dve, s, TK, g - 5, c)
                        if here(g - 2):
                            ran(dve, s["cr"], g - 2)
                            nc.vector.tensor_scalar(den[:], cr[:], 1.0, None, ALU.add).then_inc(s["den"], 1)
                        if here(g - 3):
                            norm_recip(dve, s, 1, T1, g - 3)
                        if here(g - 2):
                            ran(dve, s["den"], g - 2)
                            nc.vector.reciprocal(beta[:], den[:]).then_inc(s["beta"], 1)
                            ran(dve, s["beta"], g - 2)
                            nc.vector.tensor_tensor(alpha[:], beta[:], rq[:], ALU.mult).then_inc(s["alpha"], 1)
                        if here(g - 2):
                            ran(dve, s["alpha"], g - 2)
                            ran(dve, s["p1"], g - 2)
                            for j in range(J):
                                js = slice(j * D, (j + 1) * D)
                                last = nc.vector.scalar_tensor_tensor(out=t1[b][:, js], in0=by_kv(j)[:, 0:D], scalar=alpha[:, j:j + 1],
                                                                      in1=hn[b][:, js], op0=ALU.mult, op1=ALU.add)
                            last.then_inc(s["t1"], 1)
                        if more and here(g - 6):
                            kv_scale(dve, s, TK, v2_ps, g - 6, b)
                        if here(g - 3):
                            free2(dve, s["tc"], g - 3)
                            norm_apply(dve, s, 1, T1, nn[c], su[c], g - 3)
                        if here(g - 2):
                            ran(dve, s["t1"], g - 2)
                            ran(dve, s["v"], g - 2)
                            for j in range(J):
                                js = slice(j * D, (j + 1) * D)
                                last = nc.vector.scalar_tensor_tensor(out=su[b][:, js], in0=v_ps[:, js], scalar=beta[:, j:j + 1],
                                                                      in1=t1[b][:, js], op0=ALU.mult, op1=ALU.add)
                            last.then_inc(s["su"], 1)
                        if more and here(g - 5):
                            kv_length(dve, s, TK, g - 5)
                        if here(g - 2):
                            ran(dve, s["su"], g - 2)
                            norm_stats(dve, s, 1, T1, su[b], g - 2)
                            norm_vars(dve, s, 1, T1, g - 2)
                    step_sweep(dve, step, 6 if more else 3, NP, edges_on_dve(dve, s, Q, gcn_coef))
            return (["w", "wk", "v", "cT", "th", "q", "hn", "qf", "p1", "sq", "tc", "qc", "nq", "rq", "cr", "den",
                     "beta", "alpha", "t1", "su", "kvdone", "pace", "acopy"] + EDGE_SEMS + KV1_SEMS + norm_sems(1) + st("ld", "cTst")), emit

        def norm_shift(dve, s, k, T, g):
            ran(dve, s[f"rstd{k}"], g)
            nc.vector.scalar_tensor_tensor(out=T["nb"][:], in0=T["mv"][:, :, 0], scalar=-1.0, in1=T["rs"][:],
                                           op0=ALU.mult, op1=ALU.mult).then_inc(s[f"shift{k}"], 1)

        def norm_apply_act(act, s, k, T, dst, src, g):
            ran(act, s[f"shift{k}"], g)
            for j in range(J):
                js = slice(j * D, (j + 1) * D)
                last = nc.scalar.activation(dst[:, js], src[:, js], ACT.Identity, bias=T["nb"][:, j:j + 1],
                                            scale=T["rs"][:, j:j + 1])
            last.then_inc(s[f"nn{k}"], 1)

        def back(i, b, k):
            return i - (k - b + 1) // 2

        def middle(ctx, block, s):
            def sb(name, shape, dt=F32):
                return ctx.enter_context(nc.sbuf_tensor(f"{stage[0]}_{name}", shape, dt))
            w = weight_tiles(ctx, ["out", "w1", "w2", "w3", "gin"])
            (ta, gf, x1, xr, ag, xb, sc, gr, gx, mT, xo, n0, h0, za, r1, n1, h1, r2, n2, h2, x2, n3, h3, yo, ye) = (
                pair_of(sb, n) for n in ("ta gf x1 xr ag xb sc gr gx mT xo n0 h0 za r1 n1 h1 r2 n2 h2 x2 n3 h3 yo ye").split())
            T = [norm1_tiles(sb, f"t{k}") for k in range(4)]
            for k in (2, 3):
                T[k]["nb"] = sb(f"t{k}nb", [P, J])
            tr_ps, o_ps, t01_ps, z1_ps, z2_ps, t23_ps, z3_ps, y_ps = (
                ctx.enter_context(nc.psum_tensor(f"{stage[0]}_ps{n}", [P, GROUP], F32)) for n in range(8))
            lt, lg, lx, la, lb, xost, x2st, yost = ([s[f"{n}{b}"] for b in SLOTS] for n in (
                "lt", "lg", "lx", "la", "lb", "xost", "x2st", "yost"))
            def loaded(eng, sems, q, pair, slot, per_group=1):
                eng.wait_ge(sems[slot], 16 * per_group * (pair + 1))

            def kept(eng, sems, g, q, pair, slot, per_group=1):
                if not (isinstance(g, int) and q < 2):
                    eng.wait_ge(sems[slot], 16 * per_group * pair)

            @block.sync
            def _(sp):
                for n, v in (("out", t["L0_gnn_fc_w"]), ("w1", t["L1_gnn_W1"][0:D, :]), ("w2", t["L1_gnn_W2"]),
                             ("w3", t["L1_gnn_W3"]), ("gin", t["L2_gnn_W1"][0])):
                    sp.dma_start(w[n][:], v).then_inc(s["w"], 16)

                def step(g, i, b):
                    c = 1 - b
                    if there(g):
                        free2(sp, s["sc"], g)
                        sp.dma_start(ta[b][:], at(grouped(table[1]), g)).then_inc(lt[b], 16)
                        free2(sp, s["gx"], g)
                        sp.dma_start(gf[b][:], at(g_first, g)).then_inc(lg[b], 16)
                        sp.dma_start(x1[b][:], at(cur[0], g)).then_inc(lg[b], 16)
                    if there(g - 2):
                        free2(sp, s["xo"], g - 2)
                        if tail_of(g - 2):
                            sp.dma_start(xr[b][0:TAILP, :], x_tail).then_inc(lx[b], 16)
                        else:
                            sp.dma_start(xr[b][:], at(x_groups, g - 2)).then_inc(lx[b], 16)
                    if there(g - 4):
                        free2(sp, s["za"], g - 4)
                        sp.dma_start(ag[b][:], at(grouped(attr_sum), g - 4)).then_inc(la[b], 16)
                        ran(sp, s["xo"], g - 4)
                        sp.dma_start(at(grouped(xres[0]), g - 4), xo[b][:]).then_inc(xost[b], 16)
                    if there(g - 10):
                        ran(sp, s["x2"], g - 10)
                        sp.dma_start(at(grouped(xres[1]), g - 10), x2[b][:]).then_inc(x2st[b], 16)
                    if there(g - 8):
                        sp.wait_ge(xost[b], 16 * (back(i, b, 8) + 1))
                        sp.dma_start(xb[b][:], at(grouped(xres[0]), g - 8)).then_inc(lb[b], 16)
                    if there(g - 13):
                        ran(sp, s["ye"], g - 13)
                        sp.dma_start(at(grouped(table[0]), g - 13), yo[c][:]).then_inc(yost[c], 16)
                        sp.dma_start(at(grouped(table[1]), g - 13), ye[c][:]).then_inc(yost[c], 16)
                step_sweep(sp, step, 13)
                for sem in xost + x2st:
                    sp.wait_ge(sem, 16 * PAIRS)
                for sem in yost:
                    sp.wait_ge(sem, 32 * PAIRS)

            @block.gpsimd
            def _(pool):
                def step(g, i, b):
                    c = 1 - b
                    if there(g):
                        landed(pool, lg, g, i, b, 2)
                        free2(pool, s["mT"], g)
                        nc.gpsimd.tensor_tensor(gx[b][:], gf[b][:], x1[b][:], ALU.add).then_inc(s["gx"], 1)
                    if there(g - 1):
                        ran(pool, s["gr"], g - 1)
                        ran(pool, s["gx"], g - 1)
                        free2(pool, s["o"], g - 1)
                        nc.gpsimd.tensor_tensor(mT[c][:], gr[c][:], gx[c][:], ALU.add).then_inc(s["mT"], 1)
                    if there(g - 4):
                        ran(pool, s["za"], g - 4)
                        free2(pool, s["nn1"], g - 4)
                        pool.sem_inc(s["ppace"], 1)
                        nc.gpsimd.tensor_scalar(r1[b][:], za[b][:], 0.0, None, ALU.max).then_inc(s["r1"], 1)
                    if there(g - 11):
                        ran(pool, s["yo"], g - 11)
                        kept(pool, yost, g, g - 11, back(i, b, 11), c, 2)
                        pool.sem_inc(s["ppace"], 1)
                        nc.gpsimd.tensor_scalar(ye[c][:], yo[c][:], eps1[:, 0:1], None, ALU.mult).then_inc(s["ye"], 1)
                step_sweep(pool, step, 11)

            @block.tensor
            def _(pe):
                pe.wait_ge(s["w"], 80)
                pe.wait_ge(s["wh"], 1)

                def step(g, i, b):
                    c = 1 - b
                    if there(g - 1):
                        ran(pe, s["sc"], g - 1)
                        free1(pe, s["gr"], g - 1)
                        turn4(tr_ps, sc[c]).then_inc(s["tr"], 1)
                    if there(g - 3):
                        ran(pe, s["nn0"], g - 3)
                        free1(pe, s["h1"], g - 5)
                        turn4(t01_ps, n0[c]).then_inc(s["tn0"], 1)
                    if there(g - 6):
                        ran(pe, s["h1"], g - 6)
                        free1(pe, s["r2"], g - 6)
                        rows4(z2_ps, h1[b], w["w2"], "l1b2").then_inc(s["z2"], 1)
                    if there(g - 7):
                        ran(pe, s["nn2"], g - 7)
                        free1(pe, s["h3"], g - 9)
                        turn4(t23_ps, n2[c]).then_inc(s["tn2"], 1)
                    if there(g - 10):
                        ran(pe, s["h3"], g - 10)
                        free1(pe, s["yo"], g - 10)
                        rows4(y_ps, h3[b], w["gin"]).then_inc(s["y"], 1)
                    if there(g - 1):
                        ran(pe, s["mT"], g - 1)
                        free1(pe, s["xo"], g - 1)
                        rows4(o_ps, mT[c], w["out"], "fc").then_inc(s["o"], 1)
                    if there(g - 5):
                        ran(pe, s["nn1"], g - 5)
                        if there(g - 3):
                            ran(pe, s["h0"], g - 3)
                        turn4(t01_ps, n1[c]).then_inc(s["tn1"], 1)
                    if there(g - 3):
                        ran(pe, s["h0"], g - 3)
                        free1(pe, s["za"], g - 3)
                        rows4(z1_ps, h0[c], w["w1"], "l1c").then_inc(s["z1"], 1)
                    if there(g - 9):
                        ran(pe, s["nn3"], g - 9)
                        if there(g - 7):
                            ran(pe, s["h2"], g - 7)
                        turn4(t23_ps, n3[c]).then_inc(s["tn3"], 1)
                    if there(g - 7):
                        ran(pe, s["h2"], g - 7)
                        free1(pe, s["x2"], g - 7)
                        rows4(z3_ps, h2[c], w["w3"], "l1b3").then_inc(s["z3"], 1)
                step_sweep(pe, step, 10)

            @block.scalar
            def _(act):
                def evac(k, dst, ps, g, fn, **kw):
                    ran(act, s[f"tn{k}"], g)
                    nc.scalar.activation(dst[:], ps[:], fn, **kw).then_inc(s[f"h{k}"], 1)

                def step(g, i, b):
                    c = 1 - b
                    if there(g - 1):
                        ran(act, s["tr"], g - 1)
                        free2(act, s["mT"], g - 1)
                        nc.scalar.activation(gr[c][:], tr_ps[:], ACT.Relu, bias=bnbi[:, 3:4],
                                             scale=bnsc[:, 3:4]).then_inc(s["gr"], 1)
                    if there(g - 3):
                        free2(act, s["z1"], g - 3)
                        evac(0, h0[c], t01_ps, g - 3, ACT.Relu)
                    if there(g - 7):
                        free2(act, s["tn2"], g - 7)
                        norm_apply_act(act, s, 2, T[2], n2[c], r2[c], g - 7)
                    if there(g - 2):
                        norm_root(act, s, 0, T[0], g - 2, eps_ln)
                    if there(g - 6):
                        ran(act, s["z2"], g - 6)
                        free2(act, s["nn2"], g - 6)
                        nc.scalar.activation(r2[b][:], z2_ps[:], ACT.Relu).then_inc(s["r2"], 1)
                    if there(g - 7):
                        free2(act, s["z3"], g - 7)
                        evac(2, h2[c], t23_ps, g - 7, ACT.Identity, bias=col("be2L1"), scale=col("g2L1"))
                    if there(g - 9):
                        free2(act, s["tn3"], g - 9)
                        norm_apply_act(act, s, 3, T[3], n3[c], x2[c], g - 9)
                    if there(g - 10):
                        ran(act, s["y"], g - 10)
                        free2(act, s["ye"], g - 10)
                        kept(act, yost, g, g - 10, back(i, b, 10), b, 2)
                        nc.scalar.copy(yo[b][:], y_ps[:]).then_inc(s["yo"], 1)
                    if there(g - 8):
                        norm_root(act, s, 3, T[3], g - 8, eps_ln)
                    if there(g - 5):
                        free2(act, s["z2"], g - 5)
                        evac(1, h1[c], t01_ps, g - 5, ACT.Identity, bias=col("be1L1"), scale=col("g1L1"))
                    if there(g - 4):
                        norm_root(act, s, 1, T[1], g - 4, eps_ln)
                    if there(g - 6):
                        norm_root(act, s, 2, T[2], g - 6, eps_ln)
                    if there(g - 9):
                        free2(act, s["y"], g - 9)
                        evac(3, h3[c], t23_ps, g - 9, ACT.Relu)
                step_sweep(act, step, 10)

            @block.vector
            def _(dve):
                dve.wait_ge(s["w"], 80)
                nc.vector.tensor_scalar(w["out"][:], w["out"][:], 0.5, None, ALU.mult).then_inc(s["wh"], 1)

                def step(g, i, b):
                    c = 1 - b
                    if there(g):
                        landed(dve, lt, g, i, b)
                        free2(dve, s["tr"], g)
                        for j in range(J):
                            js = slice(j * D, (j + 1) * D)
                            last = nc.vector.tensor_scalar(sc[b][:, js], ta[b][:, js],
                                                           dinv2[:, bass.ds(g * J + j, 1)], None, ALU.mult)
                        last.then_inc(s["sc"], 1)
                    if there(g - 2):
                        ran(dve, s["o"], g - 2)
                        loaded(dve, lx, g - 2, back(i, b, 2), b)
                        kept(dve, xost, g, g - 2, back(i, b, 2), b)
                        nc.vector.tensor_tensor(xo[b][:], o_ps[:], xr[b][:], ALU.add).then_inc(s["xo"], 1)
                    if there(g - 4):
                        ran(dve, s["z1"], g - 4)
                        loaded(dve, la, g - 4, back(i, b, 4), b)
                        free2(dve, s["r1"], g - 4)
                        nc.vector.tensor_tensor(za[b][:], z1_ps[:], ag[b][:], ALU.add).then_inc(s["za"], 1)
                    if there(g - 8):
                        ran(dve, s["z3"], g - 8)
                        loaded(dve, lb, g - 8, back(i, b, 8), b)
                        free2(dve, s["nn3"], g - 8)
                        kept(dve, x2st, g, g - 8, back(i, b, 8), b)
                        nc.vector.tensor_tensor(x2[b][:], z3_ps[:], xb[b][:], ALU.add).then_inc(s["x2"], 1)
                    if there(g - 2):
                        ran(dve, s["xo"], g - 2)
                        norm_stats(dve, s, 0, T[0], xo[b], g - 2)
                    if there(g - 5):
                        norm_recip(dve, s, 1, T[1], g - 5)
                    if there(g - 2):
                        norm_vars(dve, s, 0, T[0], g - 2)
                    if there(g - 5):
                        free2(dve, s["tn1"], g - 5)
                        norm_apply(dve, s, 1, T[1], n1[c], r1[c], g - 5)
                    if there(g - 8):
                        ran(dve, s["x2"], g - 8)
                        norm_stats(dve, s, 3, T[3], x2[b], g - 8)
                    if there(g - 4):
                        ran(dve, s["r1"], g - 4)
                        norm_stats(dve, s, 1, T[1], r1[b], g - 4)
                    if there(g - 8):
                        norm_vars(dve, s, 3, T[3], g - 8)
                    if there(g - 2):
                        norm_recip(dve, s, 0, T[0], g - 2)
                    if there(g - 6):
                        ran(dve, s["r2"], g - 6)
                        norm_stats(dve, s, 2, T[2], r2[b], g - 6)
                    if there(g - 4):
                        norm_vars(dve, s, 1, T[1], g - 4)
                    if there(g - 2):
                        free2(dve, s["tn0"], g - 2)
                        norm_apply(dve, s, 0, T[0], n0[b], xo[b], g - 2)
                    if there(g - 6):
                        norm_vars(dve, s, 2, T[2], g - 6)
                    if there(g - 8):
                        free1(dve, s["nn3"], g - 8)
                        norm_recip(dve, s, 3, T[3], g - 8)
                        norm_shift(dve, s, 3, T[3], g - 8)
                    if there(g - 6):
                        free1(dve, s["nn2"], g - 6)
                        norm_recip(dve, s, 2, T[2], g - 6)
                        norm_shift(dve, s, 2, T[2], g - 6)
                step_sweep(dve, step, 8)
        MIDDLE_SEMS = (["w", "wh", "sc", "tr", "gr", "gx", "mT", "o", "xo", "tn0", "h0", "z1", "za", "r1", "tn1", "h1",
                        "z2", "r2", "tn2", "h2", "z3", "x2", "tn3", "h3", "y", "yo", "ye", "shift2", "shift3", "pace", "ppace"]
                       + norm_sems(0) + norm_sems(1) + norm_sems(2) + norm_sems(3)
                       + st("lt", "lg", "lx", "la", "lb", "xost", "x2st", "yost"))

        def project_edge_attr(ctx, block, s):
            def sb(name, shape, dt=F32):
                return ctx.enter_context(nc.sbuf_tensor(f"{stage[0]}_{name}", shape, dt))
            w = sb("w_edge", [P, D])
            ea = [sb(f"ea{r}", [EP, D]) for r in range(RING)]
            mix = [sb(f"mix{r}", [EP, EP]) for r in range(RING)]
            mixx = [sb(f"mixx{h}", [EP, EP]) for h in range(RING // 2)]
            sumT = [sb(f"sumT{r}", [P, EP]) for r in range(RING)]
            ps = [ctx.enter_context(nc.psum_tensor(f"{stage[0]}_ps{r}", [P, 512], F32)) for r in range(RING)]
            attr = t["edge_attr_128"].rearrange("(p c) d -> p c d", p=EP)

            @block.sync
            def _(sp):
                sp.dma_start(w[:], t["L1_gnn_W1"][D:2 * D, :]).then_inc(s["w"], 16)

                def body(i):
                    for r in range(RING):
                        if not first_step(i):
                            sp.wait_ge(s["sum"], RING * i + r + 1 - RING)
                        sp.dma_start(ea[r][:], attr[:, bass.ds(RING * i + r, 1), :].rearrange("p a f -> p (a f)")
                                     ).then_inc(s[f"got{r}"], 16)
                sweep(sp, EITER, body)

            @block.vector
            def _(dve):
                def body(i):
                    for r in range(RING):
                        if not first_step(i):
                            dve.wait_ge(s["sum"], RING * i + r + 1 - RING)
                        if r % 2 == 0:
                            nc.vector.tensor_copy(
                                mixx[r // 2][:], cross[:, bass.ds(RING // 2 * i + r // 2, 1), :].rearrange("p a f -> p (a f)"))
                        nc.vector.tensor_copy(mix[r][:], same[:, bass.ds(RING * i + r, 1), :].rearrange("p a f -> p (a f)")
                                              ).then_inc(s["mix"], 1)
                sweep(dve, EITER, body)

            @block.tensor
            def _(pe):
                pe.wait_ge(s["w"], 16)

                def body(i):
                    for r in range(RING):
                        pe.wait_ge(s["mix"], RING * i + r + 1)
                        pe.wait_ge(s[f"got{r}"], 16 * (i + 1))
                        if not first_step(i):
                            pe.wait_ge(s["out"], RING * i + r + 1 - RING)
                        if r % 2 == 1:
                            nc.tensor.matmul(ps[r - 1][:, 0:EP], ea[r - 1][:], mix[r - 1][:], start=True, stop=False)
                            nc.tensor.matmul(ps[r - 1][:, 0:EP], ea[r][:], mixx[r // 2][:], start=False, stop=True
                                             ).then_inc(s["sum"], 1)
                            nc.tensor.matmul(ps[r][:, 0:EP], ea[r][:], mix[r][:], start=True, stop=True).then_inc(s["sum"], 1)
                    for r in range(RING):
                        pe.wait_ge(s["sumT"], RING * i + r + 1)
                        nc.tensor.matmul(ps[r][0:EP, 128:128 + D], sumT[r][:], w[:], start=True, stop=True).then_inc(s["mm"], 1)
                sweep(pe, EITER, body)

            @block.scalar
            def _(act):
                def body(i):
                    for r in range(RING):
                        act.wait_ge(s["sum"], RING * i + r + 1)
                        if not first_step(i):
                            act.wait_ge(s["mm"], RING * i + r + 1 - RING)
                        nc.scalar.copy(sumT[r][:], ps[r][:, 0:EP]).then_inc(s["sumT"], 1)
                    for r in range(RING):
                        act.wait_ge(s["mm"], RING * i + r + 1)
                        nc.scalar.copy(added[:, bass.ds(RING * i + r, 1), :].rearrange("p a f -> p (a f)"),
                                       ps[r][0:EP, 128:128 + D]).then_inc(s["out"], 1)
                sweep(act, EITER, body)
        ATTR_SEMS = ["w", "sum", "mix", "sumT", "mm", "out"] + [f"got{r}" for r in range(RING)]

        def aggregate():
            def emit(ctx, block, s):
                def sb(name, shape, dt=F32):
                    return ctx.enter_context(nc.sbuf_tensor(f"{stage[0]}_{name}", shape, dt))
                Q = edge_tiles(ctx, sb)

                def fours(eng, part):
                    part(0)
                    with eng.Fori(1, FOURS) as i:
                        part(i)

                @block.gpsimd
                def _(pool):
                    edges_on_pool(pool, s, Q, table[0], table[1])

                @block.vector
                def _(dve):
                    fours(dve, edges_on_dve(dve, s, Q, edge_w))

                @block.tensor
                def _(pe):
                    fours(pe, edges_on_pe(pe, s, Q))

                @block.scalar
                def _(act):
                    fours(act, edges_on_act(act, s, Q))
            return EDGE_SEMS, emit

        def gcn(layer):
            def emit(ctx, block, s):
                def sb(name, shape, dt=F32):
                    return ctx.enter_context(nc.sbuf_tensor(f"{stage[0]}_{name}", shape, dt))

                def pair(name):
                    return [sb(f"{name}{b}", [P, GROUP]) for b in SLOTS]
                w = weight_tiles(ctx, ["conv"])
                ta, gf, sc, gr, gT, yo = (pair(n) for n in ("ta", "gf", "sc", "gr", "gT", "yo"))
                A, B = ([ctx.enter_context(nc.psum_tensor(f"{stage[0]}_{n}{b}", [P, GROUP], F32)) for b in SLOTS] for n in "AB")

                @block.sync
                def _(sp):
                    sp.dma_start(w["conv"][:], t["L0_gnn_conv_w"][layer + 1]).then_inc(s["w"], 16)

                    def loads(i):
                        for b in SLOTS:
                            again(sp, s["sc"], i, b)
                            sp.dma_start(ta[b][:], at(grouped(table[1]), 2 * i + b)).then_inc(s[f"lt{b}"], 16)
                            again(sp, s["gT"], i, b)
                            sp.dma_start(gf[b][:], at(g_first, 2 * i + b)).then_inc(s[f"lg{b}"], 16)

                    def stores(i):
                        for b in SLOTS:
                            sp.wait_ge(s["yo"], nth(i, b))
                            sp.dma_start(at(grouped(table[0]), 2 * i + b), yo[b][:]).then_inc(s[f"yost{b}"], 16)
                            sp.dma_start(at(grouped(table[1]), 2 * i + b), yo[b][:]).then_inc(s[f"yost{b}"], 16)
                    load_and_store(sp, loads, stores)
                    for b in SLOTS:
                        sp.wait_ge(s[f"yost{b}"], 32 * PAIRS)

                @block.vector
                def _(dve):
                    def body(i):
                        for b in SLOTS:
                            dve.wait_ge(s[f"lt{b}"], 16 * (i + 1))
                            again(dve, s["tr"], i, b)
                            for j in range(J):
                                js = slice(j * D, (j + 1) * D)
                                last = nc.vector.tensor_scalar(sc[b][:, js], ta[b][:, js],
                                                               dinv2[:, bass.ds((2 * i + b) * J + j, 1)], None, ALU.mult)
                            last.then_inc(s["sc"], 1)
                    sweep(dve, PAIRS, body)

                @block.gpsimd
                def _(pool):
                    def body(i):
                        for b in SLOTS:
                            pool.wait_ge(s["gr"], nth(i, b))
                            pool.wait_ge(s[f"lg{b}"], 16 * (i + 1))
                            again(pool, s["y"], i, b)
                            nc.gpsimd.tensor_tensor(gT[b][:], gr[b][:], gf[b][:], ALU.add).then_inc(s["gT"], 1)
                    sweep(pool, PAIRS, body)

                @block.scalar
                def _(act):
                    def body(i):
                        for b in SLOTS:
                            act.wait_ge(s["tr"], nth(i, b))
                            again(act, s["gT"], i, b)
                            nc.scalar.activation(gr[b][:], A[b][:], ACT.Relu, bias=bnbi[:, layer + 1:layer + 2],
                                                 scale=bnsc[:, layer + 1:layer + 2]).then_inc(s["gr"], 1)
                        for b in SLOTS:
                            act.wait_ge(s["y"], nth(i, b))
                            if not first_step(i):
                                act.wait_ge(s[f"yost{b}"], 32 * i)
                            nc.scalar.copy(yo[b][:], B[b][:]).then_inc(s["yo"], 1)
                    sweep(act, PAIRS, body)

                @block.tensor
                def _(pe):
                    pe.wait_ge(s["w"], 16)

                    def body(i):
                        for b in SLOTS:
                            pe.wait_ge(s["sc"], nth(i, b))
                            again(pe, s["gr"], i, b)
                            turn4(A[b], sc[b]).then_inc(s["tr"], 1)
                        for b in SLOTS:
                            pe.wait_ge(s["gT"], nth(i, b))
                            again(pe, s["yo"], i, b)
                            rows4(B[b], gT[b], w["conv"]).then_inc(s["y"], 1)
                    sweep(pe, PAIRS, body)
            return ["w", "sc", "tr", "gr", "gT", "y", "yo"] + st("lt", "lg", "yost"), emit

        QUADS = (G - 1) // 4
        LEFT = G - 4 * QUADS
        FULL = range(4)

        def in_quads(eng, body):
            body(0, FULL)
            with eng.Fori(1, QUADS) as i:
                body(i, FULL)
            body(QUADS, range(LEFT))

        def move_quads(sp, load, store):
            for b in FULL:
                load(0, b)
            with sp.Fori(0, QUADS - 1) as i:
                for b in FULL:
                    load(i + 1, b)
                for b in FULL:
                    store(i, b)
            for b in range(LEFT):
                load(QUADS, b)
            for b in FULL:
                store(QUADS - 1, b)
            for b in range(LEFT):
                store(QUADS, b)

        def through(i, b):
            return 4 * i + b + 1

        def reread(eng, sem, i, b):
            if not first_step(i):
                eng.wait_ge(sem, 4 * i + b - 3)

        def slot_stored(eng, sem, i, per_group=1):
            if not first_step(i):
                eng.wait_ge(sem, 16 * per_group * i)

        def all_stored(sp, sems, slots, per_group=1):
            for b in slots:
                sp.wait_ge(sems[b], 16 * per_group * len(range(b, G, 4)))

        def four_of(sb, name, slots=range(4)):
            return {b: sb(f"{name}{b}", [P, GROUP]) for b in slots}

        def banks(ctx, name):
            return [ctx.enter_context(nc.psum_tensor(f"{stage[0]}_{name}{b}", [P, GROUP], F32)) for b in FULL]

        def sems4(s, name, slots=range(4)):
            return {b: s[f"{name}{b}"] for b in slots}

        def st4(*names):
            return [f"{n}{b}" for n in names for b in FULL]
        ODD = (1, 3)

        def held_group(k):
            return held[:, bass.ds(k, 1), :].rearrange("p a f -> p (a f)")

        def between(tiles, i, b):
            return tiles[b][:] if b in ODD else held_group(2 * i + b // 2)

        bnmv = keep("bnmv", [P, 2])
        bnsd = keep("bnsd", [P, 1])
        gsc = keep("gsc", [P, 1])
        gbi = keep("gbi", [P, 1])
        gtmp = keep("gtmp", [P, 1])

        def batch_stats(dve, i, b, src):
            if not (isinstance(i, int) and 4 * i + b == G - 1):
                return nc.vector.bn_stats(bnstat[:, bass.ds(4 * i + b, 1), :].rearrange("p a f -> p (a f)"), src)
            for j in range(J):
                rows = slice(j * D, j * D + TAILP)
                last = nc.vector.bn_stats(bnstat[:, G - 1 + j, :], src[:, rows])
            return last

        def gin_turn(layer):
            def emit(ctx, block, s):
                def sb(name, shape, dt=F32):
                    return ctx.enter_context(nc.sbuf_tensor(f"{stage[0]}_{name}", shape, dt))
                ta, zT = four_of(sb, "ta"), four_of(sb, "zT", ODD)
                A = banks(ctx, "A")
                lt, zst = sems4(s, "lt"), sems4(s, "zst")

                @block.sync
                def _(sp):
                    def load(i, b):
                        reread(sp, s["tr"], i, b)
                        sp.dma_start(ta[b][:], at(grouped(table[1]), 4 * i + b)).then_inc(lt[b], 16)

                    def store(i, b):
                        if b in ODD:
                            sp.wait_ge(s["zT"], through(i, b))
                            sp.dma_start(at(cur[0], 4 * i + b), zT[b][:]).then_inc(zst[b], 16)
                    move_quads(sp, load, store)
                    all_stored(sp, zst, ODD)

                @block.tensor
                def _(pe):
                    def body(i, slots):
                        for b in slots:
                            pe.wait_ge(lt[b], 16 * (i + 1))
                            reread(pe, s["zT"], i, b)
                            turn4(A[b], ta[b]).then_inc(s["tr"], 1)
                    in_quads(pe, body)

                @block.scalar
                def _(act):
                    def body(i, slots):
                        for b in slots:
                            act.wait_ge(s["tr"], through(i, b))
                            if b in ODD:
                                reread(act, s["bs"], i, b)
                                slot_stored(act, zst[b], i)
                            else:
                                act.sem_inc(s["pace"], 1)
                            nc.scalar.activation(between(zT, i, b), A[b][:], ACT.Identity, bias=col(f"b1_{layer}")
                                                 ).then_inc(s["zT"], 1)
                    in_quads(act, body)
                    batch_root(act, s)

                @block.vector
                def _(dve):
                    def body(i, slots):
                        for b in slots:
                            dve.wait_ge(s["zT"], through(i, b))
                            batch_stats(dve, i, b, between(zT, i, b)).then_inc(s["bs"], 1)
                    in_quads(dve, body)
                    batch_scale(dve, s, col(f"g1_{layer}"), col(f"bt1_{layer}"))
            return ["pace", "tr", "zT", "bs", "dv", "bvar", "bstd"] + st4("lt", "zst"), emit

        def batch_root(act, s):
            act.wait_ge(s["bvar"], 1)
            nc.scalar.activation(bnsd[:], bnmv[:, 1:2], ACT.Sqrt, bias=eps_ln).then_inc(s["bstd"], 1)

        def batch_scale(dve, s, g, b):
            dve.wait_ge(s["bs"], G)
            nc.vector.bn_aggr(bnmv[:], bnstat[:, 0:G - 1 + J, :].rearrange("p a f -> p (a f)")).then_inc(s["bvar"], 1)
            dve.wait_ge(s["bstd"], 1)
            nc.vector.reciprocal(gtmp[:], bnsd[:]).then_inc(s["dv"], 1)
            dve.wait_ge(s["dv"], 1)
            nc.vector.tensor_tensor(gsc[:], gtmp[:], g, ALU.mult).then_inc(s["dv"], 1)
            dve.wait_ge(s["dv"], 2)
            nc.vector.tensor_tensor(gtmp[:], bnmv[:, 0:1], gsc[:], ALU.mult).then_inc(s["dv"], 1)
            dve.wait_ge(s["dv"], 3)
            nc.vector.tensor_tensor(gbi[:], b, gtmp[:], ALU.subtract)

        def gin_middle(layer):
            def emit(ctx, block, s):
                def sb(name, shape, dt=F32):
                    return ctx.enter_context(nc.sbuf_tensor(f"{stage[0]}_{name}", shape, dt))
                w = weight_tiles(ctx, ["w2"])
                zT, tT, uT = four_of(sb, "zT", ODD), four_of(sb, "tT"), four_of(sb, "uT", ODD)
                A = banks(ctx, "A")
                lt, ust = sems4(s, "lt"), sems4(s, "ust")
                made = {b: s["uT_odd" if b in ODD else "uT_even"] for b in FULL}

                def is_made(eng, i, b):
                    eng.wait_ge(made[b], 2 * i + b // 2 + 1)

                @block.sync
                def _(sp):
                    sp.dma_start(w["w2"][:], t["L2_gnn_W2"][layer]).then_inc(s["w"], 16)

                    def load(i, b):
                        if b in ODD:
                            reread(sp, s["tT"], i, b)
                            sp.dma_start(zT[b][:], at(cur[0], 4 * i + b)).then_inc(lt[b], 16)

                    def store(i, b):
                        if b in ODD:
                            is_made(sp, i, b)
                            sp.dma_start(at(cur[1], 4 * i + b), uT[b][:]).then_inc(ust[b], 16)
                    move_quads(sp, load, store)
                    all_stored(sp, ust, ODD)

                @block.tensor
                def _(pe):
                    pe.wait_ge(s["w"], 16)

                    def body(i, slots):
                        for b in slots:
                            pe.wait_ge(s["tT"], through(i, b))
                            if not first_step(i):
                                pe.wait_ge(made[b], 2 * i + b // 2 - 1)
                            nc.tensor.matmul(A[b][:], w["w2"][:], tT[b][:], start=True, stop=True).then_inc(s["mm"], 1)
                    in_quads(pe, body)

                @block.scalar
                def _(act):
                    def body(i, slots):
                        for b in slots:
                            if b in ODD:
                                act.wait_ge(lt[b], 16 * (i + 1))
                            reread(act, s["mm"], i, b)
                            if b not in ODD:
                                act.sem_inc(s["pace"], 1)
                            nc.scalar.activation(tT[b][:], between(zT, i, b), ACT.Relu, bias=gsc_bias[0], scale=gsc_bias[1]
                                                 ).then_inc(s["tT"], 1)
                        for b in slots:
                            if b not in ODD:
                                act.wait_ge(s["mm"], through(i, b))
                                act.sem_inc(s["pace"], 1)
                                nc.scalar.activation(between(uT, i, b), A[b][:], ACT.Relu, bias=col(f"b2_{layer}")
                                                     ).then_inc(made[b], 1)
                    in_quads(act, body)
                    batch_root(act, s)

                @block.vector
                def _(dve):
                    def body(i, slots):
                        for b in slots:
                            if b in ODD:
                                dve.wait_ge(s["mm"], through(i, b))
                                reread(dve, s["bs"], i, b)
                                slot_stored(dve, ust[b], i)
                                nc.vector.tensor_scalar(uT[b][:], A[b][:], col(f"b2_{layer}"), 0.0, ALU.add, ALU.max
                                                        ).then_inc(made[b], 1)
                        for b in slots:
                            is_made(dve, i, b)
                            batch_stats(dve, i, b, between(uT, i, b)).then_inc(s["bs"], 1)
                    in_quads(dve, body)
                    dve.wait_ge(s["tT"], G)
                    batch_scale(dve, s, col(f"g2_{layer}"), col(f"bt2_{layer}"))
            return ["pace", "w", "tT", "uT_even", "uT_odd", "mm", "bs", "dv", "bvar", "bstd"] + st4("lt", "ust"), emit
        gsc_bias = (gbi[:, 0:1], gsc[:, 0:1])

        def gin_next(layer):
            def emit(ctx, block, s):
                def sb(name, shape, dt=F32):
                    return ctx.enter_context(nc.sbuf_tensor(f"{stage[0]}_{name}", shape, dt))
                w = weight_tiles(ctx, ["w1"])
                uT, hT, yo, ye = four_of(sb, "uT", ODD), four_of(sb, "hT"), four_of(sb, "yo"), four_of(sb, "ye")
                A = banks(ctx, "A")
                lt, yost, yest = (sems4(s, n) for n in ("lt", "yost", "yest"))

                @block.sync
                def _(sp):
                    sp.dma_start(w["w1"][:], t["L2_gnn_W1"][layer + 1]).then_inc(s["w"], 16)

                    def load(i, b):
                        if b in ODD:
                            reread(sp, s["hT"], i, b)
                            sp.dma_start(uT[b][:], at(cur[1], 4 * i + b)).then_inc(lt[b], 16)

                    def store(i, b):
                        sp.wait_ge(s["yo"], through(i, b))
                        sp.dma_start(at(grouped(table[0]), 4 * i + b), yo[b][:]).then_inc(yost[b], 16)
                        sp.wait_ge(s["ye"], through(i, b))
                        sp.dma_start(at(grouped(table[1]), 4 * i + b), ye[b][:]).then_inc(yest[b], 16)
                    move_quads(sp, load, store)
                    all_stored(sp, yost, FULL)
                    all_stored(sp, yest, FULL)

                @block.tensor
                def _(pe):
                    pe.wait_ge(s["w"], 16)

                    def body(i, slots):
                        for b in slots:
                            pe.wait_ge(s["hT"], through(i, b))
                            reread(pe, s["yo"], i, b)
                            rows4(A[b], hT[b], w["w1"]).then_inc(s["mm"], 1)
                    in_quads(pe, body)

                @block.scalar
                def _(act):
                    def body(i, slots):
                        for b in slots:
                            if b in ODD:
                                act.wait_ge(lt[b], 16 * (i + 1))
                            reread(act, s["mm"], i, b)
                            if b not in ODD:
                                act.sem_inc(s["pace"], 1)
                            nc.scalar.activation(hT[b][:], between(uT, i, b), ACT.Relu, bias=gsc_bias[0], scale=gsc_bias[1]
                                                 ).then_inc(s["hT"], 1)
                        for b in slots:
                            act.wait_ge(s["mm"], through(i, b))
                            reread(act, s["ye"], i, b)
                            slot_stored(act, yost[b], i)
                            nc.scalar.copy(yo[b][:], A[b][:]).then_inc(s["yo"], 1)
                    in_quads(act, body)

                @block.vector
                def _(dve):
                    def body(i, slots):
                        for b in slots:
                            dve.wait_ge(s["yo"], through(i, b))
                            slot_stored(dve, yest[b], i)
                            nc.vector.tensor_scalar(ye[b][:], yo[b][:], eps1[:, layer + 1:layer + 2], None, ALU.mult
                                                    ).then_inc(s["ye"], 1)
                    in_quads(dve, body)
            return ["pace", "w", "hT", "mm", "yo", "ye"] + st4("lt", "yost", "yest"), emit

        def gin_last(ctx, block, s):
            def sb(name, shape, dt=F32):
                return ctx.enter_context(nc.sbuf_tensor(f"{stage[0]}_{name}", shape, dt))
            w = weight_tiles(ctx, ["w1"])
            uT = sb("uT", [P, GROUP])
            hT, xr, xo, nn, fT, yo = (pair_of(sb, n) for n in ("hT", "xr", "xo", "nn", "fT", "yo"))
            T1 = norm1_tiles(sb, "n1")
            th_ps, tn_ps, y_ps = ([ctx.enter_context(nc.psum_tensor(f"{stage[0]}_{n}{b}", [P, GROUP], F32)) for b in SLOTS]
                                  for n in ("th", "tn", "y"))
            lx, xost, yost = ([s[f"{n}{b}"] for b in SLOTS] for n in ("lx", "xost", "yost"))

            @block.sync
            def _(sp):
                sp.dma_start(w["w1"][:], t["L3_gnn_W1"]).then_inc(s["w"], 16)

                def step(g, i, b):
                    c = 1 - b
                    if there(g):
                        if b:
                            free2(sp, s["hT"], g)
                            sp.dma_start(uT[:], at(cur[1], g)).then_inc(s["lt"], 16)
                        free2(sp, s["xo"], g)
                        sp.dma_start(xr[b][:], at(grouped(xres[1]), g)).then_inc(lx[b], 16)
                    if there(g - 1):
                        ran(sp, s["xo"], g - 1)
                        sp.dma_start(at(grouped(xres[0]), g - 1), xo[c][:]).then_inc(xost[c], 16)
                    if there(g - 5):
                        ran(sp, s["yo"], g - 5)
                        sp.dma_start(at(grouped(table[0]), g - 5), yo[c][:]).then_inc(yost[c], 16)
                        sp.dma_start(at(grouped(table[1]), g - 5), yo[c][:]).then_inc(yost[c], 16)
                step_sweep(sp, step, 5)
                for sem in xost:
                    sp.wait_ge(sem, 16 * PAIRS)
                for sem in yost:
                    sp.wait_ge(sem, 32 * PAIRS)

            @block.tensor
            def _(pe):
                pe.wait_ge(s["w"], 16)

                def step(g, i, b):
                    c = 1 - b
                    if there(g - 2):
                        ran(pe, s["nn1"], g - 2)
                        free2(pe, s["fT"], g - 2)
                        turn4(tn_ps[b], nn[b]).then_inc(s["tn"], 1)
                    if there(g):
                        ran(pe, s["hT"], g)
                        free2(pe, s["xo"], g)
                        turn4(th_ps[b], hT[b]).then_inc(s["th"], 1)
                    if there(g - 3):
                        ran(pe, s["fT"], g - 3)
                        free2(pe, s["yo"], g - 3)
                        rows4(y_ps[c], fT[c], w["w1"]).then_inc(s["y"], 1)
                step_sweep(pe, step, 3)

            @block.scalar
            def _(act):
                def step(g, i, b):
                    c = 1 - b
                    if there(g):
                        if b:
                            act.wait_ge(s["lt"], 16 * (i + 1))
                        free2(act, s["th"], g)
                        if not b:
                            act.sem_inc(s["apace"], 1)
                        nc.scalar.activation(hT[b][:], uT[:] if b else held_group(i), ACT.Relu, bias=gsc_bias[0], scale=gsc_bias[1]
                                             ).then_inc(s["hT"], 1)
                    if there(g - 1):
                        norm_root(act, s, 1, T1, g - 1, eps_ln)
                    if there(g - 2):
                        ran(act, s["tn"], g - 2)
                        free2(act, s["y"], g - 2)
                        nc.scalar.activation(fT[b][:], tn_ps[b][:], ACT.Relu).then_inc(s["fT"], 1)
                    if there(g - 4):
                        ran(act, s["y"], g - 4)
                        stored(act, yost, g - 4, i - 2, b, 2)
                        nc.scalar.copy(yo[b][:], y_ps[b][:]).then_inc(s["yo"], 1)
                step_sweep(act, step, 4)

            @block.vector
            def _(dve):
                def step(g, i, b):
                    c = 1 - b
                    if there(g):
                        ran(dve, s["th"], g)
                        landed(dve, lx, g, i, b)
                        stored(dve, xost, g, i, b)
                        nc.vector.tensor_tensor(xo[b][:], th_ps[b][:], xr[b][:], ALU.add).then_inc(s["xo"], 1)
                    if there(g - 1):
                        norm_recip(dve, s, 1, T1, g - 1)
                        free2(dve, s["tn"], g - 1)
                        norm_apply(dve, s, 1, T1, nn[c], xo[c], g - 1)
                    if there(g):
                        ran(dve, s["xo"], g)
                        norm_stats(dve, s, 1, T1, xo[b], g)
                        norm_vars(dve, s, 1, T1, g)
                step_sweep(dve, step, 1)
        GIN_LAST_SEMS = (["w", "hT", "xo", "yo", "th", "tn", "fT", "y", "lt", "pace", "apace"] + norm_sems(1)
                         + st("lx", "xost", "yost"))

        def fourth(ctx, block, s):
            def sb(name, shape, dt=F32):
                return ctx.enter_context(nc.sbuf_tensor(f"{stage[0]}_{name}", shape, dt))
            w = weight_tiles(ctx, ["w2"])
            ta, xr, hT, xo = (four_of(sb, n) for n in ("ta", "xr", "hT", "xo"))
            A, B = banks(ctx, "A"), banks(ctx, "B")
            lt, lx, xost = (sems4(s, n) for n in ("lt", "lx", "xost"))

            @block.sync
            def _(sp):
                sp.dma_start(w["w2"][:], t["L3_gnn_W2"]).then_inc(s["w"], 16)

                def load(i, b):
                    reread(sp, s["tr"], i, b)
                    sp.dma_start(ta[b][:], at(grouped(table[1]), 4 * i + b)).then_inc(lt[b], 16)
                    if first_step(i):
                        residual(0, b)

                def residual(i, b):
                    sp.dma_start(xr[b][:], at(grouped(xres[0]), 4 * i + b)).then_inc(lx[b], 16)

                def store(i, b):
                    sp.wait_ge(s["xo"], through(i, b))
                    if isinstance(i, int) and 4 * i + b == G - 1:
                        sp.dma_start(out_tail, xo[b][0:TAILP, :]).then_inc(xost[b], 16)
                    else:
                        sp.dma_start(at(out_groups, 4 * i + b), xo[b][:]).then_inc(xost[b], 16)
                    if not isinstance(i, int) or 4 * (i + 1) + b < G:
                        residual(i + 1, b)
                move_quads(sp, load, store)
                all_stored(sp, xost, FULL)

            @block.tensor
            def _(pe):
                pe.wait_ge(s["w"], 16)

                def body(i, slots):
                    for b in slots:
                        pe.wait_ge(lt[b], 16 * (i + 1))
                        reread(pe, s["hT"], i, b)
                        turn4(A[b], ta[b]).then_inc(s["tr"], 1)
                    for b in slots:
                        pe.wait_ge(s["hT"], through(i, b))
                        reread(pe, s["xo"], i, b)
                        rows4(B[b], hT[b], w["w2"], "l3b2").then_inc(s["y"], 1)
                in_quads(pe, body)

            @block.scalar
            def _(act):
                def body(i, slots):
                    for b in slots:
                        act.wait_ge(s["tr"], through(i, b))
                        reread(act, s["y"], i, b)
                        nc.scalar.activation(hT[b][:], A[b][:], ACT.Relu, bias=col("b1L3")).then_inc(s["hT"], 1)
                in_quads(act, body)

            @block.vector
            def _(dve):
                def body(i, slots):
                    for b in slots:
                        dve.wait_ge(s["y"], through(i, b))
                        dve.wait_ge(lx[b], 16 * (i + 1))
                        slot_stored(dve, xost[b], i)
                        nc.vector.tensor_tensor(xo[b][:], B[b][:], xr[b][:], ALU.add).then_inc(s["xo"], 1)
                in_quads(dve, body)
        FOURTH_SEMS = ["w", "tr", "hT", "y", "xo"] + st4("lt", "lx", "xost")

        with nc.sbuf_tensor("added", [EP, TILES, D], F32) as added:
            run_block("attr", ATTR_SEMS, project_edge_attr)
            run_block("first", FIRST_SEMS, pass_first, FIRST_COUNTS)
            run_block("att0", *attention(0), dict(EDGE_COUNTS, sw_added=32 * TILES))
        run_block("gcn0", *gcn(0))
        run_block("att1a", *attention(1, (0, -(-PAIRS // 2))), EDGE_COUNTS)
        run_block("gcn1", *gcn(1))
        run_block("att1b", *attention(1, (-(-PAIRS // 2), PAIRS)), EDGE_COUNTS)
        run_block("middle", MIDDLE_SEMS, middle)
        with nc.sbuf_tensor("held", [P, PAIRS, GROUP], F32) as held:
            for layer in range(3):
                run_block(f"gin{layer}e", *aggregate(), EDGE_COUNTS)
                run_block(f"gin{layer}t", *gin_turn(layer))
                run_block(f"gin{layer}m", *gin_middle(layer))
                if layer < 2:
                    run_block(f"gin{layer}n", *gin_next(layer))
            run_block("ginlast", GIN_LAST_SEMS, gin_last)
        run_block("fourth", *aggregate(), EDGE_COUNTS)
        run_block("out", FOURTH_SEMS, fourth)


_INS = ["x", "src", "dst", "edge_attr_128", "edge_weight",
        "L0_gnn_t_fc_w", "L0_gnn_t_fc_b", "L0_gnn_t_ln_g", "L0_gnn_t_ln_b", "L0_gnn_qkv_w",
        "L0_gnn_g_fc_w", "L0_gnn_g_fc_b", "L0_gnn_bn_g", "L0_gnn_bn_b", "L0_gnn_conv_w", "L0_gnn_conv_b",
        "L0_gnn_fc_w", "L0_gnn_fc_b",
        "L1_gnn_u", "L1_gnn_W1", "L1_gnn_b1", "L1_gnn_g1", "L1_gnn_be1", "L1_gnn_W2", "L1_gnn_b2",
        "L1_gnn_g2", "L1_gnn_be2", "L1_gnn_W3", "L1_gnn_b3",
        "L2_gnn_eps_list", "L2_gnn_W1", "L2_gnn_b1", "L2_gnn_g1", "L2_gnn_bt1", "L2_gnn_W2", "L2_gnn_b2",
        "L2_gnn_g2", "L2_gnn_bt2",
        "L3_gnn_W1", "L3_gnn_b1", "L3_gnn_W2", "L3_gnn_b2"]


def kernel(**inputs):
    import numpy as _np
    import concourse.bacc as _bacc
    from concourse import mybir as _mybir
    from concourse.bass_utils import run_bass_kernel_spmd as _run

    nc = _bacc.Bacc("TRN2", target_bir_lowering=False, num_devices=1)
    arrays, args = {}, {}
    for name in _INS:
        a = _np.ascontiguousarray(inputs[name])
        arrays[f"in_{name}_dram"] = a
        args[name] = nc.dram_tensor(f"in_{name}_dram", a.shape, _mybir.dt.from_np(a.dtype), kind="ExternalInput").ap()
    shape = inputs["x"].shape
    out = nc.dram_tensor("out_0_dram", shape, _mybir.dt.float32, kind="ExternalOutput").ap()
    build(nc, args, out)
    r = _run(nc, [arrays], core_ids=[0])
    return r.results[0]["out_0_dram"]
```
